# Optimizing a Trainium2 kernel written in Bass

```python
import numpy as np
import jax
import jax.numpy as jnp

def _softmax(x, axis=-1):
    return jax.nn.softmax(x, axis=axis)

def _gelu(x):
    return jax.nn.gelu(x, approximate=True)

def _silu(x):
    return jax.nn.silu(x)

def _sigmoid(x):
    return jax.nn.sigmoid(x)

def _layernorm(x, axis=-1, eps=1e-05):
    m = jnp.mean(x, axis=axis, keepdims=True)
    v = jnp.var(x, axis=axis, keepdims=True)
    return (x - m) / jnp.sqrt(v + eps)

def _scatter_add(tgt, idx, src, axis=0):
    return tgt.at[idx].add(src)

def _segment_sum(src, seg, n):
    return jax.ops.segment_sum(src, seg, n)
kernel_name = 'mk_xattn_seq_d2_seqx_r4_09bfdb'

def setup_inputs(seed: int=0):
    np.random.seed(seed)
    _w = jnp.asarray

    def _rec_inputs():
        import jax
        import jax.numpy as jnp
        _rk = jax.random.key(seed)
        x = -0.0002928 + 1 * jax.random.normal(jax.random.fold_in(_rk, 1), (4, 512, 512), jnp.float32)
        _lenS = 512 - jax.random.randint(jax.random.fold_in(_rk, 7), (4,), 0, max(1, 512 // 4) + 1, jnp.int32)
        _lenS2 = 1024 - jax.random.randint(jax.random.fold_in(_rk, 8), (4,), 0, max(1, 1024 // 4) + 1, jnp.int32)
        _ctx_2048P = jax.random.normal(jax.random.fold_in(_rk, 11), (4, 16, 512), jnp.float32)
        _ctx_2048c = jax.random.dirichlet(jax.random.fold_in(_rk, 511), 0.3 * jnp.ones((16,), jnp.float32), (4, 1024))
        _ctx_2048t = jnp.einsum('bsk,bkd->bsd', _ctx_2048c, _ctx_2048P)
        _ctx_2048t = _ctx_2048t * jax.lax.rsqrt(jnp.mean(jnp.square(_ctx_2048t)) + 1e-12) * 0.953939
        ctx_2048 = 0.000189249 + 0.0999589 * (_ctx_2048t + 0.3 * jax.random.normal(jax.random.fold_in(_rk, 611), (4, 1024, 512), jnp.float32))
        _validS = jnp.arange(512)[None, :] < _lenS[:, None]
        _validS2 = jnp.arange(1024)[None, :] < _lenS2[:, None]
        _causal = jnp.tril(jnp.ones((512, 512), dtype=bool))
        mask_BxS2_bf1 = jnp.ones((4, 1024), dtype=bool)
        return (x, ctx_2048, mask_BxS2_bf1)
    x, ctx_2048, mask_BxS2_bf1 = _rec_inputs()

    def _L0_xattn_setup():
        import jax, jax.numpy as jnp
        import numpy as np
        B, L, E, H = (4, 128, 512, 32)
        S = E // H
        EXTRA_MAA, EXTRA_DECAY = (32, 64)
        EPS = 1e-05

        def _ln(x, w, b):
            m = jnp.mean(x, axis=-1, keepdims=True)
            v = jnp.mean((x - m) ** 2, axis=-1, keepdims=True)
            return (x - m) * jax.lax.rsqrt(v + EPS) * w + b

        def _token_shift(xn, prev_row):
            first = (prev_row - xn[:, 0])[:, None]
            rest = xn[:, :-1] - xn[:, 1:]
            return jnp.concatenate([first, rest], axis=1)
        key = jax.random.key(seed)
        ks = jax.random.split(key, 24)
        rn = lambda k, shp, s=1.0: jax.random.normal(k, shp, dtype=jnp.float32) * s
        return dict(x=rn(ks[0], (B, L, E)), state=rn(ks[1], (B, 2 + S, E), 0.1), ln1_w=jnp.ones((E,), jnp.float32), ln1_b=jnp.zeros((E,), jnp.float32), ln2_w=jnp.ones((E,), jnp.float32), ln2_b=jnp.zeros((E,), jnp.float32), maa_x=rn(ks[2], (E,), 0.02), maa_w1=rn(ks[3], (E, 5 * EXTRA_MAA), 0.02), maa_w2=rn(ks[4], (5, EXTRA_MAA, E), 0.02), maa_stack=rn(ks[5], (5, E), 0.02), time_decay=rn(ks[6], (E,), 0.5), decay_w1=rn(ks[7], (E, EXTRA_DECAY), 0.02), decay_w2=rn(ks[8], (EXTRA_DECAY, E), 0.02), faaaa=rn(ks[9], (H, S), 0.1), Wr=rn(ks[10], (E, E), 0.02), Wk=rn(ks[11], (E, E), 0.02), Wv=rn(ks[12], (E, E), 0.02), Wg=rn(ks[13], (E, E), 0.02), Wo=rn(ks[14], (E, E), 0.02), gn_w=jnp.ones((E,), jnp.float32), gn_b=jnp.zeros((E,), jnp.float32), ffn_maa_k=rn(ks[15], (E,), 0.02), ffn_maa_r=rn(ks[16], (E,), 0.02), ffn_Wk=rn(ks[17], (E, E), 0.02), ffn_Wr=rn(ks[18], (E, E), 0.02), ffn_Wv=rn(ks[19], (E, E), 0.02), i=0)
    _L0_xattn_all = _L0_xattn_setup()
    _L0_xattn_in = {k: v for k, v in _L0_xattn_all.items() if k in ('ln1_w', 'ln1_b', 'ln2_w', 'ln2_b', 'maa_x', 'maa_w1', 'maa_w2', 'maa_stack', 'time_decay', 'decay_w1', 'decay_w2', 'faaaa', 'Wr', 'Wk', 'Wv', 'Wg', 'Wo', 'gn_w', 'gn_b', 'ffn_maa_k', 'ffn_maa_r', 'ffn_Wk', 'ffn_Wr', 'ffn_Wv')}
    del _L0_xattn_all

    def _L1_xattn_setup():
        import jax, jax.numpy as jnp
        import numpy as np
        HIDDEN = 512
        HEADS = 16
        HEAD_DIM = HIDDEN // HEADS
        LN_EPS = 1e-05
        GATE_INIT = 0.5

        def _layer_norm(x, gamma, beta):
            mu = jnp.mean(x, axis=-1, keepdims=True)
            var = jnp.mean(jnp.square(x - mu), axis=-1, keepdims=True)
            return (x - mu) * jax.lax.rsqrt(var + LN_EPS) * gamma + beta
        key = jax.random.key(seed)
        ks = jax.random.split(key, 8)
        B, T_TEXT, T_AUDIO = (4, 512, 375)
        s = 0.02
        return {'hidden_states': jax.random.normal(ks[0], (B, T_TEXT, HIDDEN), jnp.float32), 'audio_kv': jax.random.normal(ks[1], (B, T_AUDIO, HIDDEN), jnp.float32), 'audio_attention_mask': jnp.ones((B, T_AUDIO), dtype=bool), 'Wq': jax.random.normal(ks[2], (HIDDEN, HIDDEN), jnp.float32) * s, 'Wk': jax.random.normal(ks[3], (HIDDEN, HIDDEN), jnp.float32) * s, 'Wv': jax.random.normal(ks[4], (HIDDEN, HIDDEN), jnp.float32) * s, 'Wo': jax.random.normal(ks[5], (HIDDEN, HIDDEN), jnp.float32) * s, 'ln_gamma': jnp.ones((HIDDEN,), jnp.float32), 'ln_beta': jnp.zeros((HIDDEN,), jnp.float32), 'gate': jnp.array([GATE_INIT], jnp.float32)}
    _L1_xattn_all = _L1_xattn_setup()
    _L1_xattn_in = {k: v for k, v in _L1_xattn_all.items() if k in ('Wq', 'Wk', 'Wv', 'Wo', 'ln_gamma', 'ln_beta', 'gate')}
    del _L1_xattn_all
    return {'x': x, 'ctx_2048': ctx_2048, 'mask_BxS2_bf1': mask_BxS2_bf1, 'L0_xattn_ln1_w': _L0_xattn_in['ln1_w'], 'L0_xattn_ln1_b': _L0_xattn_in['ln1_b'], 'L0_xattn_ln2_w': _L0_xattn_in['ln2_w'], 'L0_xattn_ln2_b': _L0_xattn_in['ln2_b'], 'L0_xattn_maa_x': _L0_xattn_in['maa_x'], 'L0_xattn_maa_w1': _L0_xattn_in['maa_w1'], 'L0_xattn_maa_w2': _L0_xattn_in['maa_w2'], 'L0_xattn_maa_stack': _L0_xattn_in['maa_stack'], 'L0_xattn_time_decay': _L0_xattn_in['time_decay'], 'L0_xattn_decay_w1': _L0_xattn_in['decay_w1'], 'L0_xattn_decay_w2': _L0_xattn_in['decay_w2'], 'L0_xattn_faaaa': _L0_xattn_in['faaaa'], 'L0_xattn_Wr': _L0_xattn_in['Wr'], 'L0_xattn_Wk': _L0_xattn_in['Wk'], 'L0_xattn_Wv': _L0_xattn_in['Wv'], 'L0_xattn_Wg': _L0_xattn_in['Wg'], 'L0_xattn_Wo': _L0_xattn_in['Wo'], 'L0_xattn_gn_w': _L0_xattn_in['gn_w'], 'L0_xattn_gn_b': _L0_xattn_in['gn_b'], 'L0_xattn_ffn_maa_k': _L0_xattn_in['ffn_maa_k'], 'L0_xattn_ffn_maa_r': _L0_xattn_in['ffn_maa_r'], 'L0_xattn_ffn_Wk': _L0_xattn_in['ffn_Wk'], 'L0_xattn_ffn_Wr': _L0_xattn_in['ffn_Wr'], 'L0_xattn_ffn_Wv': _L0_xattn_in['ffn_Wv'], 'L1_xattn_Wq': _L1_xattn_in['Wq'], 'L1_xattn_Wk': _L1_xattn_in['Wk'], 'L1_xattn_Wv': _L1_xattn_in['Wv'], 'L1_xattn_Wo': _L1_xattn_in['Wo'], 'L1_xattn_ln_gamma': _L1_xattn_in['ln_gamma'], 'L1_xattn_ln_beta': _L1_xattn_in['ln_beta'], 'L1_xattn_gate': _L1_xattn_in['gate']}

def reference(x, ctx_2048, mask_BxS2_bf1, L0_xattn_ln1_w, L0_xattn_ln1_b, L0_xattn_ln2_w, L0_xattn_ln2_b, L0_xattn_maa_x, L0_xattn_maa_w1, L0_xattn_maa_w2, L0_xattn_maa_stack, L0_xattn_time_decay, L0_xattn_decay_w1, L0_xattn_decay_w2, L0_xattn_faaaa, L0_xattn_Wr, L0_xattn_Wk, L0_xattn_Wv, L0_xattn_Wg, L0_xattn_Wo, L0_xattn_gn_w, L0_xattn_gn_b, L0_xattn_ffn_maa_k, L0_xattn_ffn_maa_r, L0_xattn_ffn_Wk, L0_xattn_ffn_Wr, L0_xattn_ffn_Wv, L1_xattn_Wq, L1_xattn_Wk, L1_xattn_Wv, L1_xattn_Wo, L1_xattn_ln_gamma, L1_xattn_ln_beta, L1_xattn_gate):
    import jax
    import jax.numpy as jnp

    def _L0_xattn_ref(x, state, ln1_w, ln1_b, ln2_w, ln2_b, maa_x, maa_w1, maa_w2, maa_stack, time_decay, decay_w1, decay_w2, faaaa, Wr, Wk, Wv, Wg, Wo, gn_w, gn_b, ffn_maa_k, ffn_maa_r, ffn_Wk, ffn_Wr, ffn_Wv, i):
        import jax, jax.numpy as jnp
        import numpy as np
        B, L, E, H = (4, 128, 512, 32)
        S = E // H
        EXTRA_MAA, EXTRA_DECAY = (32, 64)
        EPS = 1e-05

        def _ln(x, w, b):
            m = jnp.mean(x, axis=-1, keepdims=True)
            v = jnp.mean((x - m) ** 2, axis=-1, keepdims=True)
            return (x - m) * jax.lax.rsqrt(v + EPS) * w + b

        def _token_shift(xn, prev_row):
            first = (prev_row - xn[:, 0])[:, None]
            rest = xn[:, :-1] - xn[:, 1:]
            return jnp.concatenate([first, rest], axis=1)
        b, l = (x.shape[0], x.shape[1])
        i0 = (2 + S) * i + 0
        i1 = (2 + S) * i + 1
        xn = _ln(x, ln1_w, ln1_b)
        sx = _token_shift(xn, state[:, i1])
        xxx = jnp.tanh((xn + sx * maa_x) @ maa_w1).reshape(b, l, 5, 1, EXTRA_MAA)
        xxx = jnp.matmul(xxx, maa_w2).reshape(b, l, 5, E)
        x5 = xn[:, :, None] + sx[:, :, None] * (maa_stack + xxx)
        w = jnp.exp(-jnp.exp(time_decay + jnp.tanh(x5[:, :, 1] @ decay_w1) @ decay_w2))
        w = w.reshape(b, l, H, S)
        r = (x5[:, :, 3] @ Wr.T).reshape(b, l, H, S)
        k = (x5[:, :, 0] @ Wk.T).reshape(b, l, H, S)
        v = (x5[:, :, 2] @ Wv.T).reshape(b, l, H, S)
        g = jax.nn.silu(x5[:, :, 4] @ Wg.T)
        s0 = state[:, (2 + S) * i + 2:(2 + S) * (i + 1)].reshape(b, H, S, S)
        u = faaaa[None, :, :, None]

        def step(s, rkvw):
            r_t, k_t, v_t, w_t = rkvw
            a = k_t[:, :, :, None] * v_t[:, :, None, :]
            out = jnp.einsum('bhk,bhkd->bhd', r_t, u * a + s)
            return (a + w_t[:, :, :, None] * s, out)
        xs = tuple((jnp.moveaxis(t, 1, 0) for t in (r, k, v, w)))
        _, outs = jax.lax.scan(step, s0, xs)
        att = jnp.moveaxis(outs, 0, 1).reshape(b, l, E)
        a4 = att.reshape(b, l, H, S)
        m = jnp.mean(a4, axis=-1, keepdims=True)
        var = jnp.mean((a4 - m) ** 2, axis=-1, keepdims=True)
        att = ((a4 - m) * jax.lax.rsqrt(var + EPS)).reshape(b, l, E) * gn_w + gn_b
        x = x + att * g @ Wo.T
        xn2 = _ln(x, ln2_w, ln2_b)
        sx2 = _token_shift(xn2, state[:, i0])
        xk = xn2 + sx2 * ffn_maa_k
        xr = xn2 + sx2 * ffn_maa_r
        rr = jax.nn.sigmoid(xr @ ffn_Wr.T)
        kk = jnp.square(jax.nn.relu(xk @ ffn_Wk.T))
        x = x + rr * (kk @ ffn_Wv.T)
        return x

    def _L1_xattn_ref(hidden_states, audio_kv, audio_attention_mask, Wq, Wk, Wv, Wo, ln_gamma, ln_beta, gate):
        import jax, jax.numpy as jnp
        import numpy as np
        HIDDEN = 512
        HEADS = 16
        HEAD_DIM = HIDDEN // HEADS
        LN_EPS = 1e-05
        GATE_INIT = 0.5

        def _layer_norm(x, gamma, beta):
            mu = jnp.mean(x, axis=-1, keepdims=True)
            var = jnp.mean(jnp.square(x - mu), axis=-1, keepdims=True)
            return (x - mu) * jax.lax.rsqrt(var + LN_EPS) * gamma + beta
        B, Tt, D = hidden_states.shape
        Ta = audio_kv.shape[1]
        scale = HEAD_DIM ** (-0.5)
        a = _layer_norm(audio_kv, ln_gamma, ln_beta)
        Q = (hidden_states @ Wq.T).reshape(B, Tt, HEADS, HEAD_DIM).transpose(0, 2, 1, 3)
        K = (a @ Wk.T).reshape(B, Ta, HEADS, HEAD_DIM).transpose(0, 2, 1, 3)
        V = (a @ Wv.T).reshape(B, Ta, HEADS, HEAD_DIM).transpose(0, 2, 1, 3)
        scores = jnp.einsum('bhtd,bhsd->bhts', Q, K) * scale
        mask = audio_attention_mask[:, None, None, :]
        scores = jnp.where(mask, scores, jnp.float32(-jnp.inf))
        attn = jax.nn.softmax(scores, axis=-1)
        out = jnp.einsum('bhts,bhsd->bhtd', attn, V)
        out = out.transpose(0, 2, 1, 3).reshape(B, Tt, D)
        out = out @ Wo.T
        return hidden_states + jnp.tanh(gate) * out
    x = _L0_xattn_ref(x, ctx_2048, L0_xattn_ln1_w, L0_xattn_ln1_b, L0_xattn_ln2_w, L0_xattn_ln2_b, L0_xattn_maa_x, L0_xattn_maa_w1, L0_xattn_maa_w2, L0_xattn_maa_stack, L0_xattn_time_decay, L0_xattn_decay_w1, L0_xattn_decay_w2, L0_xattn_faaaa, L0_xattn_Wr, L0_xattn_Wk, L0_xattn_Wv, L0_xattn_Wg, L0_xattn_Wo, L0_xattn_gn_w, L0_xattn_gn_b, L0_xattn_ffn_maa_k, L0_xattn_ffn_maa_r, L0_xattn_ffn_Wk, L0_xattn_ffn_Wr, L0_xattn_ffn_Wv, 0)
    x = _L1_xattn_ref(x, ctx_2048, mask_BxS2_bf1, L1_xattn_Wq, L1_xattn_Wk, L1_xattn_Wv, L1_xattn_Wo, L1_xattn_ln_gamma, L1_xattn_ln_beta, L1_xattn_gate)
    return x

_drawn_inputs = setup_inputs


def setup_inputs(seed=0):
    import zlib

    import numpy as np

    out = dict(_drawn_inputs(seed))
    spreads = {'L0_xattn_ln1_w': (1.0, 0.2),
     'L0_xattn_ln1_b': (0.0, 0.1),
     'L0_xattn_ln2_w': (1.0, 0.6),
     'L0_xattn_ln2_b': (0.0, 0.8),
     'L0_xattn_gn_w': (1.0, 0.6),
     'L0_xattn_gn_b': (0.0, 0.677),
     'L1_xattn_ln_gamma': (1.0, 0.6),
     'L1_xattn_ln_beta': (0.0, 0.8)}
    factors = {'L0_xattn_maa_x': 8.0,
     'L0_xattn_maa_w1': 2.878,
     'L0_xattn_maa_w2': 2.902,
     'L0_xattn_maa_stack': 6.325,
     'L0_xattn_decay_w1': 8.0,
     'L0_xattn_decay_w2': 8.0,
     'L0_xattn_faaaa': 2.986,
     'L0_xattn_ffn_maa_k': 8.0,
     'L0_xattn_ffn_maa_r': 8.0,
     'L0_xattn_ffn_Wr': 4.133,
     'L1_xattn_Wq': 8.0,
     'L1_xattn_Wk': 8.0}
    for name, (base, spread) in spreads.items():
        noise = np.random.default_rng([zlib.crc32(name.encode()), seed]).standard_normal(out[name].shape)
        drawn = base * np.exp(spread * noise) if base else spread * noise
        out[name] = jnp.asarray(drawn.astype(out[name].dtype))
    for name, factor in factors.items():
        out[name] = (out[name] * factor).astype(out[name].dtype)
    return out
```

```python
from contextlib import ExitStack

import numpy as np

import concourse.bass as bass
from concourse import mybir

F32 = mybir.dt.float32
F32R = mybir.dt.float32r
U8 = mybir.dt.uint8
ALU = mybir.AluOpType
ACT = mybir.ActivationFunctionType
AX = mybir.AxisListType

P = 128
B = 4
L = 512
E = 512
ET = E // P
S2 = 1024
H0, D0 = 32, 16
HT = P // D0
H1, D1 = 16, 32
G = H1 * D1 // P
GH = P // D1
KT = S2 // P
MIX, DEC = 32, 64
EPS = 1e-5
SCALE = D1 ** -0.5
MASKED = -1e30

VECS = ["ln1_w", "ln1_b", "ln2_w", "ln2_b", "maa_x", "maa0", "maa1", "maa2", "maa3", "maa4", "time_decay",
        "faaaa", "gn_w", "gn_b", "ffn_maa_k", "ffn_maa_r", "ln_gamma", "ln_beta"]
V_EPS = len(VECS) * ET
V_GATE = V_EPS + 1
NV = V_GATE + 1

QUAD = 32
ND = D0 // 4


def value_row(h, d):
    return QUAD * (d % 4) + HT * (d // 4) + h


ORDER = np.zeros(P, int)
for _h in range(HT):
    for _d in range(D0):
        ORDER[value_row(_h, _d)] = _h * D0 + _d
VALUE_ORDER = np.concatenate([m * P + ORDER for m in range(ET)])

C_MEAN = 0
C_HEAD = C_MEAN + P
C_BONUS = C_HEAD + P
C_HSUM = C_BONUS + P
C_ROW = C_HSUM + ET * H0
C_HBC = C_ROW + ND * QUAD
C_PICK = C_HBC + ET * P
C_IDENT = C_PICK + D0 * P
C_ONE = C_IDENT + P
C_ABC = C_ONE + G * D1
NC_ = C_ABC + G * P


def shape_constants():
    c = np.zeros((P, NC_), np.float32)
    c[:, C_IDENT:C_IDENT + P] = np.eye(P)
    c[:, C_MEAN:C_MEAN + P] = 1.0 / E
    key_head = np.arange(P) // D0
    value_head, value_chan = ORDER // D0, ORDER % D0
    c[:, C_HEAD:C_HEAD + P] = (value_head[:, None] == value_head[None, :]) / D0
    c[:, C_BONUS:C_BONUS + P] = key_head[:, None] == value_head[None, :]
    for m in range(ET):
        for h in range(HT):
            c[value_head == h, C_HSUM + m * H0 + m * HT + h] = 1.0 / D0
            c[m * HT + h, C_HBC + m * P:C_HBC + (m + 1) * P] = value_head == h
    for n in range(ND):
        for h in range(HT):
            c[key_head == h, C_ROW + n * QUAD + n * HT + h] = 1.0
    for d in range(D0):
        c[:, C_PICK + d * P:C_PICK + (d + 1) * P] = ((value_head[:, None] == key_head[None, :])
                                                     & (value_chan[:, None] == d))
    c[:, C_ONE + G:C_ONE + D1] = 1.0
    for g in range(G):
        c[:, C_ONE + g * D1 + g] = 1.0
        for j in range(GH):
            c[D1 * j + g, C_ABC + g * P + D1 * j:C_ABC + g * P + D1 * (j + 1)] = 1.0
    return c


class Count:

    def __init__(self, *stages):
        self.per, self.first = 0, {}
        for name, n in stages:
            self.first[name] = self.per
            self.per += n

    def __call__(self, b, name, i=0):
        return b * self.per + self.first[name] + i + 1


MIXES = [("decay", 1), ("receptance", 3), ("key", 0), ("gate", 4), ("value", 2)]

PAIR = 2
NPAIR = D0 // PAIR
NU = ET * NPAIR


def time_mix(nc, ctx, a, x2_dram):
    def sb(name, shape, dt=F32):
        return ctx.enter_context(nc.sbuf_tensor(name, shape, dt))

    def sem(name):
        return ctx.enter_context(nc.semaphore(name))

    vec = sb("vec", [P, NV])
    con = sb("con", [P, C_PICK])
    pick = sb("pick", [P, D0 * P], F32R)
    w_maa1 = sb("w_maa1", [P, ET, 5 * MIX])
    w_maa2 = sb("w_maa2", [P, 5, E], F32R)
    w_dec1 = sb("w_dec1", [P, ET, DEC])
    w_dec2 = sb("w_dec2", [DEC, E])
    WEIGHTS = [("receptance", "Wr"), ("key", "Wk"), ("gate", "Wg"), ("value", "Wv"), ("wo", "Wo"),
               ("ffn_k", "fWk"), ("ffn_r", "fWr"), ("ffn_v", "fWv")]
    W = {n: sb(f"w_{n}", [P, ET, E]) for n, _ in WEIGHTS}

    xin = sb("xin", [P, ET, L])
    x = sb("x", [P, ET, L])
    xc = sb("xc", [P, ET, L])
    sq = sb("sq", [P, ET, L])
    xn = sb("xn", [P, ET, L + 1])
    sx = sb("sx", [P, ET, L])
    xa = sb("xa", [P, ET * L])
    xb = sb("xb", [P, 2 * PAIR * (L + 1)])
    r_sb = sb("r_sb", [P, ET, L])
    k_sb = sb("k_sb", [P, ET, L])
    w_sb = sb("w_sb", [P, ET, L])
    g_sb = sb("g_sb", [P, ET, L])
    v_hi = sb("v_hi", [P, ET, L], F32R)
    v_lo = sb("v_lo", [P, ET, L], F32R)
    rstd = sb("rstd", [P, L])
    s0 = sb("s0", [P, ET, D0])
    prev = sb("prev", [P, ET, 2])

    mixed = [xa[:].rearrange("p (t l) -> p t l", t=ET), xb[:, 0:ET * L].rearrange("p (t l) -> p t l", t=ET)]
    kv = sq[:].rearrange("p (u i) l -> p u i l", u=2)
    rs = xa[:].rearrange("p (u i l) -> p u i l", u=2, i=PAIR)
    st = xb[:].rearrange("p (u i l) -> p u i l", u=2, i=PAIR)
    hid, hide = rstd, g_sb[0:MIX, 0, :]
    hid_hi, hid_lo = v_lo[:, 1, :], v_lo[:, 2, :]
    hid_stack = [v_hi[:, i, :] for i in range(4)] + [v_lo[:, 0, :]]
    dec = rstd[0:DEC, :]

    bank = ctx.enter_context(nc.psum_tensor("bank", [P, 8, L], F32))

    consts_loaded = sem("consts_loaded")
    vec_loaded = sem("vec_loaded")
    pick_loaded = sem("pick_loaded")
    pick_ready = sem("pick_ready")
    maa2_loaded = sem("maa2_loaded")
    maa2_rounded = sem("maa2_rounded")
    maa2_ready = sem("maa2_ready")
    x_loaded = sem("x_loaded")
    state_loaded = sem("state_loaded")
    bank_filled = sem("bank_filled")
    act_read = sem("act_read")
    dve_read = sem("dve_read")
    squared = sem("squared")
    inverted = sem("inverted")
    scaled = sem("scaled")
    first_ready = sem("first_ready")
    xn_ready = sem("xn_ready")
    shifted = sem("shifted")
    lora_in = sem("lora_in")
    hid_rounded = sem("hid_rounded")
    hid_split = sem("hid_split")
    hide_stacked = sem("hide_stacked")
    hid_stacked = sem("hid_stacked")
    mixed_ready = sem("mixed_ready")
    mix_filled = sem("mix_filled")
    mix_read = sem("mix_read")
    decayed = sem("decayed")
    bonus_in = sem("bonus_in")
    spread = sem("spread")
    kv_ready = sem("kv_ready")
    st_first = sem("st_first")
    st_ready = sem("st_ready")
    rs_ready = sem("rs_ready")
    rs_used = sem("rs_used")
    att_ready = sem("att_ready")
    head_affine = sem("head_affine")
    gated = sem("gated")
    kk_ready = sem("kk_ready")
    x2_ready = sem("x2_ready")
    x2_stored = sem("x2_stored")

    N_CONST = 16 * (4 + len(WEIGHTS))
    N_MIXED = 7

    fills = Count(("mean1", 1), ("var1", 1), ("hidden", 2), ("decay_in", 1), ("receptance", ET), ("decay", ET),
                  ("key", ET), ("gate", ET), ("value", ET), ("bonus", ET), ("head_mean", ET), ("head_var", 1),
                  ("head_rstd", ET), ("wo", ET), ("mean2", 1), ("var2", 1), ("ffn_k", ET), ("ffn_r", ET),
                  ("ffn_v", ET))
    act_reads = Count(("var1", 1), ("hidden", 2), ("decay_in", 1), ("receptance", ET), ("decay", ET), ("key", ET),
                      ("gate", ET), ("value", ET), ("head_var", 1), ("var2", 1), ("ffn_k", ET), ("ffn_r", ET))
    dve_reads = Count(("mean1", ET), ("gate", ET), ("value", ET), ("bonus", ET), ("head_mean", ET),
                      ("head_rstd", ET), ("wo", ET), ("mean2", ET), ("ffn_v", ET))
    squares = Count(("norm1", ET), ("head", ET), ("norm2", ET))
    inversions = Count(("norm1", 1), ("head", 1), ("norm2", 1))
    norms = Count(("norm1", ET), ("norm2", ET))
    MEAN, VAR, HIDDEN, DECAY_IN, HEAD_VAR = 0, 1, 2, 0, 4
    MIX_BANK, OUT_BANK = 4, 6

    block = ctx.enter_context(nc.Block())

    def v(name, t):
        c = VECS.index(name) * ET + t
        return vec[:, c:c + 1]

    def over_pair(ap):
        return ap.unsqueeze(1).to_broadcast([P, PAIR, L])

    @block.sync
    def _(sp):
        sp.dma_start(vec[:], a["vecs"]).then_inc(vec_loaded, 16)
        sp.dma_start(con[:], a["consts"][:, 0:C_PICK]).then_inc(consts_loaded, 16)

        def load_x(b):
            sp.dma_start(xin[:], a["xT"][bass.ds(b, 1)].rearrange("o p t l -> (o p) t l")).then_inc(x_loaded, 16)

        def load_state(b):
            for to, name in ((s0, "s0"), (prev, "prev")):
                sp.dma_start(to[:], a[name][bass.ds(b, 1)].rearrange("o p t d -> (o p) t d")).then_inc(state_loaded, 16)

        load_x(0)
        load_state(0)
        for q in range(4):
            src = a["maa_w2"].rearrange("(i r) n -> r i n", r=MIX)
            rows = slice(MIX * q, MIX * (q + 1))
            sp.dma_start(r_sb[rows, :, :], src[:, 0:4, :]).then_inc(maa2_loaded, 16)
            sp.dma_start(k_sb[rows, 0, :], src[:, 4, :]).then_inc(maa2_loaded, 16)
        sp.dma_start(w_maa1[:], a["maa_w1"].rearrange("(t p) n -> p t n", p=P)).then_inc(consts_loaded, 16)
        sp.dma_start(w_dec1[:], a["decay_w1"].rearrange("(t p) n -> p t n", p=P)).then_inc(consts_loaded, 16)
        sp.dma_start(w_dec2[:], a["decay_w2"]).then_inc(consts_loaded, 16)
        for name, src in WEIGHTS:
            sp.dma_start(W[name][:], a[src].rearrange("(t p) n -> p t n", p=P)).then_inc(consts_loaded, 16)

        def stack_hidden(b):
            sp.wait_ge(hid_split, b + 1)
            for i in range(4):
                rows = slice(MIX * i, MIX * (i + 1))
                for q in range(4):
                    sp.dma_start(hid_stack[i][MIX * q:MIX * (q + 1), :].bitcast(F32),
                                 (hid_hi, hid_lo)[q % 2][rows, :].bitcast(F32)).then_inc(hid_stacked, 16)

        def store(b):
            sp.wait_ge(x2_ready, b * ET + ET)
            sp.dma_start(x2_dram[bass.ds(b, 1)].rearrange("o p t l -> (o p) t l"), x[:]).then_inc(x2_stored, 16)

        with sp.Fori(0, B - 1) as b:
            stack_hidden(b)
            sp.wait_ge(dve_read, dve_reads(b, "wo", ET - 1))
            load_x(b + 1)
            store(b)
            sp.wait_ge(x2_stored, b * 16 + 16)
            load_state(b + 1)
        stack_hidden(B - 1)
        store(B - 1)
        sp.wait_ge(x2_stored, 16 * B)

    @block.gpsimd
    def _(pool):
        with pool.Fori(0, B) as b:
            for u in range(NU):
                m = u // NPAIR
                pool.wait_ge(st_first, b * NU + u + 1)
                pool.wait_ge(st_ready, b * NU + u + 1)
                if u < 2:
                    pool.wait_ge(bank_filled, fills(b, "value", ET - 1))
                else:
                    pool.wait_ge(rs_used, b * NU + u - 1)
                pool.tensor_tensor(rs[:, u % 2], st[:, u % 2, :, 0:L], over_pair(r_sb[:, m, :]),
                                   ALU.mult).then_inc(rs_ready, 1)

    @block.scalar
    def _(act):
        act.dma_start(xa[:], a["consts"][:, C_PICK:C_IDENT]).then_inc(pick_loaded, 16)
        act.wait_ge(pick_loaded, 16)
        act.activation(pick[:], xa[:], ACT.Copy).then_inc(pick_ready, 1)
        act.wait_ge(maa2_loaded, 16 * 8)
        act.activation(w_maa2[:, 0:4, :], r_sb[:], ACT.Copy).then_inc(maa2_rounded, 1)
        act.activation(w_maa2[:, 4, :], k_sb[:, 0, :], ACT.Copy).then_inc(maa2_rounded, 1)
        act.wait_ge(vec_loaded, 16)

        def norm(b, q, row):
            for t in range(ET):
                act.wait_ge(dve_read, dve_reads(b, f"mean{q}", t))
                act.activation(sq[:, t, :], xc[:, t, :], ACT.Square).then_inc(squared, 1)
            if q == 1:
                act.wait_ge(state_loaded, b * 32 + 32)
            act.activation(xn[:, :, 0:1], prev[:, :, row:row + 1], ACT.Copy).then_inc(first_ready, 1)
            act.wait_ge(bank_filled, fills(b, f"var{q}"))
            act.activation(rstd[:], bank[:, VAR, :], ACT.Sqrt, bias=vec[:, V_EPS:V_EPS + 1]).then_inc(act_read, 1)
            for t in range(ET):
                act.wait_ge(scaled, norms(b, f"norm{q}", t))
                act.activation(xn[:, t, 1:L + 1], xc[:, t, :], ACT.Identity, scale=v(f"ln{q}_w", t),
                               bias=v(f"ln{q}_b", t)).then_inc(xn_ready, 1)

        with act.Fori(0, B) as b:
            norm(b, 1, 1)
            act.wait_ge(bank_filled, fills(b, "hidden", 0))
            act.activation(hid[:], bank[:, HIDDEN, :], ACT.Tanh).then_inc(act_read, 1)
            act.wait_ge(act_read, act_reads(b, "hidden", 0))
            act.activation(hid_hi, hid[:], ACT.Copy).then_inc(hid_rounded, 1)
            act.wait_ge(bank_filled, fills(b, "hidden", 1))
            act.activation(hide, bank[0:MIX, HIDDEN + 1, :], ACT.Tanh).then_inc(act_read, 1)
            act.wait_ge(act_read, act_reads(b, "hidden", 1))
            act.activation(hid_stack[4][0:MIX, :], hide, ACT.Copy).then_inc(hid_rounded, 1)
            act.activation(hid_stack[4][2 * MIX:3 * MIX, :], hide, ACT.Copy).then_inc(hid_rounded, 1)
            act.wait_ge(bank_filled, fills(b, "decay_in"))
            act.activation(dec, bank[0:DEC, DECAY_IN, :], ACT.Tanh).then_inc(act_read, 1)
            for m in range(ET):
                act.wait_ge(bank_filled, fills(b, "receptance", m))
                act.activation(r_sb[:, m, :], bank[:, m, :], ACT.Copy).then_inc(act_read, 1)
            for m in range(ET):
                act.wait_ge(bank_filled, fills(b, "decay", m))
                act.activation(w_sb[:, m, :], bank[:, m, :], ACT.Exp, bias=v("time_decay", m)).then_inc(act_read, 1)
            for m in range(ET):
                act.wait_ge(act_read, act_reads(b, "decay", m))
                act.activation(w_sb[:, m, :], w_sb[:, m, :], ACT.Exp, scale=-1.0).then_inc(decayed, 1)
            for m in range(ET):
                act.wait_ge(bank_filled, fills(b, "key", m))
                act.activation(k_sb[:, m, :], bank[:, m, :], ACT.Copy).then_inc(act_read, 1)
            for m in range(ET):
                act.wait_ge(bank_filled, fills(b, "gate", m))
                act.activation(g_sb[:, m, :], bank[:, m, :], ACT.Tanh, scale=0.5).then_inc(act_read, 1)
            for m in range(ET):
                act.wait_ge(bank_filled, fills(b, "value", m))
                act.activation(xc[:, m, :], bank[:, m, :], ACT.Copy)
                act.activation(v_hi[:, m, :], bank[:, m, :], ACT.Copy).then_inc(act_read, 1)
            for u in range(NU):
                m, c = u // NPAIR, (u % NPAIR) * PAIR
                if u >= 2:
                    act.wait_ge(rs_ready, b * NU + u - 1)
                act.activation(st[:, u % 2, :, 0:1], s0[:, m, c:c + PAIR].unsqueeze(2), ACT.Copy).then_inc(st_first, 1)
            for m in range(ET):
                act.wait_ge(dve_read, dve_reads(b, "head_mean", m))
                act.activation(sq[:, m, :], xc[:, m, :], ACT.Square).then_inc(squared, 1)
            act.wait_ge(bank_filled, fills(b, "head_var"))
            act.activation(rstd[0:H0, :], bank[0:H0, HEAD_VAR, :], ACT.Sqrt,
                           bias=vec[0:H0, V_EPS:V_EPS + 1]).then_inc(act_read, 1)
            for m in range(ET):
                act.wait_ge(dve_read, dve_reads(b, "head_rstd", m))
                act.activation(xc[:, m, :], xc[:, m, :], ACT.Identity, scale=v("gn_w", m),
                               bias=v("gn_b", m)).then_inc(head_affine, 1)
            norm(b, 2, 0)
            for m in range(ET):
                act.wait_ge(bank_filled, fills(b, "ffn_k", m))
                act.activation(k_sb[:, m, :], bank[:, m, :], ACT.Relu).then_inc(act_read, 1)
            for m in range(ET):
                act.wait_ge(act_read, act_reads(b, "ffn_k", m))
                act.activation(k_sb[:, m, :], k_sb[:, m, :], ACT.Square).then_inc(kk_ready, 1)
            for m in range(ET):
                act.wait_ge(bank_filled, fills(b, "ffn_r", m))
                act.activation(r_sb[:, m, :], bank[:, m, :], ACT.Tanh, scale=0.5).then_inc(act_read, 1)

    @block.vector
    def _(dve):
        dve.wait_ge(vec_loaded, 16)
        dve.wait_ge(maa2_rounded, 2)
        half = slice(2 * MIX, 4 * MIX)
        dve.tensor_tensor(w_maa2[half, 0:4, :], r_sb[half, :, :], w_maa2[half, 0:4, :].bitcast(F32),
                          ALU.subtract).then_inc(maa2_ready, 1)
        dve.tensor_tensor(w_maa2[half, 4, :], k_sb[half, 0, :], w_maa2[half, 4, :].bitcast(F32),
                          ALU.subtract).then_inc(maa2_ready, 1)

        def norm(b, q, src):
            dve.wait_ge(bank_filled, fills(b, f"mean{q}"))
            for t in range(ET):
                dve.tensor_tensor(xc[:, t, :], src[:, t, :], bank[:, MEAN, :], ALU.subtract).then_inc(dve_read, 1)
            dve.wait_ge(act_read, act_reads(b, f"var{q}"))
            dve.reciprocal(rstd[:], rstd[:]).then_inc(inverted, 1)
            dve.wait_ge(inverted, inversions(b, f"norm{q}"))
            for t in range(ET):
                dve.tensor_tensor(xc[:, t, :], xc[:, t, :], rstd[:], ALU.mult).then_inc(scaled, 1)
            dve.wait_ge(first_ready, b * 2 + q)
            for t in range(ET):
                dve.wait_ge(xn_ready, norms(b, f"norm{q}", t))
                dve.tensor_tensor(sx[:, t, :], xn[:, t, 0:L], xn[:, t, 1:L + 1], ALU.subtract).then_inc(shifted, 1)

        def kv_pair(b, u):
            m = u // NPAIR
            dve.wait_ge(spread, b * NU + u + 1)
            if u >= 2:
                dve.wait_ge(st_ready, b * NU + u - 1)
            c = PAIR * (u % 3)
            dve.tensor_tensor(kv[:, u % 2], bank[:, c:c + PAIR, :], over_pair(k_sb[:, m, :]),
                              ALU.mult).then_inc(kv_ready, 1)

        def attention_tile(b, m):
            dve.wait_ge(rs_used, b * NU + NPAIR * (m + 1))
            dve.tensor_tensor(xc[:, m, :], xc[:, m, :], bank[:, OUT_BANK + m % 2, :], ALU.add).then_inc(att_ready, 1)

        with dve.Fori(0, B) as b:
            norm(b, 1, xin)
            for t in range(ET):
                dve.wait_ge(shifted, norms(b, "norm1", t))
                dve.scalar_tensor_tensor(out=sq[:, t, :], in0=sx[:, t, :], scalar=v("maa_x", t),
                                         in1=xn[:, t, 1:L + 1], op0=ALU.mult, op1=ALU.add).then_inc(lora_in, 1)
            dve.wait_ge(hid_rounded, b * 3 + 1)
            dve.tensor_tensor(hid_lo, hid[:], hid_hi.bitcast(F32), ALU.subtract).then_inc(hid_split, 1)
            dve.wait_ge(hid_rounded, b * 3 + 3)
            for q in (1, 3):
                dve.tensor_tensor(hid_stack[4][MIX * q:MIX * (q + 1), :], hide, hid_stack[4][0:MIX, :].bitcast(F32),
                                  ALU.subtract).then_inc(hide_stacked, 1)
            last_use = [("decay_in", 0)] + [(name, ET - 1) for name, _ in MIXES[1:]]
            for s, (name, i) in enumerate(MIXES):
                to = mixed[s % 2]
                if s >= 2:
                    dve.wait_ge(bank_filled, fills(b, *last_use[s - 2]))
                for t in range(ET):
                    dve.wait_ge(mix_filled, b * 5 * ET + s * ET + t + 1)
                    dve.scalar_tensor_tensor(out=to[:, t, :], in0=bank[:, MIX_BANK + t, :], scalar=v(f"maa{i}", t),
                                             in1=sx[:, t, :], op0=ALU.add, op1=ALU.mult).then_inc(mix_read, 1)
                dve.wait_ge(mix_read, b * 5 * ET + s * ET + ET)
                dve.tensor_tensor(to, to, xn[:, :, 1:L + 1], ALU.add).then_inc(mixed_ready, 1)
            for m in range(ET):
                dve.wait_ge(act_read, act_reads(b, "key", m))
                dve.scalar_tensor_tensor(out=sq[:, m, :], in0=r_sb[:, m, :], scalar=v("faaaa", m),
                                         in1=k_sb[:, m, :], op0=ALU.mult, op1=ALU.mult).then_inc(bonus_in, 1)
            for m in range(ET):
                dve.wait_ge(act_read, act_reads(b, "gate", m))
                dve.scalar_tensor_tensor(out=g_sb[:, m, :], in0=g_sb[:, m, :], scalar=1.0, in1=bank[:, m, :],
                                         op0=ALU.add, op1=ALU.mult).then_inc(dve_read, 1)
            for m in range(ET):
                dve.wait_ge(act_read, act_reads(b, "value", m))
                dve.tensor_tensor(v_lo[:, m, :], bank[:, m, :], v_hi[:, m, :].bitcast(F32),
                                  ALU.subtract).then_inc(dve_read, 1)
            for m in range(ET):
                dve.wait_ge(bank_filled, fills(b, "bonus", m))
                dve.tensor_tensor(xc[:, m, :], bank[:, m, :], xc[:, m, :], ALU.mult).then_inc(dve_read, 1)
            dve.wait_ge(decayed, b * ET + ET)
            kv_pair(b, 0)
            for u in range(NU):
                m, c = u // NPAIR, (u % NPAIR) * PAIR
                if u + 1 < NU:
                    kv_pair(b, u + 1)
                dve.wait_ge(kv_ready, b * NU + u + 1)
                if u >= 2:
                    dve.wait_ge(rs_ready, b * NU + u - 1)
                for i in range(PAIR):
                    scan = dve.tensor_tensor_scan(st[:, u % 2, i, 1:L + 1], w_sb[:, m, :], kv[:, u % 2, i, :],
                                                  s0[:, m, c + i:c + i + 1], ALU.mult, ALU.add)
                scan.then_inc(st_ready, 1)
                if u % NPAIR == 4 and m >= 1:
                    attention_tile(b, m - 1)
            attention_tile(b, ET - 1)
            for m in range(ET):
                dve.wait_ge(bank_filled, fills(b, "head_mean", m))
                dve.tensor_tensor(xc[:, m, :], xc[:, m, :], bank[:, m, :], ALU.subtract).then_inc(dve_read, 1)
            dve.wait_ge(act_read, act_reads(b, "head_var"))
            dve.reciprocal(rstd[0:H0, :], rstd[0:H0, :]).then_inc(inverted, 1)
            for m in range(ET):
                dve.wait_ge(bank_filled, fills(b, "head_rstd", m))
                dve.tensor_tensor(xc[:, m, :], xc[:, m, :], bank[:, m, :], ALU.mult).then_inc(dve_read, 1)
            for m in range(ET):
                dve.wait_ge(head_affine, b * ET + m + 1)
                dve.scalar_tensor_tensor(out=xc[:, m, :], in0=xc[:, m, :], scalar=0.5, in1=g_sb[:, m, :],
                                         op0=ALU.mult, op1=ALU.mult).then_inc(gated, 1)
            for m in range(ET):
                dve.wait_ge(bank_filled, fills(b, "wo", m))
                dve.tensor_tensor(x[:, m, :], xin[:, m, :], bank[:, m, :], ALU.add).then_inc(dve_read, 1)
            norm(b, 2, x)
            dve.wait_ge(shifted, norms(b, "norm2", ET - 1))
            for s, name in enumerate(["ffn_maa_k", "ffn_maa_r"]):
                for t in range(ET):
                    ins = dve.scalar_tensor_tensor(out=mixed[s][:, t, :], in0=sx[:, t, :], scalar=v(name, t),
                                                   in1=xn[:, t, 1:L + 1], op0=ALU.mult, op1=ALU.add)
                ins.then_inc(mixed_ready, 1)
            for m in range(ET):
                dve.wait_ge(bank_filled, fills(b, "ffn_v", m))
                dve.scalar_tensor_tensor(out=w_sb[:, m, :], in0=r_sb[:, m, :], scalar=1.0, in1=bank[:, m, :],
                                         op0=ALU.add, op1=ALU.mult).then_inc(dve_read, 1)
            for m in range(ET):
                dve.wait_ge(dve_read, dve_reads(b, "ffn_v", m))
                dve.scalar_tensor_tensor(out=x[:, m, :], in0=w_sb[:, m, :], scalar=0.5, in1=x[:, m, :],
                                         op0=ALU.mult, op1=ALU.add).then_inc(x2_ready, 1)

    @block.tensor
    def _(pe):
        def rows(to, pairs):
            for n, (lhsT, rhs) in enumerate(pairs):
                ins = pe.matmul(to, lhsT, rhs, start=(n == 0), stop=(n == len(pairs) - 1))
            return ins

        def project(m, weight, src):
            return rows(bank[:, m, :], [(weight[:, t, m * P:(m + 1) * P], src[:, t, :]) for t in range(ET)])

        def norm(b, q, src):
            mean = con[:, C_MEAN:C_MEAN + P]
            rows(bank[:, MEAN, :], [(mean, src[:, t, :]) for t in range(ET)]).then_inc(bank_filled, 1)
            for t in range(ET):
                pe.wait_ge(squared, squares(b, f"norm{q}", t))
                ins = pe.matmul(bank[:, VAR, :], mean, sq[:, t, :], start=(t == 0), stop=(t == ET - 1))
            ins.then_inc(bank_filled, 1)

        def low_rank(b, s):
            i = MIXES[s][1]
            for t in range(ET):
                if s >= 1:
                    pe.wait_ge(mix_read, b * 5 * ET + (s - 1) * ET + t + 1)
                pe.matmul(bank[:, MIX_BANK + t, :], w_maa2[:, i, t * P:(t + 1) * P], hid_stack[i], start=True,
                          stop=True).then_inc(mix_filled, 1)

        def sum_pair(b, u):
            m, c = u // NPAIR, (u % NPAIR) * PAIR
            if u % NPAIR == 0 and m >= 2:
                pe.wait_ge(att_ready, b * ET + m - 1)
            pe.wait_ge(rs_ready, b * NU + u + 1)
            for i in range(PAIR):
                q, n = (c + i) % 4, (c + i) // 4
                ins = pe.matmul(bank[QUAD * q:QUAD * (q + 1), OUT_BANK + m % 2, :],
                                con[:, C_ROW + n * QUAD:C_ROW + (n + 1) * QUAD], rs[:, u % 2, i, :],
                                start=(n == 0), stop=(n == ND - 1))
            ins.then_inc(rs_used, 1)

        pe.wait_ge(consts_loaded, N_CONST)
        pe.wait_ge(pick_ready, 1)
        pe.wait_ge(maa2_ready, 2)
        with pe.Fori(0, B) as b:
            pe.wait_ge(x_loaded, b * 16 + 16)
            norm(b, 1, xin)
            for n, cols in enumerate((slice(0, P), slice(P, 5 * MIX))):
                for t in range(ET):
                    pe.wait_ge(lora_in, b * ET + t + 1)
                    ins = pe.matmul(bank[0:cols.stop - cols.start, HIDDEN + n, :], w_maa1[:, t, cols], sq[:, t, :],
                                    start=(t == 0), stop=(t == ET - 1))
                ins.then_inc(bank_filled, 1)
            pe.wait_ge(hid_stacked, b * 256 + 256)
            pe.wait_ge(hide_stacked, b * 2 + 2)
            low_rank(b, 0)
            low_rank(b, 1)
            pe.wait_ge(mixed_ready, b * N_MIXED + 1)
            rows(bank[0:DEC, DECAY_IN, :],
                 [(w_dec1[:, t, :], mixed[0][:, t, :]) for t in range(ET)]).then_inc(bank_filled, 1)
            low_rank(b, 2)
            pe.wait_ge(mixed_ready, b * N_MIXED + 2)
            pe.wait_ge(act_read, act_reads(b, "decay_in"))
            for m in range(ET):
                project(m, W["receptance"], mixed[1]).then_inc(bank_filled, 1)
            for m in range(ET):
                pe.wait_ge(act_read, act_reads(b, "receptance", m))
                rows(bank[:, m, :], [(w_dec2[:, m * P:(m + 1) * P], dec)]).then_inc(bank_filled, 1)
            low_rank(b, 3)
            pe.wait_ge(mixed_ready, b * N_MIXED + 3)
            for m in range(ET):
                pe.wait_ge(act_read, act_reads(b, "decay", m))
                project(m, W["key"], mixed[0]).then_inc(bank_filled, 1)
            low_rank(b, 4)
            pe.wait_ge(mixed_ready, b * N_MIXED + 4)
            for m in range(ET):
                pe.wait_ge(act_read, act_reads(b, "key", m))
                project(m, W["gate"], mixed[1]).then_inc(bank_filled, 1)
            pe.wait_ge(mixed_ready, b * N_MIXED + 5)
            for m in range(ET):
                pe.wait_ge(dve_read, dve_reads(b, "gate", m))
                project(m, W["value"], mixed[0]).then_inc(bank_filled, 1)
            for m in range(ET):
                pe.wait_ge(bonus_in, b * ET + m + 1)
                pe.wait_ge(dve_read, dve_reads(b, "value", m))
                rows(bank[:, m, :], [(con[:, C_BONUS:C_BONUS + P], sq[:, m, :])]).then_inc(bank_filled, 1)
            pe.wait_ge(dve_read, dve_reads(b, "bonus", ET - 1))
            for u in range(NU):
                m, c = u // NPAIR, (u % NPAIR) * PAIR
                if u >= 3:
                    pe.wait_ge(kv_ready, b * NU + u - 2)
                for i in range(PAIR):
                    to_d = pick[:, (c + i) * P:(c + i + 1) * P]
                    ins = rows(bank[:, PAIR * (u % 3) + i, :], [(to_d, v_hi[:, m, :]), (to_d, v_lo[:, m, :])])
                ins.then_inc(spread, 1)
                if u >= 2:
                    sum_pair(b, u - 2)
            sum_pair(b, NU - 2)
            sum_pair(b, NU - 1)
            pe.wait_ge(kv_ready, b * NU + NU)
            for m in range(ET):
                pe.wait_ge(att_ready, b * ET + m + 1)
                rows(bank[:, m, :], [(con[:, C_HEAD:C_HEAD + P], xc[:, m, :])]).then_inc(bank_filled, 1)
            for m in range(ET):
                pe.wait_ge(squared, squares(b, "head", m))
                ins = pe.matmul(bank[0:H0, HEAD_VAR, :], con[:, C_HSUM + m * H0:C_HSUM + (m + 1) * H0], sq[:, m, :],
                                start=(m == 0), stop=(m == ET - 1))
            ins.then_inc(bank_filled, 1)
            pe.wait_ge(inverted, inversions(b, "head"))
            for m in range(ET):
                rows(bank[:, m, :], [(con[:, C_HBC + m * P:C_HBC + (m + 1) * P], rstd[:])]).then_inc(bank_filled, 1)
            pe.wait_ge(gated, b * ET + ET)
            for m in range(ET):
                project(m, W["wo"], xc).then_inc(bank_filled, 1)
            pe.wait_ge(dve_read, dve_reads(b, "wo", ET - 1))
            norm(b, 2, x)
            pe.wait_ge(mixed_ready, b * N_MIXED + 6)
            for m in range(ET):
                project(m, W["ffn_k"], mixed[0]).then_inc(bank_filled, 1)
            pe.wait_ge(mixed_ready, b * N_MIXED + 7)
            for m in range(ET):
                pe.wait_ge(act_read, act_reads(b, "ffn_k", m))
                project(m, W["ffn_r"], mixed[1]).then_inc(bank_filled, 1)
            pe.wait_ge(kk_ready, b * ET + ET)
            for m in range(ET):
                pe.wait_ge(act_read, act_reads(b, "ffn_r", m))
                project(m, W["ffn_v"], k_sb).then_inc(bank_filled, 1)
            pe.wait_ge(dve_read, dve_reads(b, "ffn_v", ET - 1))


MAX_ROW, MASK_ROW = 3 * QUAD, 3 * QUAD + 1
HALF = S2 // L
NS = HALF * GH * ET
NPT = 3
N_STEP = G * KT


def cross_attention(nc, ctx, a, x2_dram, out_dram):
    def sb(name, shape, dt=F32):
        return ctx.enter_context(nc.sbuf_tensor(name, shape, dt))

    def sem(name):
        return ctx.enter_context(nc.semaphore(name))

    vec = sb("vec2", [P, NV])
    ident = sb("ident", [P, P])
    mean_w = sb("mean_w", [P, P])
    one = sb("one", [P, G * D1])
    spread_w = sb("spread_w", [P, G * P])
    W = {n: sb(f"w2_{n}", [P, ET, E]) for n in ["Wk2", "Wq2", "Wv2", "Wo2"]}
    tg = sb("tg", [P, 1])

    c = sb("ctx_rows", [P, ET, S2])
    sq = sb("sq2", [P, ET, S2])
    xq = sb("xq", [P, ET, L])
    xr = sb("xr", [P, ET, L])
    rstd = sb("rstd2", [P, HALF, L])
    mask8 = sb("mask8", [1, S2], U8)
    maskf = sb("maskf", [1, S2], F32R)
    vals = sb("vals", [P, KT, E])
    k_hi = sb("k_hi", [P, S2], F32R)
    k_lo = sb("k_lo", [P, S2], F32R)
    q_hi = sb("q_hi", [P, L], F32R)
    q_lo = sb("q_lo", [P, L], F32R)
    ka = sb("ka", [P, 2, GH, S2], F32R)
    qa = sb("qa", [P, 2, GH, L], F32R)
    pt = sb("pt", [P, NPT, GH, L])
    mx = sb("mx", [P, HALF, GH * ET])
    mxx = sb("mxx", [P, GH * ET])
    mt = sb("mt", [GH * ET, P], F32R)
    ssum = sb("ssum", [P, L])
    o = sb("o", [P, G, L])

    bank = ctx.enter_context(nc.psum_tensor("bank2", [P, 8, L], F32))
    EXP, OUT, SUM = 2, 6, 7

    consts_loaded = sem("consts_loaded2")
    rows_zeroed = sem("rows_zeroed")
    rows_set = sem("rows_set")
    c_loaded = sem("c_loaded")
    xq_loaded = sem("xq_loaded")
    xr_loaded = sem("xr_loaded")
    mask_loaded = sem("mask_loaded")
    mask_made = sem("mask_made")
    mask_placed = sem("mask_placed")
    gate_ready = sem("gate_ready")
    mean_filled = sem("mean_filled")
    var_filled = sem("var_filled")
    kq_filled = sem("kq_filled")
    scores_filled = sem("scores_filled")
    max_turned = sem("max_turned")
    values_filled = sem("values_filled")
    sum_spread = sem("sum_spread")
    out_filled = sem("out_filled")
    centred = sem("centred2")
    squared = sem("squared2")
    sd_ready = sem("sd_ready")
    inverted = sem("inverted2")
    scaled = sem("scaled2")
    normed = sem("normed2")
    kq_high = sem("kq_high")
    kq_low = sem("kq_low")
    max_row_clear = sem("max_row_clear")
    placed = sem("placed")
    scores_read = sem("scores_read")
    max_ready = sem("max_ready")
    max_taken = sem("max_taken")
    max_placed = sem("max_placed")
    values_read = sem("values_read")
    scored = sem("scored")
    exp_done = sem("exp_done")
    pv_done = sem("pv_done")
    o_read = sem("o_read")
    sum_inverted = sem("sum_inverted")
    o_normed = sem("o_normed")
    out_done = sem("out_done")
    out_stored = sem("out_stored")

    N_CONST = 16 * 9
    N_PLACED = 16 * 6 * GH
    N_MASK = 16 * GH
    N_EXP = 2 * N_STEP

    block = ctx.enter_context(nc.Block())

    def v(name, t):
        i = VECS.index(name) * ET + t
        return vec[:, i:i + 1]

    def tile_half(x, t, h):
        return x[:, t, h * L:(h + 1) * L]


    @block.sync
    def _(sp):
        def load(b):
            sp.dma_start(c[:], a["ctxT"][bass.ds(b, 1)].rearrange("o p t l -> (o p) t l")).then_inc(c_loaded, 16)
            sp.dma_start(mask8[:], a["mask"][bass.ds(b, 1)]).then_inc(mask_loaded, 16)
            sp.dma_start(xq[:], x2_dram[bass.ds(b, 1)].rearrange("o p t l -> (o p) t l")).then_inc(xq_loaded, 16)

        def load_residual(b):
            sp.dma_start(xr[:], x2_dram[bass.ds(b, 1)].rearrange("o p t l -> (o p) t l")).then_inc(xr_loaded, 16)

        load(0)
        sp.dma_start(vec[:], a["vecs"]).then_inc(consts_loaded, 16)
        sp.dma_start(mean_w[:], a["consts"][:, C_MEAN:C_MEAN + P]).then_inc(consts_loaded, 16)
        for n in W:
            sp.dma_start(W[n][:], a[n].rearrange("(t p) n -> p t n", p=P)).then_inc(consts_loaded, 16)
        sp.dma_start(ident[:], a["consts"][:, C_IDENT:C_IDENT + P]).then_inc(consts_loaded, 16)
        sp.dma_start(one[:], a["consts"][:, C_ONE:C_ABC]).then_inc(consts_loaded, 16)
        sp.dma_start(spread_w[:], a["consts"][:, C_ABC:NC_]).then_inc(consts_loaded, 16)
        load_residual(0)

        def place_group(b, g):
            sp.wait_ge(kq_low, (b * G + g) * 3 + 3)
            for j in range(GH):
                rows = slice(QUAD * j, QUAD * (j + 1))
                for to, parts in ((qa, (q_hi, q_hi, q_lo)), (ka, (k_hi, k_lo, k_hi))):
                    for n, part in enumerate(parts):
                        sp.dma_start(to[QUAD * n:QUAD * (n + 1), g % 2, j, :].bitcast(F32),
                                     part[rows, :].bitcast(F32)).then_inc(placed, 16)
            if g < 2:
                sp.wait_ge(mask_made, b + 1)
                for j in range(GH):
                    sp.dma_start(ka[MASK_ROW:MASK_ROW + 1, g, j, :].bitcast(F32),
                                 maskf[:].bitcast(F32)).then_inc(mask_placed, 16)

        def place_max(b, g):
            sp.wait_ge(max_taken, b * G + g + 1)
            sp.dma_start(qa[MAX_ROW:MAX_ROW + 1, g % 2, :, :].bitcast(F32).rearrange("o j (q l) -> o (j q) l", l=P),
                         mt[:].bitcast(F32)).then_inc(max_placed, 16)

        def batch(b, prepare):
            for g in range(1, G):
                place_group(b, g)
                if g == G - 1 and prepare:
                    load(b + 1)
                place_max(b, g)
            if prepare:
                place_group(b + 1, 0)
            sp.wait_ge(out_done, b * ET + ET)
            sp.dma_start(out_dram[bass.ds(b, 1)].rearrange("o p t l -> (o p) t l"), xr[:]).then_inc(out_stored, 16)
            if prepare:
                place_max(b + 1, 0)
                sp.wait_ge(out_stored, b * 16 + 16)
                load_residual(b + 1)

        sp.wait_ge(rows_set, 2)
        place_group(0, 0)
        place_max(0, 0)
        with sp.Fori(0, B - 1) as b:
            batch(b, True)
        batch(B - 1, False)
        sp.wait_ge(out_stored, 16 * B)

    @block.gpsimd
    def _(pool):
        last = slice(MAX_ROW, P)
        pool.memset(ka[last, :, :, :].bitcast(F32), 0.0).then_inc(rows_zeroed, 1)
        pool.memset(qa[last, :, :, :].bitcast(F32), 0.0).then_inc(rows_zeroed, 1)
        pool.wait_ge(rows_zeroed, 2)
        pool.memset(ka[MAX_ROW:MASK_ROW + 1, :, :, :].bitcast(F32), -1.0).then_inc(rows_set, 1)
        pool.memset(qa[MAX_ROW:MASK_ROW + 1, :, :, :].bitcast(F32), 1.0).then_inc(rows_set, 1)
        pool.wait_ge(rows_set, 2)
        with pool.Fori(0, B) as b:
            for g in range(G):
                pool.wait_ge(kq_filled, (b * G + g) * 3 + 3)
                row = qa[MAX_ROW:MAX_ROW + 1, g % 2, :, :]
                pool.tensor_tensor(row, row.bitcast(F32), row.bitcast(F32), ALU.subtract).then_inc(max_row_clear, 1)

    @block.scalar
    def _(act):
        act.wait_ge(consts_loaded, N_CONST)
        act.activation(tg[:], vec[:, V_GATE:V_GATE + 1], ACT.Tanh).then_inc(gate_ready, 1)

        def squares(b):
            for h in range(HALF):
                for t in range(ET):
                    act.wait_ge(centred, b * HALF * ET + h * ET + t + 1)
                    act.activation(tile_half(sq, t, h), tile_half(c, t, h), ACT.Square).then_inc(squared, 1)

        def deviations(b):
            for h in range(HALF):
                act.wait_ge(var_filled, b * HALF + h + 1)
                act.activation(rstd[:, h, :], bank[:, h, :], ACT.Sqrt, bias=vec[:, V_EPS:V_EPS + 1]).then_inc(sd_ready, 1)

        def affine(b):
            for h in range(HALF):
                for t in range(ET):
                    act.wait_ge(scaled, b * HALF * ET + h * ET + t + 1)
                    act.activation(tile_half(c, t, h), tile_half(c, t, h), ACT.Identity, scale=v("ln_gamma", t),
                                   bias=v("ln_beta", t)).then_inc(normed, 1)

        def keys_queries(b, g):
            n = (b * G + g) * 3
            if g >= 1:
                act.wait_ge(placed, (b * G + g) * N_PLACED)
            for h in range(HALF):
                act.wait_ge(kq_filled, n + h + 1)
                act.activation(k_hi[:, h * L:(h + 1) * L], bank[:, h, :], ACT.Copy).then_inc(kq_high, 1)
            act.wait_ge(kq_filled, n + 3)
            act.activation(q_hi[:], bank[:, 0, :], ACT.Copy).then_inc(kq_high, 1)

        def values(b):
            for i in range(KT):
                act.wait_ge(values_filled, b * KT + i + 1)
                act.activation(vals[:, i, :], bank[:, EXP + i % 4, :], ACT.Copy).then_inc(values_read, 1)

        def exponentials(b, step):
            for u in range(2):
                n = 2 * step + u
                act.wait_ge(scored, b * N_EXP + n + 1)
                if u == 0 and step >= NPT:
                    act.wait_ge(pv_done, b * N_STEP + step - NPT + 1)
                e = EXP + 2 * (n % 2)
                act.activation(pt[:, step % NPT, 2 * u:2 * u + 2, :], bank[:, e:e + 2, :], ACT.Exp,
                               scale=SCALE).then_inc(exp_done, 1)

        def group_out(b, g):
            act.wait_ge(pv_done, b * N_STEP + g * KT + KT)
            act.activation(o[:, g, :], bank[:, OUT, :], ACT.Copy).then_inc(o_read, 1)

        def batch(b, prepare):
            for g in range(G):
                if g + 1 < G:
                    keys_queries(b, g + 1)
                if g >= 1:
                    group_out(b, g - 1)
                for kt in range(KT):
                    exponentials(b, g * KT + kt)
                    if g == G - 1 and prepare:
                        if kt == 0:
                            squares(b + 1)
                        if kt == 3:
                            deviations(b + 1)
            group_out(b, G - 1)
            if prepare:
                affine(b + 1)
                keys_queries(b + 1, 0)
                values(b + 1)

        squares(0)
        deviations(0)
        affine(0)
        keys_queries(0, 0)
        values(0)
        with act.Fori(0, B - 1) as b:
            batch(b, True)
        batch(B - 1, False)

    @block.vector
    def _(dve):
        def centre(b):
            dve.wait_ge(mask_loaded, b * 16 + 16)
            dve.tensor_scalar(maskf[:], mask8[:], 1.0, -MASKED, ALU.subtract, ALU.mult).then_inc(mask_made, 1)
            for h in range(HALF):
                dve.wait_ge(mean_filled, b * HALF + h + 1)
                for t in range(ET):
                    dve.tensor_tensor(tile_half(c, t, h), tile_half(c, t, h), bank[:, h, :],
                                      ALU.subtract).then_inc(centred, 1)

        def scale(b):
            for h in range(HALF):
                dve.wait_ge(sd_ready, b * HALF + h + 1)
                dve.reciprocal(rstd[:, h, :], rstd[:, h, :]).then_inc(inverted, 1)
                dve.wait_ge(inverted, b * HALF + h + 1)
                for t in range(ET):
                    dve.tensor_tensor(tile_half(c, t, h), tile_half(c, t, h), rstd[:, h, :],
                                      ALU.mult).then_inc(scaled, 1)

        def keys_queries(b, g):
            n = (b * G + g) * 3
            for h in range(HALF):
                dve.wait_ge(kq_high, n + h + 1)
                s = slice(h * L, (h + 1) * L)
                dve.tensor_tensor(k_lo[:, s], bank[:, h, :], k_hi[:, s].bitcast(F32), ALU.subtract).then_inc(kq_low, 1)
            dve.wait_ge(kq_high, n + 3)
            dve.tensor_tensor(q_lo[:], bank[:, 0, :], q_hi[:].bitcast(F32), ALU.subtract).then_inc(kq_low, 1)

        def maxima(b, g):
            gi = b * G + g
            for i in range(NS):
                dve.wait_ge(scores_filled, gi * NS + i + 1)
                n = i // HALF
                dve.reduce_max(mx[:, i % HALF, n:n + 1], bank[:, (i + 1) % 2, :], AX.X).then_inc(scores_read, 1)
            dve.wait_ge(scores_read, gi * NS + NS)
            dve.tensor_tensor(mxx[:], mx[:, 0, :], mx[:, 1, :], ALU.max).then_inc(max_ready, 1)
            dve.wait_ge(max_turned, gi + 1)
            dve.tensor_copy(mt[:], bank[0:GH * ET, 1, 0:P]).then_inc(max_taken, 1)

        def batch(b, prepare):
            for g in range(1, G):
                keys_queries(b, g)
                maxima(b, g)
            if prepare:
                dve.wait_ge(mask_placed, b * 2 * N_MASK + 2 * N_MASK)
                centre(b + 1)
                scale(b + 1)
                keys_queries(b + 1, 0)
            dve.wait_ge(pv_done, b * N_STEP + N_STEP)
            dve.reciprocal(ssum[:], bank[:, SUM, :]).then_inc(sum_inverted, 1)
            for g in range(G):
                dve.wait_ge(sum_spread, b * G + g + 1)
                dve.wait_ge(o_read, b * G + g + 1)
                dve.tensor_tensor(o[:, g, :], o[:, g, :], bank[:, EXP + g, :], ALU.mult).then_inc(o_normed, 1)
            dve.wait_ge(xr_loaded, b * 16 + 16)
            for m in range(ET):
                dve.wait_ge(out_filled, b * ET + m + 1)
                dve.scalar_tensor_tensor(out=xr[:, m, :], in0=bank[:, EXP + m, :], scalar=tg[:, 0:1],
                                         in1=xr[:, m, :], op0=ALU.mult, op1=ALU.add).then_inc(out_done, 1)
            if prepare:
                maxima(b + 1, 0)

        centre(0)
        scale(0)
        keys_queries(0, 0)
        dve.wait_ge(gate_ready, 1)
        maxima(0, 0)
        with dve.Fori(0, B - 1) as b:
            batch(b, True)
        batch(B - 1, False)

    @block.tensor
    def _(pe):
        def rows(to, pairs):
            for n, (lhsT, rhs) in enumerate(pairs):
                ins = pe.matmul(to, lhsT, rhs, start=(n == 0), stop=(n == len(pairs) - 1))
            return ins

        def means(b):
            pe.wait_ge(c_loaded, b * 16 + 16)
            for h in range(HALF):
                rows(bank[:, h, :], [(mean_w[:], tile_half(c, t, h)) for t in range(ET)]).then_inc(mean_filled, 1)

        def variances(b):
            for h in range(HALF):
                for t in range(ET):
                    if t == 0:
                        pe.wait_ge(centred, b * HALF * ET + h * ET + ET)
                    pe.wait_ge(squared, b * HALF * ET + h * ET + t + 1)
                    ins = pe.matmul(bank[:, h, :], mean_w[:], tile_half(sq, t, h), start=(t == 0), stop=(t == ET - 1))
                ins.then_inc(var_filled, 1)

        def keys_queries(b, g):
            gi, col = b * G + g, slice(g * P, (g + 1) * P)
            for h in range(HALF):
                if g >= 1 and h == 1:
                    pe.wait_ge(max_taken, gi)
                rows(bank[:, h, :], [(W["Wk2"][:, t, col], tile_half(c, t, h)) for t in range(ET)]).then_inc(kq_filled, 1)
            pe.wait_ge(kq_low, gi * 3 + 1)
            rows(bank[:, 0, :], [(W["Wq2"][:, t, col], xq[:, t, :]) for t in range(ET)]).then_inc(kq_filled, 1)

        def scores(b, g, i):
            gi = b * G + g
            if i == 0:
                pe.wait_ge(placed, gi * N_PLACED + N_PLACED)
                pe.wait_ge(max_row_clear, gi + 1)
                if g < 2:
                    pe.wait_ge(mask_placed, b * 2 * N_MASK + (g + 1) * N_MASK)
            if i < 2:
                pe.wait_ge(kq_low, gi * 3 + 2 + i)
            else:
                pe.wait_ge(scores_read, gi * NS + i - 1)
            n, h = i // HALF, i % HALF
            j, qt = n // ET, n % ET
            pe.matmul(bank[:, (i + 1) % 2, :], qa[:, g % 2, j, qt * P:(qt + 1) * P],
                      ka[:, g % 2, j, h * L:(h + 1) * L], start=True, stop=True).then_inc(scores_filled, 1)

        def turn_maxima(b, g):
            pe.wait_ge(max_ready, b * G + g + 1)
            pe.transpose(bank[0:GH * ET, 1, 0:P], mxx[:], ident[:]).then_inc(max_turned, 1)

        def value_rows(b, i):
            if i >= 4:
                pe.wait_ge(values_read, b * KT + i - 3)
            rows(bank[:, EXP + i % 4, :], [(c[:, t, i * P:(i + 1) * P], W["Wv2"][:, t, :])
                                           for t in range(ET)]).then_inc(values_filled, 1)

        def values_and_scores(b):
            for i in range(KT // 2, KT):
                value_rows(b, i)
                n = NS // (KT // 2)
                for s in range(n * (i - KT // 2), n * (i - KT // 2 + 1)):
                    scores(b, 0, s)
            turn_maxima(b, 0)

        def scores_again(b, g, kt):
            for u in range(2):
                n = 2 * (g * KT + kt) + u
                if n >= 2:
                    pe.wait_ge(exp_done, b * N_EXP + n - 1)
                for j in (2 * u, 2 * u + 1):
                    ins = pe.matmul(bank[:, EXP + 2 * (n % 2) + j % 2, :], ka[:, g % 2, j, kt * P:(kt + 1) * P],
                                    qa[:, g % 2, j, :], start=True, stop=True)
                ins.then_inc(scored, 1)

        def attend(b, step):
            g, kt = step // KT, step % KT
            pe.wait_ge(exp_done, b * N_EXP + 2 * step + 2)
            if kt == 0 and g >= 1:
                pe.wait_ge(o_read, b * G + g)
            for j in range(GH):
                pe.matmul(bank[D1 * j:D1 * (j + 1), OUT, :], vals[:, kt, g * P + D1 * j:g * P + D1 * (j + 1)],
                          pt[:, step % NPT, j, :], start=(kt == 0), stop=(kt == KT - 1))
            for j in range(GH):
                ins = pe.matmul(bank[D1 * j:D1 * (j + 1), SUM, :], one[:, g * D1:(g + 1) * D1],
                                pt[:, step % NPT, j, :], start=(step == 0), stop=(step == N_STEP - 1))
            ins.then_inc(pv_done, 1)

        def batch(b, prepare):
            pe.wait_ge(values_read, b * KT + KT)
            for g in range(G):
                if g + 1 < G:
                    keys_queries(b, g + 1)
                pe.wait_ge(max_placed, (b * G + g) * 16 + 16)
                for kt in range(KT):
                    scores_again(b, g, kt)
                    if g + 1 < G and kt >= 2:
                        for i in range(NS * (kt - 2) // (KT - 2), NS * (kt - 1) // (KT - 2)):
                            scores(b, g + 1, i)
                    if g * KT + kt >= 1:
                        attend(b, g * KT + kt - 1)
                    if g == G - 1 and prepare and kt == 2:
                        variances(b + 1)
                if g + 1 < G:
                    turn_maxima(b, g + 1)
                if g == G - 2 and prepare:
                    pe.wait_ge(max_taken, b * G + G)
                    means(b + 1)
            attend(b, N_STEP - 1)
            if prepare:
                pe.wait_ge(normed, (b + 1) * HALF * ET + HALF * ET)
                pe.wait_ge(xq_loaded, (b + 1) * 16 + 16)
                keys_queries(b + 1, 0)
                for i in range(KT // 2):
                    value_rows(b + 1, i)
            pe.wait_ge(sum_inverted, b + 1)
            for g in range(G):
                if prepare:
                    pe.wait_ge(values_read, (b + 1) * KT + g + 1)
                rows(bank[:, EXP + g, :], [(spread_w[:, g * P:(g + 1) * P], ssum[:])]).then_inc(sum_spread, 1)
            pe.wait_ge(o_normed, b * G + G)
            for m in range(ET):
                rows(bank[:, EXP + m, :], [(W["Wo2"][:, t, m * P:(m + 1) * P], o[:, t, :])
                                           for t in range(ET)]).then_inc(out_filled, 1)
            pe.wait_ge(out_done, b * ET + ET)
            if prepare:
                values_and_scores(b + 1)

        pe.wait_ge(consts_loaded, N_CONST)
        means(0)
        variances(0)
        pe.wait_ge(normed, HALF * ET)
        pe.wait_ge(xq_loaded, 16)
        keys_queries(0, 0)
        for i in range(KT // 2):
            value_rows(0, i)
        values_and_scores(0)
        with pe.Fori(0, B - 1) as b:
            batch(b, True)
        batch(B - 1, False)


def build(nc, a, out_dram):
    x2_dram = nc.dram_tensor("x2_dram", [B, P, ET, L], F32, kind="Internal").ap()
    with ExitStack() as ctx:
        time_mix(nc, ctx, a, x2_dram)
    with ExitStack() as ctx:
        cross_attention(nc, ctx, a, x2_dram, out_dram)


def kernel(**inputs):
    import concourse.bacc as bacc
    from concourse.bass_utils import run_bass_kernel_spmd

    i = {k: np.asarray(v) for k, v in inputs.items()}
    t0, t1 = "L0_xattn_", "L1_xattn_"
    x, c = i["x"], i["ctx_2048"]

    def tiled(z):
        return z.reshape(z.shape[0], z.shape[1], ET, P).transpose(0, 3, 2, 1)

    w_v, w_g, w_o = i[t0 + "Wv"].T[:, VALUE_ORDER], i[t0 + "Wg"].T[:, VALUE_ORDER], i[t0 + "Wo"].T[VALUE_ORDER]
    rows = [i[t0 + n] for n in ("ln1_w", "ln1_b", "ln2_w", "ln2_b", "maa_x")]
    rows += list(i[t0 + "maa_stack"])
    rows += [i[t0 + "time_decay"], i[t0 + "faaaa"].reshape(E)]
    rows += [i[t0 + "gn_w"][VALUE_ORDER], i[t0 + "gn_b"][VALUE_ORDER]]
    rows += [i[t0 + n] for n in ("ffn_maa_k", "ffn_maa_r")]
    rows += [i[t1 + "ln_gamma"], i[t1 + "ln_beta"]]
    vecs = np.stack(rows).reshape(len(rows), ET, P).transpose(2, 0, 1).reshape(P, len(rows) * ET)
    vecs = np.concatenate([vecs, np.full((P, 1), EPS, np.float32), np.broadcast_to(i[t1 + "gate"], (P, 1))], 1)
    arrays = {
        "xT": tiled(x), "ctxT": tiled(c), "prev": tiled(c[:, 0:2]),
        "s0": c[:, 2:2 + D0].reshape(B, ET, P, D0).transpose(0, 2, 1, 3),
        "mask": i["mask_BxS2_bf1"].view(np.uint8), "vecs": vecs, "consts": shape_constants(),
        "maa_w1": i[t0 + "maa_w1"], "maa_w2": i[t0 + "maa_w2"].reshape(5 * MIX, E),
        "decay_w1": i[t0 + "decay_w1"], "decay_w2": i[t0 + "decay_w2"],
        "Wr": i[t0 + "Wr"].T, "Wk": i[t0 + "Wk"].T, "Wg": w_g, "Wv": w_v, "Wo": w_o,
        "fWk": i[t0 + "ffn_Wk"].T, "fWr": i[t0 + "ffn_Wr"].T, "fWv": i[t0 + "ffn_Wv"].T,
        "Wq2": i[t1 + "Wq"].T, "Wk2": i[t1 + "Wk"].T, "Wv2": i[t1 + "Wv"].T, "Wo2": i[t1 + "Wo"].T,
    }
    arrays = {f"in_{k}": np.ascontiguousarray(z) for k, z in arrays.items()}
    nc = bacc.Bacc("TRN2", target_bir_lowering=False, num_devices=1)
    a = {k[3:]: nc.dram_tensor(k, z.shape, mybir.dt.from_np(z.dtype), kind="ExternalInput").ap()
         for k, z in arrays.items()}
    out = nc.dram_tensor("out", (B, P, ET, L), F32, kind="ExternalOutput").ap()
    build(nc, a, out)
    got = run_bass_kernel_spmd(nc, [arrays], core_ids=[0]).results[0]["out"]
    return np.ascontiguousarray(got.transpose(0, 3, 2, 1)).reshape(B, L, E)
```

```python
from contextlib import ExitStack

import numpy as np

import concourse.bass as bass
from concourse import mybir

F32 = mybir.dt.float32
F32R = mybir.dt.float32r
U8 = mybir.dt.uint8
ALU = mybir.AluOpType
ACT = mybir.ActivationFunctionType
AX = mybir.AxisListType

P = 128
B = 4
L = 512
E = 512
ET = E // P
S2 = 1024
H0, D0 = 32, 16
HT = P // D0
H1, D1 = 16, 32
G = H1 * D1 // P
GH = P // D1
KT = S2 // P
MIX, DEC = 32, 64
EPS = 1e-5
SCALE = D1 ** -0.5
MASKED = -1e30

VECS = ["ln1_w", "ln1_b", "ln2_w", "ln2_b", "maa_x", "maa0", "maa1", "maa2", "maa3", "maa4", "time_decay",
        "faaaa", "gn_w", "gn_b", "ffn_maa_k", "ffn_maa_r", "ln_gamma", "ln_beta"]
V_EPS = len(VECS) * ET
V_GATE = V_EPS + 1
NV = V_GATE + 1

QUAD = 32
ND = D0 // 4


def value_row(h, d):
    return QUAD * (d % 4) + HT * (d // 4) + h


ORDER = np.zeros(P, int)
for _h in range(HT):
    for _d in range(D0):
        ORDER[value_row(_h, _d)] = _h * D0 + _d
VALUE_ORDER = np.concatenate([m * P + ORDER for m in range(ET)])

C_MEAN = 0
C_HEAD = C_MEAN + P
C_BONUS = C_HEAD + P
C_HSUM = C_BONUS + P
C_ROW = C_HSUM + ET * H0
C_HBC = C_ROW + ND * QUAD
C_PICK = C_HBC + ET * P
C_IDENT = C_PICK + D0 * P
C_ONE = C_IDENT + P
C_ABC = C_ONE + G * D1
NC_ = C_ABC + G * P


def shape_constants():
    c = np.zeros((P, NC_), np.float32)
    c[:, C_IDENT:C_IDENT + P] = np.eye(P)
    c[:, C_MEAN:C_MEAN + P] = 1.0 / E
    key_head = np.arange(P) // D0
    value_head, value_chan = ORDER // D0, ORDER % D0
    c[:, C_HEAD:C_HEAD + P] = (value_head[:, None] == value_head[None, :]) / D0
    c[:, C_BONUS:C_BONUS + P] = key_head[:, None] == value_head[None, :]
    for m in range(ET):
        for h in range(HT):
            c[value_head == h, C_HSUM + m * H0 + m * HT + h] = 1.0 / D0
            c[m * HT + h, C_HBC + m * P:C_HBC + (m + 1) * P] = value_head == h
    for n in range(ND):
        for h in range(HT):
            c[key_head == h, C_ROW + n * QUAD + n * HT + h] = 1.0
    for d in range(D0):
        c[:, C_PICK + d * P:C_PICK + (d + 1) * P] = ((value_head[:, None] == key_head[None, :])
                                                     & (value_chan[:, None] == d))
    c[:, C_ONE + G:C_ONE + D1] = 1.0
    for g in range(G):
        c[:, C_ONE + g * D1 + g] = 1.0
        for j in range(GH):
            c[D1 * j + g, C_ABC + g * P + D1 * j:C_ABC + g * P + D1 * (j + 1)] = 1.0
    return c


class Count:

    def __init__(self, *stages):
        self.per, self.first = 0, {}
        for name, n in stages:
            self.first[name] = self.per
            self.per += n

    def __call__(self, b, name, i=0):
        return b * self.per + self.first[name] + i + 1


MIXES = [("decay", 1), ("receptance", 3), ("key", 0), ("gate", 4), ("value", 2)]

PAIR = 2
NPAIR = D0 // PAIR
NU = ET * NPAIR


def time_mix(nc, ctx, a, x2_dram):
    def sb(name, shape, dt=F32):
        return ctx.enter_context(nc.sbuf_tensor(name, shape, dt))

    def sem(name):
        return ctx.enter_context(nc.semaphore(name))

    vec = sb("vec", [P, NV])
    con = sb("con", [P, C_PICK])
    pick = sb("pick", [P, D0 * P], F32R)
    w_maa1 = sb("w_maa1", [P, ET, 5 * MIX])
    w_maa2 = sb("w_maa2", [P, 5, E], F32R)
    w_dec1 = sb("w_dec1", [P, ET, DEC])
    w_dec2 = sb("w_dec2", [DEC, E])
    WEIGHTS = [("receptance", "Wr"), ("key", "Wk"), ("gate", "Wg"), ("value", "Wv"), ("wo", "Wo"),
               ("ffn_k", "fWk"), ("ffn_r", "fWr"), ("ffn_v", "fWv")]
    W = {n: sb(f"w_{n}", [P, ET, E]) for n, _ in WEIGHTS}

    xin = sb("xin", [P, ET, L])
    x = sb("x", [P, ET, L])
    xc = sb("xc", [P, ET, L])
    sq = sb("sq", [P, ET, L])
    xn = sb("xn", [P, ET, L + 1])
    sx = sb("sx", [P, ET, L])
    xa = sb("xa", [P, ET * L])
    xb = sb("xb", [P, 2 * PAIR * (L + 1)])
    r_sb = sb("r_sb", [P, ET, L])
    k_sb = sb("k_sb", [P, ET, L])
    w_sb = sb("w_sb", [P, ET, L])
    g_sb = sb("g_sb", [P, ET, L])
    v_hi = sb("v_hi", [P, ET, L], F32R)
    v_lo = sb("v_lo", [P, ET, L], F32R)
    rstd = sb("rstd", [P, L])
    s0 = sb("s0", [P, ET, D0])
    prev = sb("prev", [P, ET, 2])

    mixed = [xa[:].rearrange("p (t l) -> p t l", t=ET), xb[:, 0:ET * L].rearrange("p (t l) -> p t l", t=ET)]
    kv = sq[:].rearrange("p (u i) l -> p u i l", u=2)
    rs = xa[:].rearrange("p (u i l) -> p u i l", u=2, i=PAIR)
    st = xb[:].rearrange("p (u i l) -> p u i l", u=2, i=PAIR)
    hid, hide = rstd, g_sb[0:MIX, 0, :]
    hid_hi, hid_lo = v_lo[:, 1, :], v_lo[:, 2, :]
    hid_stack = [v_hi[:, i, :] for i in range(4)] + [v_lo[:, 0, :]]
    dec = rstd[0:DEC, :]

    bank = ctx.enter_context(nc.psum_tensor("bank", [P, 8, L], F32))

    consts_loaded = sem("consts_loaded")
    vec_loaded = sem("vec_loaded")
    pick_loaded = sem("pick_loaded")
    pick_ready = sem("pick_ready")
    maa2_loaded = sem("maa2_loaded")
    maa2_rounded = sem("maa2_rounded")
    maa2_ready = sem("maa2_ready")
    x_loaded = sem("x_loaded")
    state_loaded = sem("state_loaded")
    bank_filled = sem("bank_filled")
    act_read = sem("act_read")
    dve_read = sem("dve_read")
    squared = sem("squared")
    inverted = sem("inverted")
    scaled = sem("scaled")
    first_ready = sem("first_ready")
    xn_ready = sem("xn_ready")
    shifted = sem("shifted")
    lora_in = sem("lora_in")
    hid_rounded = sem("hid_rounded")
    hid_split = sem("hid_split")
    hide_stacked = sem("hide_stacked")
    hid_stacked = sem("hid_stacked")
    mixed_ready = sem("mixed_ready")
    mix_filled = sem("mix_filled")
    mix_read = sem("mix_read")
    decayed = sem("decayed")
    bonus_in = sem("bonus_in")
    spread = sem("spread")
    kv_ready = sem("kv_ready")
    st_first = sem("st_first")
    st_ready = sem("st_ready")
    rs_ready = sem("rs_ready")
    rs_used = sem("rs_used")
    att_ready = sem("att_ready")
    head_affine = sem("head_affine")
    gated = sem("gated")
    kk_ready = sem("kk_ready")
    x2_ready = sem("x2_ready")
    x2_stored = sem("x2_stored")

    N_CONST = 16 * (4 + len(WEIGHTS))
    N_MIXED = 7

    fills = Count(("mean1", 1), ("var1", 1), ("hidden", 2), ("decay_in", 1), ("receptance", ET), ("decay", ET),
                  ("key", ET), ("gate", ET), ("value", ET), ("bonus", ET), ("head_mean", ET), ("head_var", 1),
                  ("head_rstd", ET), ("wo", ET), ("mean2", 1), ("var2", 1), ("ffn_k", ET), ("ffn_r", ET),
                  ("ffn_v", ET))
    act_reads = Count(("var1", 1), ("hidden", 2), ("decay_in", 1), ("receptance", ET), ("decay", ET), ("key", ET),
                      ("gate", ET), ("value", ET), ("head_var", 1), ("var2", 1), ("ffn_k", ET), ("ffn_r", ET))
    dve_reads = Count(("mean1", ET), ("gate", ET), ("value", ET), ("bonus", ET), ("head_mean", ET),
                      ("head_rstd", ET), ("wo", ET), ("mean2", ET), ("ffn_v", ET))
    squares = Count(("norm1", ET), ("head", ET), ("norm2", ET))
    inversions = Count(("norm1", 1), ("head", 1), ("norm2", 1))
    norms = Count(("norm1", ET), ("norm2", ET))
    MEAN, VAR, HIDDEN, DECAY_IN, HEAD_VAR = 0, 1, 2, 0, 4
    MIX_BANK, OUT_BANK = 4, 6

    block = ctx.enter_context(nc.Block())

    def v(name, t):
        c = VECS.index(name) * ET + t
        return vec[:, c:c + 1]

    def over_pair(ap):
        return ap.unsqueeze(1).to_broadcast([P, PAIR, L])

    @block.sync
    def _(sp):
        sp.dma_start(vec[:], a["vecs"]).then_inc(vec_loaded, 16)
        sp.dma_start(con[:], a["consts"][:, 0:C_PICK]).then_inc(consts_loaded, 16)

        def load_x(b):
            sp.dma_start(xin[:], a["xT"][bass.ds(b, 1)].rearrange("o p t l -> (o p) t l")).then_inc(x_loaded, 16)

        def load_state(b):
            for to, name in ((s0, "s0"), (prev, "prev")):
                sp.dma_start(to[:], a[name][bass.ds(b, 1)].rearrange("o p t d -> (o p) t d")).then_inc(state_loaded, 16)

        load_x(0)
        load_state(0)
        for q in range(4):
            src = a["maa_w2"].rearrange("(i r) n -> r i n", r=MIX)
            rows = slice(MIX * q, MIX * (q + 1))
            sp.dma_start(r_sb[rows, :, :], src[:, 0:4, :]).then_inc(maa2_loaded, 16)
            sp.dma_start(k_sb[rows, 0, :], src[:, 4, :]).then_inc(maa2_loaded, 16)
        sp.dma_start(w_maa1[:], a["maa_w1"].rearrange("(t p) n -> p t n", p=P)).then_inc(consts_loaded, 16)
        sp.dma_start(w_dec1[:], a["decay_w1"].rearrange("(t p) n -> p t n", p=P)).then_inc(consts_loaded, 16)
        sp.dma_start(w_dec2[:], a["decay_w2"]).then_inc(consts_loaded, 16)
        for name, src in WEIGHTS:
            sp.dma_start(W[name][:], a[src].rearrange("(t p) n -> p t n", p=P)).then_inc(consts_loaded, 16)

        def stack_hidden(b):
            sp.wait_ge(hid_split, b + 1)
            for i in range(4):
                rows = slice(MIX * i, MIX * (i + 1))
                for q in range(4):
                    sp.dma_start(hid_stack[i][MIX * q:MIX * (q + 1), :].bitcast(F32),
                                 (hid_hi, hid_lo)[q % 2][rows, :].bitcast(F32)).then_inc(hid_stacked, 16)

        def store(b):
            sp.wait_ge(x2_ready, b * ET + ET)
            sp.dma_start(x2_dram[bass.ds(b, 1)].rearrange("o p t l -> (o p) t l"), x[:]).then_inc(x2_stored, 16)

        with sp.Fori(0, B - 1) as b:
            stack_hidden(b)
            sp.wait_ge(dve_read, dve_reads(b, "wo", ET - 1))
            load_x(b + 1)
            store(b)
            sp.wait_ge(x2_stored, b * 16 + 16)
            load_state(b + 1)
        stack_hidden(B - 1)
        store(B - 1)
        sp.wait_ge(x2_stored, 16 * B)

    @block.gpsimd
    def _(pool):
        with pool.Fori(0, B) as b:
            for u in range(NU):
                m = u // NPAIR
                pool.wait_ge(st_first, b * NU + u + 1)
                pool.wait_ge(st_ready, b * NU + u + 1)
                if u < 2:
                    pool.wait_ge(bank_filled, fills(b, "value", ET - 1))
                else:
                    pool.wait_ge(rs_used, b * NU + u - 1)
                pool.tensor_tensor(rs[:, u % 2], st[:, u % 2, :, 0:L], over_pair(r_sb[:, m, :]),
                                   ALU.mult).then_inc(rs_ready, 1)

    @block.scalar
    def _(act):
        act.dma_start(xa[:], a["consts"][:, C_PICK:C_IDENT]).then_inc(pick_loaded, 16)
        act.wait_ge(pick_loaded, 16)
        act.activation(pick[:], xa[:], ACT.Copy).then_inc(pick_ready, 1)
        act.wait_ge(maa2_loaded, 16 * 8)
        act.activation(w_maa2[:, 0:4, :], r_sb[:], ACT.Copy).then_inc(maa2_rounded, 1)
        act.activation(w_maa2[:, 4, :], k_sb[:, 0, :], ACT.Copy).then_inc(maa2_rounded, 1)
        act.wait_ge(vec_loaded, 16)

        def norm(b, q, row):
            for t in range(ET):
                act.wait_ge(dve_read, dve_reads(b, f"mean{q}", t))
                act.activation(sq[:, t, :], xc[:, t, :], ACT.Square).then_inc(squared, 1)
            if q == 1:
                act.wait_ge(state_loaded, b * 32 + 32)
            act.activation(xn[:, :, 0:1], prev[:, :, row:row + 1], ACT.Copy).then_inc(first_ready, 1)
            act.wait_ge(bank_filled, fills(b, f"var{q}"))
            act.activation(rstd[:], bank[:, VAR, :], ACT.Sqrt, bias=vec[:, V_EPS:V_EPS + 1]).then_inc(act_read, 1)
            for t in range(ET):
                act.wait_ge(scaled, norms(b, f"norm{q}", t))
                act.activation(xn[:, t, 1:L + 1], xc[:, t, :], ACT.Identity, scale=v(f"ln{q}_w", t),
                               bias=v(f"ln{q}_b", t)).then_inc(xn_ready, 1)

        with act.Fori(0, B) as b:
            norm(b, 1, 1)
            act.wait_ge(bank_filled, fills(b, "hidden", 0))
            act.activation(hid[:], bank[:, HIDDEN, :], ACT.Tanh).then_inc(act_read, 1)
            act.wait_ge(act_read, act_reads(b, "hidden", 0))
            act.activation(hid_hi, hid[:], ACT.Copy).then_inc(hid_rounded, 1)
            act.wait_ge(bank_filled, fills(b, "hidden", 1))
            act.activation(hide, bank[0:MIX, HIDDEN + 1, :], ACT.Tanh).then_inc(act_read, 1)
            act.wait_ge(act_read, act_reads(b, "hidden", 1))
            act.activation(hid_stack[4][0:MIX, :], hide, ACT.Copy).then_inc(hid_rounded, 1)
            act.activation(hid_stack[4][2 * MIX:3 * MIX, :], hide, ACT.Copy).then_inc(hid_rounded, 1)
            act.wait_ge(bank_filled, fills(b, "decay_in"))
            act.activation(dec, bank[0:DEC, DECAY_IN, :], ACT.Tanh).then_inc(act_read, 1)
            for m in range(ET):
                act.wait_ge(bank_filled, fills(b, "receptance", m))
                act.activation(r_sb[:, m, :], bank[:, m, :], ACT.Copy).then_inc(act_read, 1)
            for m in range(ET):
                act.wait_ge(bank_filled, fills(b, "decay", m))
                act.activation(w_sb[:, m, :], bank[:, m, :], ACT.Exp, bias=v("time_decay", m)).then_inc(act_read, 1)
            for m in range(ET):
                act.wait_ge(act_read, act_reads(b, "decay", m))
                act.activation(w_sb[:, m, :], w_sb[:, m, :], ACT.Exp, scale=-1.0).then_inc(decayed, 1)
            for m in range(ET):
                act.wait_ge(bank_filled, fills(b, "key", m))
                act.activation(k_sb[:, m, :], bank[:, m, :], ACT.Copy).then_inc(act_read, 1)
            for m in range(ET):
                act.wait_ge(bank_filled, fills(b, "gate", m))
                act.activation(g_sb[:, m, :], bank[:, m, :], ACT.Tanh, scale=0.5).then_inc(act_read, 1)
            for m in range(ET):
                act.wait_ge(bank_filled, fills(b, "value", m))
                act.activation(xc[:, m, :], bank[:, m, :], ACT.Copy)
                act.activation(v_hi[:, m, :], bank[:, m, :], ACT.Copy).then_inc(act_read, 1)
            for u in range(NU):
                m, c = u // NPAIR, (u % NPAIR) * PAIR
                if u >= 2:
                    act.wait_ge(rs_ready, b * NU + u - 1)
                act.activation(st[:, u % 2, :, 0:1], s0[:, m, c:c + PAIR].unsqueeze(2), ACT.Copy).then_inc(st_first, 1)
            for m in range(ET):
                act.wait_ge(dve_read, dve_reads(b, "head_mean", m))
                act.activation(sq[:, m, :], xc[:, m, :], ACT.Square).then_inc(squared, 1)
            act.wait_ge(bank_filled, fills(b, "head_var"))
            act.activation(rstd[0:H0, :], bank[0:H0, HEAD_VAR, :], ACT.Sqrt,
                           bias=vec[0:H0, V_EPS:V_EPS + 1]).then_inc(act_read, 1)
            for m in range(ET):
                act.wait_ge(dve_read, dve_reads(b, "head_rstd", m))
                act.activation(xc[:, m, :], xc[:, m, :], ACT.Identity, scale=v("gn_w", m),
                               bias=v("gn_b", m)).then_inc(head_affine, 1)
            norm(b, 2, 0)
            for m in range(ET):
                act.wait_ge(bank_filled, fills(b, "ffn_k", m))
                act.activation(k_sb[:, m, :], bank[:, m, :], ACT.Relu).then_inc(act_read, 1)
            for m in range(ET):
                act.wait_ge(act_read, act_reads(b, "ffn_k", m))
                act.activation(k_sb[:, m, :], k_sb[:, m, :], ACT.Square).then_inc(kk_ready, 1)
            for m in range(ET):
                act.wait_ge(bank_filled, fills(b, "ffn_r", m))
                act.activation(r_sb[:, m, :], bank[:, m, :], ACT.Tanh, scale=0.5).then_inc(act_read, 1)

    @block.vector
    def _(dve):
        dve.wait_ge(vec_loaded, 16)
        dve.wait_ge(maa2_rounded, 2)
        half = slice(2 * MIX, 4 * MIX)
        dve.tensor_tensor(w_maa2[half, 0:4, :], r_sb[half, :, :], w_maa2[half, 0:4, :].bitcast(F32),
                          ALU.subtract).then_inc(maa2_ready, 1)
        dve.tensor_tensor(w_maa2[half, 4, :], k_sb[half, 0, :], w_maa2[half, 4, :].bitcast(F32),
                          ALU.subtract).then_inc(maa2_ready, 1)

        def norm(b, q, src):
            dve.wait_ge(bank_filled, fills(b, f"mean{q}"))
            for t in range(ET):
                dve.tensor_tensor(xc[:, t, :], src[:, t, :], bank[:, MEAN, :], ALU.subtract).then_inc(dve_read, 1)
            dve.wait_ge(act_read, act_reads(b, f"var{q}"))
            dve.reciprocal(rstd[:], rstd[:]).then_inc(inverted, 1)
            dve.wait_ge(inverted, inversions(b, f"norm{q}"))
            for t in range(ET):
                dve.tensor_tensor(xc[:, t, :], xc[:, t, :], rstd[:], ALU.mult).then_inc(scaled, 1)
            dve.wait_ge(first_ready, b * 2 + q)
            for t in range(ET):
                dve.wait_ge(xn_ready, norms(b, f"norm{q}", t))
                dve.tensor_tensor(sx[:, t, :], xn[:, t, 0:L], xn[:, t, 1:L + 1], ALU.subtract).then_inc(shifted, 1)

        def kv_pair(b, u):
            m = u // NPAIR
            dve.wait_ge(spread, b * NU + u + 1)
            if u >= 2:
                dve.wait_ge(st_ready, b * NU + u - 1)
            c = PAIR * (u % 3)
            dve.tensor_tensor(kv[:, u % 2], bank[:, c:c + PAIR, :], over_pair(k_sb[:, m, :]),
                              ALU.mult).then_inc(kv_ready, 1)

        def attention_tile(b, m):
            dve.wait_ge(rs_used, b * NU + NPAIR * (m + 1))
            dve.tensor_tensor(xc[:, m, :], xc[:, m, :], bank[:, OUT_BANK + m % 2, :], ALU.add).then_inc(att_ready, 1)

        with dve.Fori(0, B) as b:
            norm(b, 1, xin)
            for t in range(ET):
                dve.wait_ge(shifted, norms(b, "norm1", t))
                dve.scalar_tensor_tensor(out=sq[:, t, :], in0=sx[:, t, :], scalar=v("maa_x", t),
                                         in1=xn[:, t, 1:L + 1], op0=ALU.mult, op1=ALU.add).then_inc(lora_in, 1)
            dve.wait_ge(hid_rounded, b * 3 + 1)
            dve.tensor_tensor(hid_lo, hid[:], hid_hi.bitcast(F32), ALU.subtract).then_inc(hid_split, 1)
            dve.wait_ge(hid_rounded, b * 3 + 3)
            for q in (1, 3):
                dve.tensor_tensor(hid_stack[4][MIX * q:MIX * (q + 1), :], hide, hid_stack[4][0:MIX, :].bitcast(F32),
                                  ALU.subtract).then_inc(hide_stacked, 1)
            last_use = [("decay_in", 0)] + [(name, ET - 1) for name, _ in MIXES[1:]]
            for s, (name, i) in enumerate(MIXES):
                to = mixed[s % 2]
                if s >= 2:
                    dve.wait_ge(bank_filled, fills(b, *last_use[s - 2]))
                for t in range(ET):
                    dve.wait_ge(mix_filled, b * 5 * ET + s * ET + t + 1)
                    dve.scalar_tensor_tensor(out=to[:, t, :], in0=bank[:, MIX_BANK + t, :], scalar=v(f"maa{i}", t),
                                             in1=sx[:, t, :], op0=ALU.add, op1=ALU.mult).then_inc(mix_read, 1)
                dve.wait_ge(mix_read, b * 5 * ET + s * ET + ET)
                dve.tensor_tensor(to, to, xn[:, :, 1:L + 1], ALU.add).then_inc(mixed_ready, 1)
            for m in range(ET):
                dve.wait_ge(act_read, act_reads(b, "key", m))
                dve.scalar_tensor_tensor(out=sq[:, m, :], in0=r_sb[:, m, :], scalar=v("faaaa", m),
                                         in1=k_sb[:, m, :], op0=ALU.mult, op1=ALU.mult).then_inc(bonus_in, 1)
            for m in range(ET):
                dve.wait_ge(act_read, act_reads(b, "gate", m))
                dve.scalar_tensor_tensor(out=g_sb[:, m, :], in0=g_sb[:, m, :], scalar=1.0, in1=bank[:, m, :],
                                         op0=ALU.add, op1=ALU.mult).then_inc(dve_read, 1)
            for m in range(ET):
                dve.wait_ge(act_read, act_reads(b, "value", m))
                dve.tensor_tensor(v_lo[:, m, :], bank[:, m, :], v_hi[:, m, :].bitcast(F32),
                                  ALU.subtract).then_inc(dve_read, 1)
            for m in range(ET):
                dve.wait_ge(bank_filled, fills(b, "bonus", m))
                dve.tensor_tensor(xc[:, m, :], bank[:, m, :], xc[:, m, :], ALU.mult).then_inc(dve_read, 1)
            dve.wait_ge(decayed, b * ET + ET)
            kv_pair(b, 0)
            for u in range(NU):
                m, c = u // NPAIR, (u % NPAIR) * PAIR
                if u + 1 < NU:
                    kv_pair(b, u + 1)
                dve.wait_ge(kv_ready, b * NU + u + 1)
                if u >= 2:
                    dve.wait_ge(rs_ready, b * NU + u - 1)
                for i in range(PAIR):
                    scan = dve.tensor_tensor_scan(st[:, u % 2, i, 1:L + 1], w_sb[:, m, :], kv[:, u % 2, i, :],
                                                  s0[:, m, c + i:c + i + 1], ALU.mult, ALU.add)
                scan.then_inc(st_ready, 1)
                if u % NPAIR == 4 and m >= 1:
                    attention_tile(b, m - 1)
            attention_tile(b, ET - 1)
            for m in range(ET):
                dve.wait_ge(bank_filled, fills(b, "head_mean", m))
                dve.tensor_tensor(xc[:, m, :], xc[:, m, :], bank[:, m, :], ALU.subtract).then_inc(dve_read, 1)
            dve.wait_ge(act_read, act_reads(b, "head_var"))
            dve.reciprocal(rstd[0:H0, :], rstd[0:H0, :]).then_inc(inverted, 1)
            for m in range(ET):
                dve.wait_ge(bank_filled, fills(b, "head_rstd", m))
                dve.tensor_tensor(xc[:, m, :], xc[:, m, :], bank[:, m, :], ALU.mult).then_inc(dve_read, 1)
            for m in range(ET):
                dve.wait_ge(head_affine, b * ET + m + 1)
                dve.scalar_tensor_tensor(out=xc[:, m, :], in0=xc[:, m, :], scalar=0.5, in1=g_sb[:, m, :],
                                         op0=ALU.mult, op1=ALU.mult).then_inc(gated, 1)
            for m in range(ET):
                dve.wait_ge(bank_filled, fills(b, "wo", m))
                dve.tensor_tensor(x[:, m, :], xin[:, m, :], bank[:, m, :], ALU.add).then_inc(dve_read, 1)
            norm(b, 2, x)
            dve.wait_ge(shifted, norms(b, "norm2", ET - 1))
            for s, name in enumerate(["ffn_maa_k", "ffn_maa_r"]):
                for t in range(ET):
                    ins = dve.scalar_tensor_tensor(out=mixed[s][:, t, :], in0=sx[:, t, :], scalar=v(name, t),
                                                   in1=xn[:, t, 1:L + 1], op0=ALU.mult, op1=ALU.add)
                ins.then_inc(mixed_ready, 1)
            for m in range(ET):
                dve.wait_ge(bank_filled, fills(b, "ffn_v", m))
                dve.scalar_tensor_tensor(out=w_sb[:, m, :], in0=r_sb[:, m, :], scalar=1.0, in1=bank[:, m, :],
                                         op0=ALU.add, op1=ALU.mult).then_inc(dve_read, 1)
            for m in range(ET):
                dve.wait_ge(dve_read, dve_reads(b, "ffn_v", m))
                dve.scalar_tensor_tensor(out=x[:, m, :], in0=w_sb[:, m, :], scalar=0.5, in1=x[:, m, :],
                                         op0=ALU.mult, op1=ALU.add).then_inc(x2_ready, 1)

    @block.tensor
    def _(pe):
        def rows(to, pairs):
            for n, (lhsT, rhs) in enumerate(pairs):
                ins = pe.matmul(to, lhsT, rhs, start=(n == 0), stop=(n == len(pairs) - 1))
            return ins

        def project(m, weight, src):
            return rows(bank[:, m, :], [(weight[:, t, m * P:(m + 1) * P], src[:, t, :]) for t in range(ET)])

        def norm(b, q, src):
            mean = con[:, C_MEAN:C_MEAN + P]
            rows(bank[:, MEAN, :], [(mean, src[:, t, :]) for t in range(ET)]).then_inc(bank_filled, 1)
            for t in range(ET):
                pe.wait_ge(squared, squares(b, f"norm{q}", t))
                ins = pe.matmul(bank[:, VAR, :], mean, sq[:, t, :], start=(t == 0), stop=(t == ET - 1))
            ins.then_inc(bank_filled, 1)

        def low_rank(b, s):
            i = MIXES[s][1]
            for t in range(ET):
                if s >= 1:
                    pe.wait_ge(mix_read, b * 5 * ET + (s - 1) * ET + t + 1)
                pe.matmul(bank[:, MIX_BANK + t, :], w_maa2[:, i, t * P:(t + 1) * P], hid_stack[i], start=True,
                          stop=True).then_inc(mix_filled, 1)

        def sum_pair(b, u):
            m, c = u // NPAIR, (u % NPAIR) * PAIR
            if u % NPAIR == 0 and m >= 2:
                pe.wait_ge(att_ready, b * ET + m - 1)
            pe.wait_ge(rs_ready, b * NU + u + 1)
            for i in range(PAIR):
                q, n = (c + i) % 4, (c + i) // 4
                ins = pe.matmul(bank[QUAD * q:QUAD * (q + 1), OUT_BANK + m % 2, :],
                                con[:, C_ROW + n * QUAD:C_ROW + (n + 1) * QUAD], rs[:, u % 2, i, :],
                                start=(n == 0), stop=(n == ND - 1))
            ins.then_inc(rs_used, 1)

        pe.wait_ge(consts_loaded, N_CONST)
        pe.wait_ge(pick_ready, 1)
        pe.wait_ge(maa2_ready, 2)
        with pe.Fori(0, B) as b:
            pe.wait_ge(x_loaded, b * 16 + 16)
            norm(b, 1, xin)
            for n, cols in enumerate((slice(0, P), slice(P, 5 * MIX))):
                for t in range(ET):
                    pe.wait_ge(lora_in, b * ET + t + 1)
                    ins = pe.matmul(bank[0:cols.stop - cols.start, HIDDEN + n, :], w_maa1[:, t, cols], sq[:, t, :],
                                    start=(t == 0), stop=(t == ET - 1))
                ins.then_inc(bank_filled, 1)
            pe.wait_ge(hid_stacked, b * 256 + 256)
            pe.wait_ge(hide_stacked, b * 2 + 2)
            low_rank(b, 0)
            low_rank(b, 1)
            pe.wait_ge(mixed_ready, b * N_MIXED + 1)
            rows(bank[0:DEC, DECAY_IN, :],
                 [(w_dec1[:, t, :], mixed[0][:, t, :]) for t in range(ET)]).then_inc(bank_filled, 1)
            low_rank(b, 2)
            pe.wait_ge(mixed_ready, b * N_MIXED + 2)
            pe.wait_ge(act_read, act_reads(b, "decay_in"))
            for m in range(ET):
                project(m, W["receptance"], mixed[1]).then_inc(bank_filled, 1)
            for m in range(ET):
                pe.wait_ge(act_read, act_reads(b, "receptance", m))
                rows(bank[:, m, :], [(w_dec2[:, m * P:(m + 1) * P], dec)]).then_inc(bank_filled, 1)
            low_rank(b, 3)
            pe.wait_ge(mixed_ready, b * N_MIXED + 3)
            for m in range(ET):
                pe.wait_ge(act_read, act_reads(b, "decay", m))
                project(m, W["key"], mixed[0]).then_inc(bank_filled, 1)
            low_rank(b, 4)
            pe.wait_ge(mixed_ready, b * N_MIXED + 4)
            for m in range(ET):
                pe.wait_ge(act_read, act_reads(b, "key", m))
                project(m, W["gate"], mixed[1]).then_inc(bank_filled, 1)
            pe.wait_ge(mixed_ready, b * N_MIXED + 5)
            for m in range(ET):
                pe.wait_ge(dve_read, dve_reads(b, "gate", m))
                project(m, W["value"], mixed[0]).then_inc(bank_filled, 1)
            for m in range(ET):
                pe.wait_ge(bonus_in, b * ET + m + 1)
                pe.wait_ge(dve_read, dve_reads(b, "value", m))
                rows(bank[:, m, :], [(con[:, C_BONUS:C_BONUS + P], sq[:, m, :])]).then_inc(bank_filled, 1)
            pe.wait_ge(dve_read, dve_reads(b, "bonus", ET - 1))
            for u in range(NU):
                m, c = u // NPAIR, (u % NPAIR) * PAIR
                if u >= 3:
                    pe.wait_ge(kv_ready, b * NU + u - 2)
                for i in range(PAIR):
                    to_d = pick[:, (c + i) * P:(c + i + 1) * P]
                    ins = rows(bank[:, PAIR * (u % 3) + i, :], [(to_d, v_hi[:, m, :]), (to_d, v_lo[:, m, :])])
                ins.then_inc(spread, 1)
                if u >= 3:
                    sum_pair(b, u - 3)
            for u in range(NU - 3, NU):
                sum_pair(b, u)
            pe.wait_ge(kv_ready, b * NU + NU)
            for m in range(ET):
                pe.wait_ge(att_ready, b * ET + m + 1)
                rows(bank[:, m, :], [(con[:, C_HEAD:C_HEAD + P], xc[:, m, :])]).then_inc(bank_filled, 1)
            for m in range(ET):
                pe.wait_ge(squared, squares(b, "head", m))
                ins = pe.matmul(bank[0:H0, HEAD_VAR, :], con[:, C_HSUM + m * H0:C_HSUM + (m + 1) * H0], sq[:, m, :],
                                start=(m == 0), stop=(m == ET - 1))
            ins.then_inc(bank_filled, 1)
            pe.wait_ge(inverted, inversions(b, "head"))
            for m in range(ET):
                rows(bank[:, m, :], [(con[:, C_HBC + m * P:C_HBC + (m + 1) * P], rstd[:])]).then_inc(bank_filled, 1)
            pe.wait_ge(gated, b * ET + ET)
            for m in range(ET):
                project(m, W["wo"], xc).then_inc(bank_filled, 1)
            pe.wait_ge(dve_read, dve_reads(b, "wo", ET - 1))
            norm(b, 2, x)
            pe.wait_ge(mixed_ready, b * N_MIXED + 6)
            for m in range(ET):
                project(m, W["ffn_k"], mixed[0]).then_inc(bank_filled, 1)
            pe.wait_ge(mixed_ready, b * N_MIXED + 7)
            for m in range(ET):
                pe.wait_ge(act_read, act_reads(b, "ffn_k", m))
                project(m, W["ffn_r"], mixed[1]).then_inc(bank_filled, 1)
            pe.wait_ge(kk_ready, b * ET + ET)
            for m in range(ET):
                pe.wait_ge(act_read, act_reads(b, "ffn_r", m))
                project(m, W["ffn_v"], k_sb).then_inc(bank_filled, 1)
            pe.wait_ge(dve_read, dve_reads(b, "ffn_v", ET - 1))


MASK_ROW, MAX_ROW = 3 * QUAD, 3 * QUAD + 1
HALF = S2 // L
NS = HALF * GH * ET
NPT = 3
N_STEP = G * KT
SCORE_KT = 2
FILL_KT = 3
SUM_KT = 2


def score_slots(kt):
    n = KT - SCORE_KT
    return range(NS * (kt - SCORE_KT) // n, NS * (kt - SCORE_KT + 1) // n) if kt >= SCORE_KT else range(0)


def fill_slots(g, kt):
    return [kt - FILL_KT] if g + 2 < G and FILL_KT <= kt < FILL_KT + 3 else []


FIRST_SCORES = [range(NS * i // (KT // 2), NS * (i + 1) // (KT // 2)) for i in range(KT // 2)]


def cross_attention(nc, ctx, a, x2_dram, out_dram):
    def sb(name, shape, dt=F32):
        return ctx.enter_context(nc.sbuf_tensor(name, shape, dt))

    def sem(name):
        return ctx.enter_context(nc.semaphore(name))

    vec = sb("vec2", [P, NV])
    ident = sb("ident", [P, P])
    mean_w = sb("mean_w", [P, P])
    one = sb("one", [P, G * D1])
    spread_w = sb("spread_w", [P, G * P])
    W = {n: sb(f"w2_{n}", [P, ET, E]) for n in ["Wk2", "Wq2", "Wv2", "Wo2"]}
    tg = sb("tg", [P, 1])

    c = sb("ctx_rows", [P, ET, S2])
    sq = sb("sq2", [P, ET, L])
    xq = sb("xq", [P, ET, L])
    xr = sb("xr", [P, ET, L])
    rstd = sb("rstd2", [P, HALF, L])
    mask8 = sb("mask8", [1, S2], U8)
    vals = sb("vals", [P, KT, E])
    part = sb("part", [P, 3, S2 + L], F32R)
    stack = sb("stack", [P, 2, HALF + 1, GH, L], F32R)
    ka, qa = stack[:, :, 0:HALF], stack[:, :, HALF]
    pt = sb("pt", [P, NPT, GH, L])
    acc = sb("acc", [P, GH, L])
    mx = sb("mx", [P, HALF, GH * ET])
    mxx = sb("mxx", [P, GH * ET])
    mt = sb("mt", [GH * ET, P], F32R)
    ssum = sb("ssum", [P, L])
    o = sb("o", [P, G, L])
    maskf = sq[0:1, 0:HALF, :].bitcast(F32R)

    bank = ctx.enter_context(nc.psum_tensor("bank2", [P, 8, L], F32))
    EXP, OUT, KQ = 2, 6, 7

    consts_loaded = sem("consts_loaded2")
    rows_zeroed = sem("rows_zeroed")
    rows_set = sem("rows_set")
    c_loaded = sem("c_loaded")
    xq_loaded = sem("xq_loaded")
    xr_loaded = sem("xr_loaded")
    mask_loaded = sem("mask_loaded")
    mask_made = sem("mask_made")
    mask_placed = sem("mask_placed")
    gate_ready = sem("gate_ready")
    mean_filled = sem("mean_filled")
    var_filled = sem("var_filled")
    kq_filled = sem("kq_filled")
    scores_filled = sem("scores_filled")
    max_turned = sem("max_turned")
    values_filled = sem("values_filled")
    sum_spread = sem("sum_spread")
    out_filled = sem("out_filled")
    centred = sem("centred2")
    squared = sem("squared2")
    sd_ready = sem("sd_ready")
    inverted = sem("inverted2")
    scaled = sem("scaled2")
    normed = sem("normed2")
    kq_high = sem("kq_high")
    kq_low = sem("kq_low")
    placed = sem("placed")
    scores_read = sem("scores_read")
    max_ready = sem("max_ready")
    max_taken = sem("max_taken")
    max_placed = sem("max_placed")
    values_read = sem("values_read")
    scored = sem("scored")
    exp_done = sem("exp_done")
    pv_done = sem("pv_done")
    o_read = sem("o_read")
    added = sem("added")
    summed = sem("summed")
    sum_kept = sem("sum_kept")
    sum_inverted = sem("sum_inverted")
    o_normed = sem("o_normed")
    out_done = sem("out_done")
    out_stored = sem("out_stored")

    N_CONST = 16 * 9
    N_PLACED = 16 * 3 * GH
    N_MASK = 16 * HALF
    N_EXP = 2 * N_STEP
    N_ADD = KT - 1

    block = ctx.enter_context(nc.Block())

    def v(name, t):
        i = VECS.index(name) * ET + t
        return vec[:, i:i + 1]

    def tile_half(x, t, h):
        return x[:, t, h * L:(h + 1) * L]


    @block.sync
    def _(sp):
        def load(b):
            sp.dma_start(c[:], a["ctxT"][bass.ds(b, 1)].rearrange("o p t l -> (o p) t l")).then_inc(c_loaded, 16)
            sp.dma_start(mask8[:], a["mask"][bass.ds(b, 1)]).then_inc(mask_loaded, 16)
            sp.dma_start(xq[:], x2_dram[bass.ds(b, 1)].rearrange("o p t l -> (o p) t l")).then_inc(xq_loaded, 16)

        def load_residual(b):
            sp.dma_start(xr[:], x2_dram[bass.ds(b, 1)].rearrange("o p t l -> (o p) t l")).then_inc(xr_loaded, 16)

        load(0)
        sp.dma_start(vec[:], a["vecs"]).then_inc(consts_loaded, 16)
        sp.dma_start(mean_w[:], a["consts"][:, C_MEAN:C_MEAN + P]).then_inc(consts_loaded, 16)
        for n in W:
            sp.dma_start(W[n][:], a[n].rearrange("(t p) n -> p t n", p=P)).then_inc(consts_loaded, 16)
        sp.dma_start(ident[:], a["consts"][:, C_IDENT:C_IDENT + P]).then_inc(consts_loaded, 16)
        sp.dma_start(one[:], a["consts"][:, C_ONE:C_ABC]).then_inc(consts_loaded, 16)
        sp.dma_start(spread_w[:], a["consts"][:, C_ABC:NC_]).then_inc(consts_loaded, 16)
        load_residual(0)

        def place_group(b, g):
            if g < 2:
                sp.wait_ge(kq_low, (b * G + g) * 3 + 3)
            if g >= 2:
                sp.wait_ge(scored, b * N_EXP + 2 * KT * (g - 1))
            for j in range(GH):
                rows = slice(QUAD * j, QUAD * (j + 1))
                for n in range(3):
                    sp.dma_start(stack[QUAD * n:QUAD * (n + 1), g % 2, :, j, :].bitcast(F32),
                                 part[rows, n, :].bitcast(F32).rearrange("p (h l) -> p h l", l=L)
                                 ).then_inc(placed, 16)
            if g < 2:
                sp.wait_ge(mask_made, b + 1)
                for h in range(HALF):
                    sp.dma_start(ka[MASK_ROW:MASK_ROW + 1, g, h].bitcast(F32),
                                 maskf[:, h, :].bitcast(F32).unsqueeze(1).to_broadcast([1, GH, L])
                                 ).then_inc(mask_placed, 16)

        def place_max(b, g):
            sp.wait_ge(max_taken, b * G + g + 1)
            sp.dma_start(qa[MAX_ROW:MAX_ROW + 1, g % 2, :, :].bitcast(F32).rearrange("o j (q l) -> o (j q) l", l=P),
                         mt[:].bitcast(F32)).then_inc(max_placed, 16)

        def batch(b, prepare):
            for g in range(G):
                place_max(b, g)
                if 1 <= g < G - 1:
                    place_group(b, g + 1)
                if g == 2 and prepare:
                    load(b + 1)
            if prepare:
                place_group(b + 1, 0)
            sp.wait_ge(out_done, b * ET + ET)
            sp.dma_start(out_dram[bass.ds(b, 1)].rearrange("o p t l -> (o p) t l"), xr[:]).then_inc(out_stored, 16)
            if prepare:
                sp.wait_ge(out_stored, b * 16 + 16)
                load_residual(b + 1)
                place_group(b + 1, 1)

        sp.wait_ge(rows_set, 2)
        place_group(0, 0)
        place_group(0, 1)
        with sp.Fori(0, B - 1) as b:
            batch(b, True)
        batch(B - 1, False)
        sp.wait_ge(out_stored, 16 * B)

    @block.gpsimd
    def _(pool):
        last = slice(MASK_ROW, P)
        pool.memset(stack[last].bitcast(F32), 0.0).then_inc(rows_zeroed, 1)
        pool.wait_ge(rows_zeroed, 1)
        pool.memset(ka[MASK_ROW:MAX_ROW + 1].bitcast(F32), -1.0).then_inc(rows_set, 1)
        pool.memset(qa[MASK_ROW:MAX_ROW + 1, :, :, :].bitcast(F32), 1.0).then_inc(rows_set, 1)
        with pool.Fori(0, B) as b:
            for g in range(G):
                for kt in range(1, KT):
                    step = g * KT + kt
                    if kt == 1 and g >= 1:
                        pool.wait_ge(summed, b * G + g)
                    if kt >= 2:
                        pool.wait_ge(added, (b * G + g) * N_ADD + kt - 1)
                    pool.wait_ge(exp_done, b * N_EXP + 2 * step + 2)
                    before = pt[:, (step - 1) % NPT, :, :] if kt == 1 else acc[:]
                    pool.tensor_tensor(acc[:], before, pt[:, step % NPT, :, :], ALU.add).then_inc(added, 1)

    @block.scalar
    def _(act):
        act.wait_ge(consts_loaded, N_CONST)
        act.activation(tg[:], vec[:, V_GATE:V_GATE + 1], ACT.Tanh).then_inc(gate_ready, 1)

        def squares(b, h):
            if h == 1:
                act.wait_ge(var_filled, b * HALF + 1)
            for t in range(ET):
                act.wait_ge(centred, b * HALF * ET + h * ET + t + 1)
                act.activation(sq[:, t, :], tile_half(c, t, h), ACT.Square).then_inc(squared, 1)

        def deviations(b):
            for h in range(HALF):
                act.wait_ge(var_filled, b * HALF + h + 1)
                act.activation(rstd[:, h, :], bank[:, h, :], ACT.Sqrt, bias=vec[:, V_EPS:V_EPS + 1]).then_inc(sd_ready, 1)

        def affine(b):
            for h in range(HALF):
                for t in range(ET):
                    act.wait_ge(scaled, b * HALF * ET + h * ET + t + 1)
                    act.activation(tile_half(c, t, h), tile_half(c, t, h), ACT.Identity, scale=v("ln_gamma", t),
                                   bias=v("ln_beta", t)).then_inc(normed, 1)

        def high_part(b, g, i, first=False):
            n = (b * G + g) * 3
            if i == 0 and not first:
                act.wait_ge(placed, (b * G + g) * N_PLACED)
            act.wait_ge(kq_filled, n + i + 1)
            to = part[:, 0:2, S2:S2 + L] if i == 2 else part[:, 0:3:2, i * L:(i + 1) * L]
            act.activation(to, bank[:, KQ, :].unsqueeze(1).to_broadcast([P, 2, L]), ACT.Copy).then_inc(kq_high, 1)

        def values(b, i):
            act.wait_ge(values_filled, b * KT + i + 1)
            act.activation(vals[:, i, :], bank[:, EXP + i % 4, :], ACT.Copy).then_inc(values_read, 1)

        def prepare_first(b, first=False):
            for i in range(KT // 2):
                if i < 3:
                    high_part(b, 0, i, first)
                values(b, i)
            for i in range(KT // 2):
                values(b, KT // 2 + i)
                if i < 3:
                    high_part(b, 1, i)

        def exponentials(b, step):
            for u in range(2):
                n = 2 * step + u
                act.wait_ge(scored, b * N_EXP + n + 1)
                if u == 0 and step >= NPT:
                    act.wait_ge(pv_done, b * N_STEP + step - NPT + 1)
                    g, kt = (step - NPT) // KT, (step - NPT) % KT
                    act.wait_ge(added, (b * G + g) * N_ADD + max(kt, 1))
                e = EXP + 2 * (n % 2)
                act.activation(pt[:, step % NPT, 2 * u:2 * u + 2, :], bank[:, e:e + 2, :], ACT.Exp,
                               scale=SCALE).then_inc(exp_done, 1)

        def group_out(b, g):
            act.wait_ge(pv_done, b * N_STEP + g * KT + KT)
            act.activation(o[:, g, :], bank[:, OUT, :], ACT.Copy).then_inc(o_read, 1)

        def batch(b, prepare):
            for g in range(G):
                for kt in range(KT):
                    exponentials(b, g * KT + kt)
                    if kt == 0 and g >= 1:
                        group_out(b, g - 1)
                    for i in fill_slots(g, kt):
                        high_part(b, g + 2, i)
                    if g == G - 1 and prepare:
                        if kt == 0:
                            squares(b + 1, 0)
                        if kt == 2:
                            squares(b + 1, 1)
                        if kt == 4:
                            deviations(b + 1)
            group_out(b, G - 1)
            if prepare:
                affine(b + 1)
                prepare_first(b + 1)

        squares(0, 0)
        squares(0, 1)
        deviations(0)
        affine(0)
        prepare_first(0, True)
        with act.Fori(0, B - 1) as b:
            batch(b, True)
        batch(B - 1, False)

    @block.vector
    def _(dve):
        def centre(b):
            for h in range(HALF):
                dve.wait_ge(mean_filled, b * HALF + h + 1)
                for t in range(ET):
                    dve.tensor_tensor(tile_half(c, t, h), tile_half(c, t, h), bank[:, h, :],
                                      ALU.subtract).then_inc(centred, 1)

        def scale(b):
            for h in range(HALF):
                dve.wait_ge(sd_ready, b * HALF + h + 1)
                dve.reciprocal(rstd[:, h, :], rstd[:, h, :]).then_inc(inverted, 1)
                dve.wait_ge(inverted, b * HALF + h + 1)
                for t in range(ET):
                    dve.tensor_tensor(tile_half(c, t, h), tile_half(c, t, h), rstd[:, h, :],
                                      ALU.mult).then_inc(scaled, 1)
            dve.wait_ge(mask_loaded, b * 16 + 16)
            dve.tensor_scalar(maskf, mask8[:].rearrange("o (h l) -> o h l", l=L), 1.0, -MASKED, ALU.subtract,
                              ALU.mult).then_inc(mask_made, 1)

        def low_part(b, g, i):
            dve.wait_ge(kq_high, (b * G + g) * 3 + i + 1)
            s = slice(i * L, (i + 1) * L)
            dve.tensor_tensor(part[:, 2 if i == 2 else 1, s], bank[:, KQ, :], part[:, 0, s].bitcast(F32),
                              ALU.subtract).then_inc(kq_low, 1)

        def maximum(b, g, i):
            dve.wait_ge(scores_filled, (b * G + g) * NS + i + 1)
            n = i // HALF
            dve.reduce_max(mx[:, i % HALF, n:n + 1], bank[:, (i + 1) % 2, :], AX.X).then_inc(scores_read, 1)

        def maxima(b, g):
            gi = b * G + g
            dve.wait_ge(scores_read, gi * NS + NS)
            dve.tensor_tensor(mxx[:], mx[:, 0, :], mx[:, 1, :], ALU.max).then_inc(max_ready, 1)
            dve.wait_ge(max_turned, gi + 1)
            if g + 1 < G:
                dve.wait_ge(kq_low, gi * 3 + 6)
            dve.tensor_copy(mt[:], bank[0:GH * ET, 1, 0:P]).then_inc(max_taken, 1)

        def keep_sum(b, g):
            dve.wait_ge(summed, b * G + g + 1)
            if g == 0:
                dve.tensor_copy(ssum[:], bank[:, KQ, :]).then_inc(sum_kept, 1)
            else:
                dve.wait_ge(sum_kept, b * G + g)
                dve.tensor_tensor(ssum[:], ssum[:], bank[:, KQ, :], ALU.add).then_inc(sum_kept, 1)

        def first_maxima(b):
            for n, slots in enumerate(FIRST_SCORES):
                for i in slots:
                    maximum(b, 0, i)
                if n < 3:
                    low_part(b, 1, n)
            maxima(b, 0)

        def batch(b, prepare):
            for g in range(G):
                if g == G - 1 and prepare:
                    dve.wait_ge(mask_placed, b * 2 * N_MASK + 2 * N_MASK)
                    centre(b + 1)
                for kt in range(KT):
                    if g + 1 < G:
                        for i in score_slots(kt):
                            maximum(b, g + 1, i)
                    for i in fill_slots(g, kt):
                        low_part(b, g + 2, i)
                    if kt == SUM_KT and g >= 1:
                        keep_sum(b, g - 1)
                if g + 1 < G:
                    maxima(b, g + 1)
            if prepare:
                scale(b + 1)
                for i in range(3):
                    low_part(b + 1, 0, i)
            keep_sum(b, G - 1)
            dve.wait_ge(sum_kept, b * G + G)
            dve.reciprocal(ssum[:], ssum[:]).then_inc(sum_inverted, 1)
            for g in range(G):
                dve.wait_ge(sum_spread, b * G + g + 1)
                dve.wait_ge(o_read, b * G + g + 1)
                dve.tensor_tensor(o[:, g, :], o[:, g, :], bank[:, EXP + g, :], ALU.mult).then_inc(o_normed, 1)
            dve.wait_ge(xr_loaded, b * 16 + 16)
            for m in range(ET):
                dve.wait_ge(out_filled, b * ET + m + 1)
                dve.scalar_tensor_tensor(out=xr[:, m, :], in0=bank[:, EXP + m, :], scalar=tg[:, 0:1],
                                         in1=xr[:, m, :], op0=ALU.mult, op1=ALU.add).then_inc(out_done, 1)
            if prepare:
                first_maxima(b + 1)

        centre(0)
        scale(0)
        for i in range(3):
            low_part(0, 0, i)
        dve.wait_ge(gate_ready, 1)
        first_maxima(0)
        with dve.Fori(0, B - 1) as b:
            batch(b, True)
        batch(B - 1, False)

    @block.tensor
    def _(pe):
        def rows(to, pairs):
            for n, (lhsT, rhs) in enumerate(pairs):
                ins = pe.matmul(to, lhsT, rhs, start=(n == 0), stop=(n == len(pairs) - 1))
            return ins

        def means(b):
            pe.wait_ge(c_loaded, b * 16 + 16)
            for h in range(HALF):
                rows(bank[:, h, :], [(mean_w[:], tile_half(c, t, h)) for t in range(ET)]).then_inc(mean_filled, 1)

        def variance(b, h):
            pe.wait_ge(centred, b * HALF * ET + h * ET + ET)
            for t in range(ET):
                pe.wait_ge(squared, b * HALF * ET + h * ET + t + 1)
                ins = pe.matmul(bank[:, h, :], mean_w[:], sq[:, t, :], start=(t == 0), stop=(t == ET - 1))
            ins.then_inc(var_filled, 1)

        def fill(b, g, i, t):
            if t == 0 and (i >= 1 or g == 1):
                pe.wait_ge(kq_low, (b * G + g) * 3 + i)
            weight, src = (W["Wq2"], xq) if i == 2 else (W["Wk2"], c)
            s = slice(0, L) if i == 2 else slice(i * L, (i + 1) * L)
            ins = pe.matmul(bank[:, KQ, :], weight[:, t, g * P:(g + 1) * P], src[:, t, s], start=(t == 0),
                            stop=(t == ET - 1))
            if t == ET - 1:
                ins.then_inc(kq_filled, 1)

        def scores(b, g, i):
            gi = b * G + g
            if i == 0:
                pe.wait_ge(placed, gi * N_PLACED + N_PLACED)
                if g < 2:
                    pe.wait_ge(mask_placed, b * 2 * N_MASK + (g + 1) * N_MASK)
                if g >= 1:
                    pe.wait_ge(max_taken, gi)
            if i >= 2:
                pe.wait_ge(scores_read, gi * NS + i - 1)
            n, h = i // HALF, i % HALF
            j, qt = n // ET, n % ET
            pe.matmul(bank[:, (i + 1) % 2, :], qa[0:MASK_ROW + 1, g % 2, j, qt * P:(qt + 1) * P],
                      ka[0:MASK_ROW + 1, g % 2, h, j, :], start=True, stop=True).then_inc(scores_filled, 1)

        def turn_maxima(b, g):
            pe.wait_ge(max_ready, b * G + g + 1)
            pe.transpose(bank[0:GH * ET, 1, 0:P], mxx[:], ident[:]).then_inc(max_turned, 1)

        def value_rows(b, i, t):
            if t == 0 and i >= 4:
                pe.wait_ge(values_read, b * KT + i - 3)
            ins = pe.matmul(bank[:, EXP + i % 4, :], c[:, t, i * P:(i + 1) * P], W["Wv2"][:, t, :], start=(t == 0),
                            stop=(t == ET - 1))
            if t == ET - 1:
                ins.then_inc(values_filled, 1)

        def first_half(b):
            pe.wait_ge(normed, b * HALF * ET + HALF * ET)
            pe.wait_ge(xq_loaded, b * 16 + 16)
            for i in range(KT // 2):
                for t in range(ET):
                    if i < 3:
                        fill(b, 0, i, t)
                for t in range(ET):
                    value_rows(b, i, t)

        def second_half(b):
            for n, slots in enumerate(FIRST_SCORES):
                for t in range(ET):
                    value_rows(b, KT // 2 + n, t)
                    scores(b, 0, slots[2 * t])
                    if n < 3:
                        fill(b, 1, n, t)
                    scores(b, 0, slots[2 * t + 1])
            turn_maxima(b, 0)

        def scores_again(b, g, kt):
            for u in range(2):
                n = 2 * (g * KT + kt) + u
                if n >= 2:
                    pe.wait_ge(exp_done, b * N_EXP + n - 1)
                for j in (2 * u, 2 * u + 1):
                    ins = pe.matmul(bank[:, EXP + 2 * (n % 2) + j % 2, :], ka[:, g % 2, kt * P // L, j, kt * P % L:kt * P % L + P],
                                    qa[:, g % 2, j, :], start=True, stop=True)
                ins.then_inc(scored, 1)

        def attend(b, step):
            g, kt = step // KT, step % KT
            pe.wait_ge(exp_done, b * N_EXP + 2 * step + 2)
            if kt == 0 and g >= 1:
                pe.wait_ge(o_read, b * G + g)
            for j in range(GH):
                ins = pe.matmul(bank[D1 * j:D1 * (j + 1), OUT, :], vals[:, kt, g * P + D1 * j:g * P + D1 * (j + 1)],
                                pt[:, step % NPT, j, :], start=(kt == 0), stop=(kt == KT - 1))
            ins.then_inc(pv_done, 1)

        def sum_group(b, g):
            pe.wait_ge(added, (b * G + g) * N_ADD + N_ADD)
            for j in range(GH):
                ins = pe.matmul(bank[D1 * j:D1 * (j + 1), KQ, :], one[:, g * D1:(g + 1) * D1], acc[:, j, :],
                                start=True, stop=True)
            ins.then_inc(summed, 1)

        def batch(b, prepare):
            pe.wait_ge(values_read, b * KT + KT)
            for g in range(G):
                pe.wait_ge(max_placed, (b * G + g) * 16 + 16)
                for kt in range(KT):
                    scores_again(b, g, kt)
                    slots = score_slots(kt) if g + 1 < G else []
                    for i in fill_slots(g, kt):
                        if i == 0 and g == 0:
                            pe.wait_ge(kq_low, b * G * 3 + 6)
                        elif i == 0:
                            pe.wait_ge(sum_kept, b * G + g)
                        for t in range(ET):
                            scores(b, g + 1, slots[t])
                            fill(b, g + 2, i, t)
                    done = ET if fill_slots(g, kt) else 2
                    if not fill_slots(g, kt):
                        for i in slots[:2]:
                            scores(b, g + 1, i)
                    if g * KT + kt >= 1:
                        attend(b, g * KT + kt - 1)
                    for i in slots[done:]:
                        scores(b, g + 1, i)
                    if kt == SUM_KT and g >= 1:
                        if g + 1 < G:
                            pe.wait_ge(kq_low, (b * G + g + 1) * 3 + 3)
                        else:
                            pe.wait_ge(sum_kept, b * G + g - 1)
                        sum_group(b, g - 1)
                    if g == G - 1 and prepare and kt in (1, 3):
                        variance(b + 1, kt // 2)
                if g + 1 < G:
                    turn_maxima(b, g + 1)
                if g == G - 2 and prepare:
                    pe.wait_ge(max_taken, b * G + G)
                    means(b + 1)
            attend(b, N_STEP - 1)
            pe.wait_ge(sum_kept, b * G + G - 1)
            if prepare:
                first_half(b + 1)
                pe.wait_ge(kq_low, (b + 1) * G * 3 + 3)
            sum_group(b, G - 1)
            pe.wait_ge(sum_inverted, b + 1)
            for g in range(G):
                if prepare:
                    pe.wait_ge(values_read, (b + 1) * KT + g + 1)
                rows(bank[:, EXP + g, :], [(spread_w[:, g * P:(g + 1) * P], ssum[:])]).then_inc(sum_spread, 1)
            pe.wait_ge(o_normed, b * G + G)
            for m in range(ET):
                rows(bank[:, EXP + m, :], [(W["Wo2"][:, t, m * P:(m + 1) * P], o[:, t, :])
                                           for t in range(ET)]).then_inc(out_filled, 1)
            pe.wait_ge(out_done, b * ET + ET)
            if prepare:
                second_half(b + 1)

        pe.wait_ge(consts_loaded, N_CONST)
        means(0)
        variance(0, 0)
        variance(0, 1)
        first_half(0)
        second_half(0)
        with pe.Fori(0, B - 1) as b:
            batch(b, True)
        batch(B - 1, False)


def build(nc, a, out_dram):
    x2_dram = nc.dram_tensor("x2_dram", [B, P, ET, L], F32, kind="Internal").ap()
    with ExitStack() as ctx:
        time_mix(nc, ctx, a, x2_dram)
    with ExitStack() as ctx:
        cross_attention(nc, ctx, a, x2_dram, out_dram)


def kernel(**inputs):
    import concourse.bacc as bacc
    from concourse.bass_utils import run_bass_kernel_spmd

    i = {k: np.asarray(v) for k, v in inputs.items()}
    t0, t1 = "L0_xattn_", "L1_xattn_"
    x, c = i["x"], i["ctx_2048"]

    def tiled(z):
        return z.reshape(z.shape[0], z.shape[1], ET, P).transpose(0, 3, 2, 1)

    w_v, w_g, w_o = i[t0 + "Wv"].T[:, VALUE_ORDER], i[t0 + "Wg"].T[:, VALUE_ORDER], i[t0 + "Wo"].T[VALUE_ORDER]
    rows = [i[t0 + n] for n in ("ln1_w", "ln1_b", "ln2_w", "ln2_b", "maa_x")]
    rows += list(i[t0 + "maa_stack"])
    rows += [i[t0 + "time_decay"], i[t0 + "faaaa"].reshape(E)]
    rows += [i[t0 + "gn_w"][VALUE_ORDER], i[t0 + "gn_b"][VALUE_ORDER]]
    rows += [i[t0 + n] for n in ("ffn_maa_k", "ffn_maa_r")]
    rows += [i[t1 + "ln_gamma"], i[t1 + "ln_beta"]]
    vecs = np.stack(rows).reshape(len(rows), ET, P).transpose(2, 0, 1).reshape(P, len(rows) * ET)
    vecs = np.concatenate([vecs, np.full((P, 1), EPS, np.float32), np.broadcast_to(i[t1 + "gate"], (P, 1))], 1)
    arrays = {
        "xT": tiled(x), "ctxT": tiled(c), "prev": tiled(c[:, 0:2]),
        "s0": c[:, 2:2 + D0].reshape(B, ET, P, D0).transpose(0, 2, 1, 3),
        "mask": i["mask_BxS2_bf1"].view(np.uint8), "vecs": vecs, "consts": shape_constants(),
        "maa_w1": i[t0 + "maa_w1"], "maa_w2": i[t0 + "maa_w2"].reshape(5 * MIX, E),
        "decay_w1": i[t0 + "decay_w1"], "decay_w2": i[t0 + "decay_w2"],
        "Wr": i[t0 + "Wr"].T, "Wk": i[t0 + "Wk"].T, "Wg": w_g, "Wv": w_v, "Wo": w_o,
        "fWk": i[t0 + "ffn_Wk"].T, "fWr": i[t0 + "ffn_Wr"].T, "fWv": i[t0 + "ffn_Wv"].T,
        "Wq2": i[t1 + "Wq"].T, "Wk2": i[t1 + "Wk"].T, "Wv2": i[t1 + "Wv"].T, "Wo2": i[t1 + "Wo"].T,
    }
    arrays = {f"in_{k}": np.ascontiguousarray(z) for k, z in arrays.items()}
    nc = bacc.Bacc("TRN2", target_bir_lowering=False, num_devices=1)
    a = {k[3:]: nc.dram_tensor(k, z.shape, mybir.dt.from_np(z.dtype), kind="ExternalInput").ap()
         for k, z in arrays.items()}
    out = nc.dram_tensor("out", (B, P, ET, L), F32, kind="ExternalOutput").ap()
    build(nc, a, out)
    got = run_bass_kernel_spmd(nc, [arrays], core_ids=[0]).results[0]["out"]
    return np.ascontiguousarray(got.transpose(0, 3, 2, 1)).reshape(B, L, E)
```

```python
from contextlib import ExitStack

import numpy as np

import concourse.bass as bass
from concourse import mybir

F32 = mybir.dt.float32
F32R = mybir.dt.float32r
U8 = mybir.dt.uint8
ALU = mybir.AluOpType
ACT = mybir.ActivationFunctionType
AX = mybir.AxisListType

P = 128
B = 4
L = 512
E = 512
ET = E // P
S2 = 1024
H0, D0 = 32, 16
HT = P // D0
H1, D1 = 16, 32
G = H1 * D1 // P
GH = P // D1
KT = S2 // P
MIX, DEC = 32, 64
EPS = 1e-5
SCALE = D1 ** -0.5
MASKED = -1e30

VECS = ["ln1_w", "ln1_b", "ln2_w", "ln2_b", "maa_x", "maa0", "maa1", "maa2", "maa3", "maa4", "time_decay",
        "faaaa", "gn_w", "gn_b", "ffn_maa_k", "ffn_maa_r", "ln_gamma", "ln_beta"]
V_EPS = len(VECS) * ET
V_GATE = V_EPS + 1
NV = V_GATE + 1

QUAD = 32
ND = D0 // 4


def value_row(h, d):
    return QUAD * (d % 4) + HT * (d // 4) + h


ORDER = np.zeros(P, int)
for _h in range(HT):
    for _d in range(D0):
        ORDER[value_row(_h, _d)] = _h * D0 + _d
VALUE_ORDER = np.concatenate([m * P + ORDER for m in range(ET)])

C_MEAN = 0
C_HEAD = C_MEAN + P
C_BONUS = C_HEAD + P
C_HSUM = C_BONUS + P
C_ROW = C_HSUM + ET * H0
C_HBC = C_ROW + ND * QUAD
C_PICK = C_HBC + ET * P
C_IDENT = C_PICK + D0 * P
C_ONE = C_IDENT + P
C_ABC = C_ONE + G * D1
NC_ = C_ABC + G * P


def shape_constants():
    c = np.zeros((P, NC_), np.float32)
    c[:, C_IDENT:C_IDENT + P] = np.eye(P)
    c[:, C_MEAN:C_MEAN + P] = 1.0 / E
    key_head = np.arange(P) // D0
    value_head, value_chan = ORDER // D0, ORDER % D0
    c[:, C_HEAD:C_HEAD + P] = (value_head[:, None] == value_head[None, :]) / D0
    c[:, C_BONUS:C_BONUS + P] = key_head[:, None] == value_head[None, :]
    for m in range(ET):
        for h in range(HT):
            c[value_head == h, C_HSUM + m * H0 + m * HT + h] = 1.0 / D0
            c[m * HT + h, C_HBC + m * P:C_HBC + (m + 1) * P] = value_head == h
    for n in range(ND):
        for h in range(HT):
            c[key_head == h, C_ROW + n * QUAD + n * HT + h] = 1.0
    for d in range(D0):
        c[:, C_PICK + d * P:C_PICK + (d + 1) * P] = ((value_head[:, None] == key_head[None, :])
                                                     & (value_chan[:, None] == d))
    c[:, C_ONE + G:C_ONE + D1] = 1.0
    for g in range(G):
        c[:, C_ONE + g * D1 + g] = 1.0
        for j in range(GH):
            c[D1 * j + g, C_ABC + g * P + D1 * j:C_ABC + g * P + D1 * (j + 1)] = 1.0
    return c


class Count:

    def __init__(self, *stages):
        self.per, self.first = 0, {}
        for name, n in stages:
            self.first[name] = self.per
            self.per += n

    def __call__(self, b, name, i=0):
        return b * self.per + self.first[name] + i + 1


MIXES = [("decay", 1), ("receptance", 3), ("key", 0), ("value", 2), ("gate", 4)]

PAIR = 2
NPAIR = D0 // PAIR
NU = ET * NPAIR


def load_context(sp, a, shared, b):
    return sp.dma_start(shared[:].rearrange("p (t l) -> p t l", t=ET),
                        a["ctxT"][bass.ds(b, 1)].rearrange("o p t l -> (o p) t l"))


def time_mix(nc, ctx, a, x2_dram, shared, c_loaded):
    def sb(name, shape, dt=F32):
        return ctx.enter_context(nc.sbuf_tensor(name, shape, dt))

    def sem(name):
        return ctx.enter_context(nc.semaphore(name))

    vec = sb("vec", [P, NV])
    con = sb("con", [P, C_PICK])
    pick = sb("pick", [P, D0 * P], F32R)
    w_maa1 = sb("w_maa1", [P, ET, 5 * MIX])
    w_maa2 = sb("w_maa2", [P, 5, E], F32R)
    w_dec1 = sb("w_dec1", [P, ET, DEC])
    w_dec2 = sb("w_dec2", [DEC, E])
    WEIGHTS = [("receptance", "Wr"), ("key", "Wk"), ("gate", "Wg"), ("value", "Wv"), ("wo", "Wo"),
               ("ffn_k", "fWk"), ("ffn_r", "fWr"), ("ffn_v", "fWv")]
    W = {n: sb(f"w_{n}", [P, ET, E]) for n, _ in WEIGHTS}

    xin = sb("xin", [P, ET, L])
    x = sb("x", [P, ET, L])
    buffers = shared[:].rearrange("p (n t l) -> p n t l", n=2, t=ET)
    xc, g_sb = buffers[:, 0], buffers[:, 1]
    sq = sb("sq", [P, ET, L])
    xn = sb("xn", [P, ET, L + 1])
    sx = sb("sx", [P, ET, L])
    xa = sb("xa", [P, ET * L])
    xb = sb("xb", [P, 2 * PAIR * (L + 1)])
    r_sb = sb("r_sb", [P, ET, L])
    k_sb = sb("k_sb", [P, ET, L])
    w_sb = sb("w_sb", [P, ET, L])
    v_hi = sb("v_hi", [P, ET, L], F32R)
    v_lo = sb("v_lo", [P, ET, L], F32R)
    rstd = sb("rstd", [P, L])
    s0 = sb("s0", [P, ET, D0])
    prev = sb("prev", [P, ET, 2])

    mixed = [xa[:].rearrange("p (t l) -> p t l", t=ET), xb[:, 0:ET * L].rearrange("p (t l) -> p t l", t=ET)]
    kv = sq[:].rearrange("p (u i) l -> p u i l", u=2)
    rs = xa[:].rearrange("p (u i l) -> p u i l", u=2, i=PAIR)
    st = xb[:].rearrange("p (u i l) -> p u i l", u=2, i=PAIR)
    hid, hide = rstd, xc[0:MIX, 0, :]
    hid_hi, hid_lo = v_lo[:, 1, :], v_lo[:, 2, :]
    hid_stack = [v_hi[:, i, :] for i in range(4)] + [v_lo[:, 0, :]]
    dec = rstd[0:DEC, :]
    centre_of = {1: g_sb, 2: xc}
    rstd_of = {1: w_sb[:, 0, :], 2: rstd[:]}

    bank = ctx.enter_context(nc.psum_tensor("bank", [P, 8, L], F32))

    con_loaded = sem("con_loaded")
    maa1_loaded = sem("maa1_loaded")
    consts_loaded = sem("consts_loaded")
    vec_loaded = sem("vec_loaded")
    pick_loaded = sem("pick_loaded")
    pick_ready = sem("pick_ready")
    maa2_loaded = sem("maa2_loaded")
    maa2_rounded = sem("maa2_rounded")
    maa2_ready = sem("maa2_ready")
    x_loaded = sem("x_loaded")
    prev_loaded = sem("prev_loaded")
    s0_loaded = sem("s0_loaded")
    front_filled = sem("front_filled")
    front_act_read = sem("front_act_read")
    front_dve_read = sem("front_dve_read")
    bank_filled = sem("bank_filled")
    act_read = sem("act_read")
    dve_read = sem("dve_read")
    squared = sem("squared")
    inverted = sem("inverted")
    scaled = sem("scaled")
    first_ready = sem("first_ready")
    xn_ready = sem("xn_ready")
    shifted = sem("shifted")
    lora_in = sem("lora_in")
    hid_rounded = sem("hid_rounded")
    hid_split = sem("hid_split")
    hide_stacked = sem("hide_stacked")
    hid_stacked = sem("hid_stacked")
    mixed_ready = sem("mixed_ready")
    mix_filled = sem("mix_filled")
    mix_read = sem("mix_read")
    decayed = sem("decayed")
    bonus_in = sem("bonus_in")
    spread = sem("spread")
    kv_ready = sem("kv_ready")
    st_first = sem("st_first")
    st_ready = sem("st_ready")
    rs_ready = sem("rs_ready")
    rs_used = sem("rs_used")
    att_ready = sem("att_ready")
    head_affine = sem("head_affine")
    gated = sem("gated")
    x_added = sem("x_added")
    squares_added = sem("squares_added")
    decay_mixed = sem("decay_mixed")
    ffn_mixed = sem("ffn_mixed")
    kk_ready = sem("kk_ready")
    x2_ready = sem("x2_ready")
    x2_stored = sem("x2_stored")

    N_CONST = 16 * (2 + len(WEIGHTS))
    N_MIXED = 5

    front_fills = Count(("mean1", 1), ("var1", 1), ("hidden", 2))
    front_act_reads = Count(("var1", 1), ("hidden", 2))
    fills = Count(("decay_in", 1), ("receptance", ET), ("decay", ET),
                  ("key", ET), ("value", ET), ("bonus", ET), ("gate", ET), ("head_mean", ET), ("head_var", 1),
                  ("head_rstd", ET), ("wo", ET), ("mean2", 1), ("var2", 1), ("ffn_k", ET), ("ffn_r", ET),
                  ("ffn_v", ET))
    act_reads = Count(("decay_in", 1), ("receptance", ET), ("decay", ET), ("key", ET),
                      ("value", ET), ("gate", ET), ("head_var", 1), ("var2", 1), ("ffn_k", ET), ("ffn_r", ET))
    dve_reads = Count(("value", ET), ("bonus", ET), ("gate", ET), ("head_mean", ET),
                      ("head_rstd", ET), ("wo", ET), ("mean2", ET), ("ffn_v", ET))
    squares = Count(("norm1", ET), ("head", ET), ("norm2", ET))
    inversions = Count(("norm1", 1), ("head", 1), ("norm2", 1))
    norms = Count(("norm1", ET), ("norm2", ET))
    MEAN, VAR, HIDDEN, DECAY_IN, HEAD_VAR = 4, 5, 6, 0, 4
    MIX_BANK, GATE_BANK, OUT_BANK = 4, 4, 6

    block = ctx.enter_context(nc.Block())

    def v(name, t):
        c = VECS.index(name) * ET + t
        return vec[:, c:c + 1]

    def over_pair(ap):
        return ap.unsqueeze(1).to_broadcast([P, PAIR, L])

    @block.sync
    def _(sp):
        sp.dma_start(vec[:], a["vecs"]).then_inc(vec_loaded, 16)
        def load_x(b):
            sp.dma_start(xin[:], a["xT"][bass.ds(b, 1)].rearrange("o p t l -> (o p) t l")).then_inc(x_loaded, 16)

        def load_prev(b):
            sp.dma_start(prev[:], a["prev"][bass.ds(b, 1)].rearrange("o p t d -> (o p) t d")).then_inc(prev_loaded, 16)

        def load_s0(b):
            sp.dma_start(s0[:], a["s0"][bass.ds(b, 1)].rearrange("o p t d -> (o p) t d")).then_inc(s0_loaded, 16)

        load_x(0)
        sp.dma_start(con[:], a["consts"][:, 0:C_PICK]).then_inc(con_loaded, 16)
        load_prev(0)
        sp.dma_start(w_maa1[:], a["maa_w1"].rearrange("(t p) n -> p t n", p=P)).then_inc(maa1_loaded, 16)
        for q in range(4):
            src = a["maa_w2"].rearrange("(i r) n -> r i n", r=MIX)
            rows = slice(MIX * q, MIX * (q + 1))
            sp.dma_start(r_sb[rows, :, :], src[:, 0:4, :]).then_inc(maa2_loaded, 16)
            sp.dma_start(k_sb[rows, 0, :], src[:, 4, :]).then_inc(maa2_loaded, 16)
        sp.dma_start(w_dec1[:], a["decay_w1"].rearrange("(t p) n -> p t n", p=P)).then_inc(consts_loaded, 16)
        sp.dma_start(w_dec2[:], a["decay_w2"]).then_inc(consts_loaded, 16)
        for name, src in WEIGHTS:
            sp.dma_start(W[name][:], a[src].rearrange("(t p) n -> p t n", p=P)).then_inc(consts_loaded, 16)
        load_s0(0)

        def stack_hidden(b):
            sp.wait_ge(hid_split, b + 1)
            for i in range(4):
                rows = slice(MIX * i, MIX * (i + 1))
                for q in range(4):
                    sp.dma_start(hid_stack[i][MIX * q:MIX * (q + 1), :].bitcast(F32),
                                 (hid_hi, hid_lo)[q % 2][rows, :].bitcast(F32)).then_inc(hid_stacked, 16)

        def store(b):
            sp.wait_ge(x2_ready, b * ET + ET)
            sp.dma_start(x2_dram[bass.ds(b, 1)].rearrange("o p t l -> (o p) t l"), x[:]).then_inc(x2_stored, 16)

        stack_hidden(0)
        with sp.Fori(0, B - 1) as b:
            sp.wait_ge(dve_read, dve_reads(b, "wo", ET - 1))
            load_x(b + 1)
            sp.wait_ge(first_ready, b * 2 + 2)
            load_prev(b + 1)
            stack_hidden(b + 1)
            store(b)
            sp.wait_ge(x2_stored, b * 16 + 16)
            load_s0(b + 1)
        sp.wait_ge(xn_ready, norms(B - 1, "norm2", ET - 1))
        load_context(sp, a, shared, 0).then_inc(c_loaded, 16)
        store(B - 1)
        sp.wait_ge(x2_stored, 16 * B)

    @block.gpsimd
    def _(pool):
        def add_tiles(b, to, src, added):
            half = ET // 2
            pool.tensor_tensor(to[:, 0:half, :], src[:, 0:half, :], src[:, half:ET, :], ALU.add).then_inc(added, 1)
            pool.wait_ge(added, b * 2 + 1)
            pool.tensor_tensor(to[:, 0, :], to[:, 0, :], to[:, 1, :], ALU.add).then_inc(added, 1)

        def front(b):
            pool.wait_ge(x_loaded, b * 16 + 16)
            add_tiles(b, centre_of[1], xin, x_added)
            pool.wait_ge(squared, squares(b, "norm1", ET - 1))
            add_tiles(b, sq, sq, squares_added)

        def batch(b, prepare):
            for u in range(NU):
                m = u // NPAIR
                pool.wait_ge(st_first, b * NU + u + 1)
                pool.wait_ge(st_ready, b * NU + u + 1)
                if u < 2:
                    pool.wait_ge(bank_filled, fills(b, "value", ET - 1))
                else:
                    pool.wait_ge(rs_used, b * NU + u - 1)
                pool.tensor_tensor(rs[:, u % 2], st[:, u % 2, :, 0:L], over_pair(r_sb[:, m, :]),
                                   ALU.mult).then_inc(rs_ready, 1)
            if prepare:
                front(b + 1)

        front(0)
        with pool.Fori(0, B - 1) as b:
            batch(b, True)
        batch(B - 1, False)

    @block.scalar
    def _(act):
        act.dma_start(xa[:], a["consts"][:, C_PICK:C_IDENT]).then_inc(pick_loaded, 16)
        act.wait_ge(vec_loaded, 16)

        def norm_squares(b, q):
            for t in range(ET):
                if q == 1:
                    act.wait_ge(front_dve_read, b * ET + t + 1)
                else:
                    act.wait_ge(dve_read, dve_reads(b, "mean2", t))
                act.activation(sq[:, t, :], centre_of[q][:, t, :], ACT.Square).then_inc(squared, 1)

        def norm_deviation(b, q):
            if q == 1:
                act.wait_ge(front_filled, front_fills(b, "var1"))
            else:
                act.wait_ge(bank_filled, fills(b, "var2"))
            act.activation(rstd_of[q], bank[:, VAR, :], ACT.Sqrt, bias=vec[:, V_EPS:V_EPS + 1]
                           ).then_inc(front_act_read if q == 1 else act_read, 1)

        def norm_affine(b, q):
            if q == 1:
                act.wait_ge(prev_loaded, b * 16 + 16)
            for t in range(ET):
                act.wait_ge(scaled, norms(b, f"norm{q}", t))
                if t == 0:
                    act.activation(xn[:, :, 0:1], prev[:, :, 2 - q:3 - q], ACT.Copy).then_inc(first_ready, 1)
                act.activation(xn[:, t, 1:L + 1], centre_of[q][:, t, :], ACT.Identity, scale=v(f"ln{q}_w", t),
                               bias=v(f"ln{q}_b", t)).then_inc(xn_ready, 1)

        def gate(b, m):
            act.wait_ge(bank_filled, fills(b, "gate", m))
            act.activation(g_sb[:, m, :], bank[:, GATE_BANK + m % 2, :], ACT.Tanh, scale=0.5).then_inc(act_read, 1)

        def hidden(b):
            act.wait_ge(front_filled, front_fills(b, "hidden", 0))
            act.activation(hid[:], bank[:, HIDDEN, :], ACT.Tanh).then_inc(front_act_read, 1)
            act.wait_ge(front_act_read, front_act_reads(b, "hidden", 0))
            act.activation(hid_hi, hid[:], ACT.Copy).then_inc(hid_rounded, 1)
            act.wait_ge(front_filled, front_fills(b, "hidden", 1))
            act.activation(hide, bank[0:MIX, HIDDEN + 1, :], ACT.Tanh).then_inc(front_act_read, 1)
            act.wait_ge(front_act_read, front_act_reads(b, "hidden", 1))
            act.activation(hid_stack[4][0:MIX, :], hide, ACT.Copy).then_inc(hid_rounded, 1)
            act.activation(hid_stack[4][2 * MIX:3 * MIX, :], hide, ACT.Copy).then_inc(hid_rounded, 1)

        def batch(b, prepare):
            act.wait_ge(bank_filled, fills(b, "decay_in"))
            act.activation(dec, bank[0:DEC, DECAY_IN, :], ACT.Tanh).then_inc(act_read, 1)
            for m in range(ET):
                act.wait_ge(bank_filled, fills(b, "receptance", m))
                act.activation(r_sb[:, m, :], bank[:, m, :], ACT.Copy).then_inc(act_read, 1)
            for m in range(ET):
                act.wait_ge(bank_filled, fills(b, "decay", m))
                act.activation(w_sb[:, m, :], bank[:, m, :], ACT.Exp, bias=v("time_decay", m)).then_inc(act_read, 1)
            for m in range(ET):
                act.wait_ge(act_read, act_reads(b, "decay", m))
                act.activation(w_sb[:, m, :], w_sb[:, m, :], ACT.Exp, scale=-1.0).then_inc(decayed, 1)
            for m in range(ET):
                act.wait_ge(bank_filled, fills(b, "key", m))
                act.activation(k_sb[:, m, :], bank[:, m, :], ACT.Copy).then_inc(act_read, 1)
            for m in range(ET):
                act.wait_ge(bank_filled, fills(b, "value", m))
                act.activation(xc[:, m, :], bank[:, m, :], ACT.Copy)
                act.activation(v_hi[:, m, :], bank[:, m, :], ACT.Copy).then_inc(act_read, 1)
            for u in range(NU):
                m, c = u // NPAIR, (u % NPAIR) * PAIR
                if u == 0:
                    act.wait_ge(s0_loaded, b * 16 + 16)
                if u >= 2:
                    act.wait_ge(rs_ready, b * NU + u - 1)
                act.activation(st[:, u % 2, :, 0:1], s0[:, m, c:c + PAIR].unsqueeze(2), ACT.Copy).then_inc(st_first, 1)
                if u % NPAIR == 0 and m >= 1:
                    gate(b, m - 1)
            gate(b, ET - 1)
            for m in range(ET):
                act.wait_ge(dve_read, dve_reads(b, "head_mean", m))
                act.activation(sq[:, m, :], xc[:, m, :], ACT.Square).then_inc(squared, 1)
            act.wait_ge(bank_filled, fills(b, "head_var"))
            act.activation(rstd[0:H0, :], bank[0:H0, HEAD_VAR, :], ACT.Sqrt,
                           bias=vec[0:H0, V_EPS:V_EPS + 1]).then_inc(act_read, 1)
            for m in range(ET):
                act.wait_ge(dve_read, dve_reads(b, "head_rstd", m))
                act.activation(xc[:, m, :], xc[:, m, :], ACT.Identity, scale=v("gn_w", m),
                               bias=v("gn_b", m)).then_inc(head_affine, 1)
            norm_squares(b, 2)
            norm_deviation(b, 2)
            norm_affine(b, 2)
            if prepare:
                norm_squares(b + 1, 1)
            for m in range(ET):
                act.wait_ge(bank_filled, fills(b, "ffn_k", m))
                act.activation(k_sb[:, m, :], bank[:, m, :], ACT.Relu).then_inc(act_read, 1)
            if prepare:
                norm_deviation(b + 1, 1)
                norm_affine(b + 1, 1)
            for m in range(ET):
                act.wait_ge(act_read, act_reads(b, "ffn_k", m))
                act.activation(k_sb[:, m, :], k_sb[:, m, :], ACT.Square).then_inc(kk_ready, 1)
            for m in range(ET):
                act.wait_ge(bank_filled, fills(b, "ffn_r", m))
                act.activation(r_sb[:, m, :], bank[:, m, :], ACT.Tanh, scale=0.5).then_inc(act_read, 1)
                if m == 1 and prepare:
                    hidden(b + 1)

        norm_squares(0, 1)
        norm_deviation(0, 1)
        norm_affine(0, 1)
        act.wait_ge(pick_loaded, 16)
        act.activation(pick[:], xa[:], ACT.Copy).then_inc(pick_ready, 1)
        act.wait_ge(maa2_loaded, 16 * 8)
        act.activation(w_maa2[:, 0:4, :], r_sb[:], ACT.Copy).then_inc(maa2_rounded, 1)
        act.activation(w_maa2[:, 4, :], k_sb[:, 0, :], ACT.Copy).then_inc(maa2_rounded, 1)
        hidden(0)
        with act.Fori(0, B - 1) as b:
            batch(b, True)
        batch(B - 1, False)

    @block.vector
    def _(dve):
        dve.wait_ge(vec_loaded, 16)
        def centre(b, q, src):
            if q == 1:
                dve.wait_ge(front_filled, front_fills(b, "mean1"))
            else:
                dve.wait_ge(bank_filled, fills(b, "mean2"))
            for t in range(ET):
                dve.tensor_tensor(centre_of[q][:, t, :], src[:, t, :], bank[:, MEAN, :], ALU.subtract
                                  ).then_inc(front_dve_read if q == 1 else dve_read, 1)

        def scale(b, q):
            if q == 1:
                dve.wait_ge(front_act_read, front_act_reads(b, "var1"))
            else:
                dve.wait_ge(act_read, act_reads(b, "var2"))
            dve.reciprocal(rstd_of[q], rstd_of[q]).then_inc(inverted, 1)
            dve.wait_ge(inverted, inversions(b, f"norm{q}"))
            for t in range(ET):
                dve.tensor_tensor(centre_of[q][:, t, :], centre_of[q][:, t, :], rstd_of[q], ALU.mult
                                  ).then_inc(scaled, 1)

        def shift(b, q, t):
            dve.wait_ge(xn_ready, norms(b, f"norm{q}", t))
            dve.tensor_tensor(sx[:, t, :], xn[:, t, 0:L], xn[:, t, 1:L + 1], ALU.subtract).then_inc(shifted, 1)

        def kv_pair(b, u):
            m = u // NPAIR
            dve.wait_ge(spread, b * NU + u + 1)
            if u >= 2:
                dve.wait_ge(st_ready, b * NU + u - 1)
            c = PAIR * (u % 2)
            dve.tensor_tensor(kv[:, u % 2], bank[:, c:c + PAIR, :], over_pair(k_sb[:, m, :]),
                              ALU.mult).then_inc(kv_ready, 1)

        def gate(b, m):
            dve.wait_ge(act_read, act_reads(b, "gate", m))
            dve.scalar_tensor_tensor(out=g_sb[:, m, :], in0=g_sb[:, m, :], scalar=1.0,
                                     in1=bank[:, GATE_BANK + m % 2, :], op0=ALU.add, op1=ALU.mult
                                     ).then_inc(dve_read, 1)

        def add_mix(b, m):
            dve.wait_ge(dve_read, dve_reads(b, "ffn_v", m))
            dve.scalar_tensor_tensor(out=x[:, m, :], in0=w_sb[:, m, :], scalar=0.5, in1=x[:, m, :],
                                     op0=ALU.mult, op1=ALU.add).then_inc(x2_ready, 1)

        def attention_tile(b, m):
            dve.wait_ge(rs_used, b * NU + NPAIR * (m + 1))
            dve.tensor_tensor(xc[:, m, :], xc[:, m, :], bank[:, OUT_BANK + m % 2, :], ALU.add).then_inc(att_ready, 1)

        def front(b):
            scale(b, 1)
            dve.wait_ge(first_ready, b * 2 + 1)
            for t in range(ET):
                shift(b, 1, t)
                dve.wait_ge(shifted, norms(b, "norm1", t))
                dve.scalar_tensor_tensor(out=sq[:, t, :], in0=sx[:, t, :], scalar=v("maa_x", t),
                                         in1=xn[:, t, 1:L + 1], op0=ALU.mult, op1=ALU.add).then_inc(lora_in, 1)

        def hidden(b):
            dve.wait_ge(hid_rounded, b * 3 + 1)
            dve.tensor_tensor(hid_lo, hid[:], hid_hi.bitcast(F32), ALU.subtract).then_inc(hid_split, 1)
            dve.wait_ge(hid_rounded, b * 3 + 3)
            for q in (1, 3):
                dve.tensor_tensor(hid_stack[4][MIX * q:MIX * (q + 1), :], hide, hid_stack[4][0:MIX, :].bitcast(F32),
                                  ALU.subtract).then_inc(hide_stacked, 1)

        def batch(b, prepare):
            last_use = [("decay_in", 0)] + [(name, ET - 1) for name, _ in MIXES[1:]]
            for s, (name, i) in enumerate(MIXES):
                to = sx[:] if name == "gate" else mixed[s % 2]
                if s >= 2 and name != "gate":
                    dve.wait_ge(bank_filled, fills(b, *last_use[s - 2]))
                for t in range(ET):
                    dve.wait_ge(mix_filled, b * 5 * ET + s * ET + t + 1)
                    dve.scalar_tensor_tensor(out=to[:, t, :], in0=bank[:, MIX_BANK + t, :], scalar=v(f"maa{i}", t),
                                             in1=sx[:, t, :], op0=ALU.add, op1=ALU.mult).then_inc(mix_read, 1)
                    if s == 0:
                        dve.wait_ge(mix_read, b * 5 * ET + t + 1)
                        dve.tensor_tensor(to[:, t, :], to[:, t, :], xn[:, t, 1:L + 1], ALU.add).then_inc(decay_mixed, 1)
                if s >= 1:
                    dve.wait_ge(mix_read, b * 5 * ET + s * ET + ET)
                    dve.tensor_tensor(to, to, xn[:, :, 1:L + 1], ALU.add).then_inc(mixed_ready, 1)
            for m in range(ET):
                dve.wait_ge(act_read, act_reads(b, "key", m))
                dve.scalar_tensor_tensor(out=sq[:, m, :], in0=r_sb[:, m, :], scalar=v("faaaa", m),
                                         in1=k_sb[:, m, :], op0=ALU.mult, op1=ALU.mult).then_inc(bonus_in, 1)
            for m in range(ET):
                dve.wait_ge(act_read, act_reads(b, "value", m))
                dve.tensor_tensor(v_lo[:, m, :], bank[:, m, :], v_hi[:, m, :].bitcast(F32),
                                  ALU.subtract).then_inc(dve_read, 1)
            for m in range(ET):
                dve.wait_ge(bank_filled, fills(b, "bonus", m))
                dve.tensor_tensor(xc[:, m, :], bank[:, m, :], xc[:, m, :], ALU.mult).then_inc(dve_read, 1)
            dve.wait_ge(decayed, b * ET + ET)
            dve.wait_ge(s0_loaded, b * 16 + 16)
            kv_pair(b, 0)
            for u in range(NU):
                m, c = u // NPAIR, (u % NPAIR) * PAIR
                if u + 1 < NU:
                    kv_pair(b, u + 1)
                dve.wait_ge(kv_ready, b * NU + u + 1)
                if u >= 2:
                    dve.wait_ge(rs_ready, b * NU + u - 1)
                for i in range(PAIR):
                    scan = dve.tensor_tensor_scan(st[:, u % 2, i, 1:L + 1], w_sb[:, m, :], kv[:, u % 2, i, :],
                                                  s0[:, m, c + i:c + i + 1], ALU.mult, ALU.add)
                scan.then_inc(st_ready, 1)
                if u % NPAIR == 2 and m >= 1:
                    gate(b, m - 1)
                if u % NPAIR == 4 and m >= 1:
                    attention_tile(b, m - 1)
            attention_tile(b, ET - 1)
            gate(b, ET - 1)
            for m in range(ET):
                dve.wait_ge(bank_filled, fills(b, "head_mean", m))
                dve.tensor_tensor(xc[:, m, :], xc[:, m, :], bank[:, m, :], ALU.subtract).then_inc(dve_read, 1)
            dve.wait_ge(act_read, act_reads(b, "head_var"))
            dve.reciprocal(rstd[0:H0, :], rstd[0:H0, :]).then_inc(inverted, 1)
            for m in range(ET):
                dve.wait_ge(bank_filled, fills(b, "head_rstd", m))
                dve.tensor_tensor(xc[:, m, :], xc[:, m, :], bank[:, m, :], ALU.mult).then_inc(dve_read, 1)
            for m in range(ET):
                dve.wait_ge(head_affine, b * ET + m + 1)
                dve.scalar_tensor_tensor(out=xc[:, m, :], in0=xc[:, m, :], scalar=0.5, in1=g_sb[:, m, :],
                                         op0=ALU.mult, op1=ALU.mult).then_inc(gated, 1)
            for m in range(ET):
                dve.wait_ge(bank_filled, fills(b, "wo", m))
                dve.tensor_tensor(x[:, m, :], xin[:, m, :], bank[:, m, :], ALU.add).then_inc(dve_read, 1)
            centre(b, 2, x)
            scale(b, 2)
            dve.wait_ge(first_ready, b * 2 + 2)
            for t in range(ET):
                shift(b, 2, t)
                dve.wait_ge(shifted, norms(b, "norm2", t))
                dve.scalar_tensor_tensor(out=mixed[0][:, t, :], in0=sx[:, t, :], scalar=v("ffn_maa_k", t),
                                         in1=xn[:, t, 1:L + 1], op0=ALU.mult, op1=ALU.add).then_inc(ffn_mixed, 1)
            if prepare:
                centre(b + 1, 1, xin)
            for t in range(ET):
                ins = dve.scalar_tensor_tensor(out=mixed[1][:, t, :], in0=sx[:, t, :], scalar=v("ffn_maa_r", t),
                                               in1=xn[:, t, 1:L + 1], op0=ALU.mult, op1=ALU.add)
            ins.then_inc(mixed_ready, 1)
            if prepare:
                front(b + 1)
                hidden(b + 1)
            for m in range(ET):
                dve.wait_ge(bank_filled, fills(b, "ffn_v", m))
                dve.scalar_tensor_tensor(out=w_sb[:, m, :], in0=r_sb[:, m, :], scalar=1.0, in1=bank[:, m, :],
                                         op0=ALU.add, op1=ALU.mult).then_inc(dve_read, 1)
                if m >= 1:
                    add_mix(b, m - 1)
            add_mix(b, ET - 1)

        centre(0, 1, xin)
        front(0)
        dve.wait_ge(maa2_rounded, 2)
        half = slice(2 * MIX, 4 * MIX)
        dve.tensor_tensor(w_maa2[half, 0:4, :], r_sb[half, :, :], w_maa2[half, 0:4, :].bitcast(F32),
                          ALU.subtract).then_inc(maa2_ready, 1)
        dve.tensor_tensor(w_maa2[half, 4, :], k_sb[half, 0, :], w_maa2[half, 4, :].bitcast(F32),
                          ALU.subtract).then_inc(maa2_ready, 1)
        hidden(0)
        with dve.Fori(0, B - 1) as b:
            batch(b, True)
        batch(B - 1, False)

    @block.tensor
    def _(pe):
        mean_w = con[:, C_MEAN:C_MEAN + P]

        def rows(to, pairs):
            for n, (lhsT, rhs) in enumerate(pairs):
                ins = pe.matmul(to, lhsT, rhs, start=(n == 0), stop=(n == len(pairs) - 1))
            return ins

        def project(m, weight, src):
            return rows(bank[:, m, :], [(weight[:, t, m * P:(m + 1) * P], src[:, t, :]) for t in range(ET)])

        def project_by_input(weight, src, ready, b):
            for t in range(ET):
                pe.wait_ge(ready, b * ET + t + 1)
                for m in range(ET):
                    ins = pe.matmul(bank[:, m, :], weight[:, t, m * P:(m + 1) * P], src[:, t, :], start=(t == 0),
                                    stop=(t == ET - 1))
                    if t == ET - 1:
                        ins.then_inc(bank_filled, 1)

        def norm_var(b):
            for t in range(ET):
                pe.wait_ge(squared, squares(b, "norm2", t))
                ins = pe.matmul(bank[:, VAR, :], mean_w, sq[:, t, :], start=(t == 0), stop=(t == ET - 1))
            return ins

        def front_mean(b):
            pe.wait_ge(x_added, b * 2 + 2)
            rows(bank[:, MEAN, :], [(mean_w, centre_of[1][:, 0, :])]).then_inc(front_filled, 1)

        def front_var(b):
            pe.wait_ge(squares_added, b * 2 + 2)
            rows(bank[:, VAR, :], [(mean_w, sq[:, 0, :])]).then_inc(front_filled, 1)

        def hidden(b):
            for n, cols in enumerate((slice(0, P), slice(P, 5 * MIX))):
                for t in range(ET):
                    pe.wait_ge(lora_in, b * ET + t + 1)
                    ins = pe.matmul(bank[0:cols.stop - cols.start, HIDDEN + n, :], w_maa1[:, t, cols], sq[:, t, :],
                                    start=(t == 0), stop=(t == ET - 1))
                ins.then_inc(front_filled, 1)

        def low_rank(b, s):
            i = MIXES[s][1]
            for t in range(ET):
                if s >= 1:
                    pe.wait_ge(mix_read, b * 5 * ET + (s - 1) * ET + t + 1)
                pe.matmul(bank[:, MIX_BANK + t, :], w_maa2[:, i, t * P:(t + 1) * P], hid_stack[i], start=True,
                          stop=True).then_inc(mix_filled, 1)

        def sum_pair(b, u):
            m, c = u // NPAIR, (u % NPAIR) * PAIR
            if u % NPAIR == 0 and m >= 2:
                pe.wait_ge(att_ready, b * ET + m - 1)
            pe.wait_ge(rs_ready, b * NU + u + 1)
            for i in range(PAIR):
                q, n = (c + i) % 4, (c + i) // 4
                ins = pe.matmul(bank[QUAD * q:QUAD * (q + 1), OUT_BANK + m % 2, :],
                                con[:, C_ROW + n * QUAD:C_ROW + (n + 1) * QUAD], rs[:, u % 2, i, :],
                                start=(n == 0), stop=(n == ND - 1))
            ins.then_inc(rs_used, 1)

        def gate_part(b, n):
            m, t = n // ET, n % ET
            if n == 0:
                pe.wait_ge(mixed_ready, b * N_MIXED + 4)
            if t == 0 and m >= 2:
                pe.wait_ge(dve_read, dve_reads(b, "gate", m - 2))
            ins = pe.matmul(bank[:, GATE_BANK + m % 2, :], W["gate"][:, t, m * P:(m + 1) * P], sx[:, t, :],
                            start=(t == 0), stop=(t == ET - 1))
            if t == ET - 1:
                ins.then_inc(bank_filled, 1)

        def batch(b, prepare):
            pe.wait_ge(hid_stacked, b * 256 + 256)
            pe.wait_ge(hide_stacked, b * 2 + 2)
            low_rank(b, 0)
            low_rank(b, 1)
            for t in range(ET):
                pe.wait_ge(decay_mixed, b * ET + t + 1)
                ins = pe.matmul(bank[0:DEC, DECAY_IN, :], w_dec1[:, t, :], mixed[0][:, t, :], start=(t == 0),
                                stop=(t == ET - 1))
            ins.then_inc(bank_filled, 1)
            low_rank(b, 2)
            pe.wait_ge(mixed_ready, b * N_MIXED + 1)
            pe.wait_ge(act_read, act_reads(b, "decay_in"))
            for m in range(ET):
                project(m, W["receptance"], mixed[1]).then_inc(bank_filled, 1)
            for m in range(ET):
                pe.wait_ge(act_read, act_reads(b, "receptance", m))
                rows(bank[:, m, :], [(w_dec2[:, m * P:(m + 1) * P], dec)]).then_inc(bank_filled, 1)
            low_rank(b, 3)
            pe.wait_ge(mixed_ready, b * N_MIXED + 2)
            for m in range(ET):
                pe.wait_ge(act_read, act_reads(b, "decay", m))
                project(m, W["key"], mixed[0]).then_inc(bank_filled, 1)
            low_rank(b, 4)
            pe.wait_ge(mixed_ready, b * N_MIXED + 3)
            for m in range(ET):
                pe.wait_ge(act_read, act_reads(b, "key", m))
                project(m, W["value"], mixed[1]).then_inc(bank_filled, 1)
            for m in range(ET):
                pe.wait_ge(bonus_in, b * ET + m + 1)
                pe.wait_ge(dve_read, dve_reads(b, "value", m))
                rows(bank[:, m, :], [(con[:, C_BONUS:C_BONUS + P], sq[:, m, :])]).then_inc(bank_filled, 1)
            pe.wait_ge(dve_read, dve_reads(b, "bonus", ET - 1))
            for u in range(NU):
                m, c = u // NPAIR, (u % NPAIR) * PAIR
                if u >= 2:
                    pe.wait_ge(kv_ready, b * NU + u - 1)
                for i in range(PAIR):
                    to_d = pick[:, (c + i) * P:(c + i + 1) * P]
                    ins = rows(bank[:, PAIR * (u % 2) + i, :], [(to_d, v_hi[:, m, :]), (to_d, v_lo[:, m, :])])
                ins.then_inc(spread, 1)
                if u % 2 == 1:
                    gate_part(b, u // 2)
                if u >= 3:
                    sum_pair(b, u - 3)
            for u in range(NU - 3, NU):
                sum_pair(b, u)
            pe.wait_ge(kv_ready, b * NU + NU)
            for m in range(ET):
                pe.wait_ge(att_ready, b * ET + m + 1)
                rows(bank[:, m, :], [(con[:, C_HEAD:C_HEAD + P], xc[:, m, :])]).then_inc(bank_filled, 1)
            for m in range(ET):
                pe.wait_ge(squared, squares(b, "head", m))
                ins = pe.matmul(bank[0:H0, HEAD_VAR, :], con[:, C_HSUM + m * H0:C_HSUM + (m + 1) * H0], sq[:, m, :],
                                start=(m == 0), stop=(m == ET - 1))
            ins.then_inc(bank_filled, 1)
            pe.wait_ge(inverted, inversions(b, "head"))
            for m in range(ET):
                rows(bank[:, m, :], [(con[:, C_HBC + m * P:C_HBC + (m + 1) * P], rstd[:])]).then_inc(bank_filled, 1)
            pe.wait_ge(dve_read, dve_reads(b, "head_rstd", ET - 1))
            project_by_input(W["wo"], xc, gated, b)
            pe.wait_ge(dve_read, dve_reads(b, "wo", ET - 1))
            rows(bank[:, MEAN, :], [(mean_w, x[:, t, :]) for t in range(ET)]).then_inc(bank_filled, 1)
            norm_var(b).then_inc(bank_filled, 1)
            if prepare:
                front_mean(b + 1)
            project_by_input(W["ffn_k"], mixed[0], ffn_mixed, b)
            if prepare:
                front_var(b + 1)
            pe.wait_ge(mixed_ready, b * N_MIXED + 5)
            for m in range(ET):
                pe.wait_ge(act_read, act_reads(b, "ffn_k", m))
                project(m, W["ffn_r"], mixed[1]).then_inc(bank_filled, 1)
                if m == 1 and prepare:
                    hidden(b + 1)
            pe.wait_ge(kk_ready, b * ET + ET)
            for m in range(ET):
                pe.wait_ge(act_read, act_reads(b, "ffn_r", m))
                project(m, W["ffn_v"], k_sb).then_inc(bank_filled, 1)
            pe.wait_ge(dve_read, dve_reads(b, "ffn_v", ET - 1))

        pe.wait_ge(con_loaded, 16)
        front_mean(0)
        front_var(0)
        pe.wait_ge(maa1_loaded, 16)
        hidden(0)
        pe.wait_ge(consts_loaded, N_CONST)
        pe.wait_ge(pick_ready, 1)
        pe.wait_ge(maa2_ready, 2)
        with pe.Fori(0, B - 1) as b:
            batch(b, True)
        batch(B - 1, False)


MASK_ROW, MAX_ROW = 3 * QUAD, 3 * QUAD + 1
HALF = S2 // L
NS = HALF * GH * ET
NPT = 3
N_STEP = G * KT
SCORE_KT = 2
FILL_KT = 3
ADD_KT = 6
MEAN_KT = 5
TURN_KT = KT - 1


def score_slots(kt):
    n, i = TURN_KT - SCORE_KT, kt - SCORE_KT
    return range(NS * i // n, NS * (i + 1) // n) if 0 <= i < n else range(0)


def fill_slots(g, kt):
    return [kt - FILL_KT] if g + 2 < G and FILL_KT <= kt < FILL_KT + 3 else []


FIRST_FILLS = [[0], [], [1], [], [2]]
FIRST_SCORES = [range(NS * i // 3, NS * (i + 1) // 3) for i in range(3)]


def cross_attention(nc, ctx, a, x2_dram, out_dram, shared, c_loaded):
    def sb(name, shape, dt=F32):
        return ctx.enter_context(nc.sbuf_tensor(name, shape, dt))

    def sem(name):
        return ctx.enter_context(nc.semaphore(name))

    vec = sb("vec2", [P, NV])
    ident = sb("ident", [P, P])
    mean_w = sb("mean_w", [P, P])
    one = sb("one", [P, G * D1])
    spread_w = sb("spread_w", [P, G * P])
    W = {n: sb(f"w2_{n}", [P, ET, E]) for n in ["Wk2", "Wq2", "Wv2", "Wo2"]}
    tg = sb("tg", [P, 1])

    c = shared[:].rearrange("p (t l) -> p t l", t=ET)
    sq = sb("sq2", [P, ET, L])
    xq = sb("xq", [P, ET, L])
    xr = sb("xr", [P, ET, L])
    rstd = sb("rstd2", [P, HALF, L])
    mask8 = sb("mask8", [1, S2], U8)
    vals = sb("vals", [P, KT, E])
    part = sb("part", [P, 3, S2 + L], F32R)
    stack = sb("stack", [P, 2, HALF + 1, GH, L], F32R)
    ka, qa = stack[:, :, 0:HALF], stack[:, :, HALF]
    pt = sb("pt", [P, NPT, GH, L])
    acc = sb("acc", [P, GH, L])
    mx = sb("mx", [P, HALF, GH * ET])
    mxx = sb("mxx", [P, GH * ET])
    mt = sb("mt", [GH * ET, P], F32R)
    ssum = sb("ssum", [P, L])
    o = sb("o", [P, G, L])
    maskf = sq[0:1, 0:HALF, :].bitcast(F32R)

    bank = ctx.enter_context(nc.psum_tensor("bank2", [P, 8, L], F32))
    EXP, OUT, KQ = 2, 6, 7

    vec_loaded = sem("vec_loaded2")
    mean_loaded = sem("mean_loaded")
    consts_loaded = sem("consts_loaded2")
    rows_zeroed = sem("rows_zeroed")
    rows_set = sem("rows_set")
    xq_loaded = sem("xq_loaded")
    xr_loaded = sem("xr_loaded")
    mask_loaded = sem("mask_loaded")
    mask_made = sem("mask_made")
    mask_placed = sem("mask_placed")
    gate_ready = sem("gate_ready")
    mean_filled = sem("mean_filled")
    var_filled = sem("var_filled")
    kq_filled = sem("kq_filled")
    scores_filled = sem("scores_filled")
    max_turned = sem("max_turned")
    values_filled = sem("values_filled")
    sum_spread = sem("sum_spread")
    out_filled = sem("out_filled")
    centred = sem("centred2")
    squared = sem("squared2")
    sd_ready = sem("sd_ready")
    inverted = sem("inverted2")
    scaled = sem("scaled2")
    normed = sem("normed2")
    kq_high = sem("kq_high")
    kq_low = sem("kq_low")
    placed = sem("placed")
    scores_read = sem("scores_read")
    max_ready = sem("max_ready")
    max_taken = sem("max_taken")
    max_placed = sem("max_placed")
    values_read = sem("values_read")
    scored = sem("scored")
    exp_done = sem("exp_done")
    pv_done = sem("pv_done")
    o_read = sem("o_read")
    added = sem("added")
    summed = sem("summed")
    sum_kept = sem("sum_kept")
    sum_inverted = sem("sum_inverted")
    o_normed = sem("o_normed")
    out_done = sem("out_done")
    out_stored = sem("out_stored")

    N_CONST = 16 * 7
    N_PLACED = 16 * 3 * GH
    N_MASK = 16 * HALF
    N_EXP = 2 * N_STEP
    N_ADD = ADD_KT - 1

    block = ctx.enter_context(nc.Block())

    def v(name, t):
        i = VECS.index(name) * ET + t
        return vec[:, i:i + 1]

    def tile_half(x, t, h):
        return x[:, t, h * L:(h + 1) * L]


    @block.sync
    def _(sp):
        def load(b):
            sp.dma_start(mask8[:], a["mask"][bass.ds(b, 1)]).then_inc(mask_loaded, 16)
            sp.dma_start(xq[:], x2_dram[bass.ds(b, 1)].rearrange("o p t l -> (o p) t l")).then_inc(xq_loaded, 16)

        def load_residual(b):
            sp.dma_start(xr[:], x2_dram[bass.ds(b, 1)].rearrange("o p t l -> (o p) t l")).then_inc(xr_loaded, 16)

        sp.dma_start(mean_w[:], a["consts"][:, C_MEAN:C_MEAN + P]).then_inc(mean_loaded, 16)
        sp.dma_start(vec[:], a["vecs"]).then_inc(vec_loaded, 16)
        load(0)
        for n in W:
            sp.dma_start(W[n][:], a[n].rearrange("(t p) n -> p t n", p=P)).then_inc(consts_loaded, 16)
        sp.dma_start(ident[:], a["consts"][:, C_IDENT:C_IDENT + P]).then_inc(consts_loaded, 16)
        sp.dma_start(one[:], a["consts"][:, C_ONE:C_ABC]).then_inc(consts_loaded, 16)
        sp.dma_start(spread_w[:], a["consts"][:, C_ABC:NC_]).then_inc(consts_loaded, 16)
        load_residual(0)

        def place_group(b, g):
            if g < 2:
                sp.wait_ge(kq_low, (b * G + g) * 3 + 3)
            if g >= 2:
                sp.wait_ge(scored, b * N_EXP + 2 * KT * (g - 1))
            for j in range(GH):
                rows = slice(QUAD * j, QUAD * (j + 1))
                for n in range(3):
                    sp.dma_start(stack[QUAD * n:QUAD * (n + 1), g % 2, :, j, :].bitcast(F32),
                                 part[rows, n, :].bitcast(F32).rearrange("p (h l) -> p h l", l=L)
                                 ).then_inc(placed, 16)
            if g < 2:
                sp.wait_ge(mask_made, b + 1)
                for h in range(HALF):
                    sp.dma_start(ka[MASK_ROW:MASK_ROW + 1, g, h].bitcast(F32),
                                 maskf[:, h, :].bitcast(F32).unsqueeze(1).to_broadcast([1, GH, L])
                                 ).then_inc(mask_placed, 16)

        def place_max(b, g):
            sp.wait_ge(max_taken, b * G + g + 1)
            sp.dma_start(qa[MAX_ROW:MAX_ROW + 1, g % 2, :, :].bitcast(F32).rearrange("o j (q l) -> o (j q) l", l=P),
                         mt[:].bitcast(F32)).then_inc(max_placed, 16)

        def batch(b, prepare):
            for g in range(G):
                place_max(b, g)
                if g + 1 < G:
                    place_group(b, g + 1)
                if g == 2 and prepare:
                    load_context(sp, a, shared, b + 1).then_inc(c_loaded, 16)
                    load(b + 1)
            if prepare:
                place_group(b + 1, 0)
            sp.wait_ge(out_done, b * ET + ET)
            sp.dma_start(out_dram[bass.ds(b, 1)].rearrange("o p t l -> (o p) t l"), xr[:]).then_inc(out_stored, 16)
            if prepare:
                sp.wait_ge(out_stored, b * 16 + 16)
                load_residual(b + 1)

        sp.wait_ge(rows_set, 2)
        place_group(0, 0)
        with sp.Fori(0, B - 1) as b:
            batch(b, True)
        batch(B - 1, False)
        sp.wait_ge(out_stored, 16 * B)

    @block.gpsimd
    def _(pool):
        last = slice(MASK_ROW, P)
        pool.memset(stack[last].bitcast(F32), 0.0).then_inc(rows_zeroed, 1)
        pool.wait_ge(rows_zeroed, 1)
        pool.memset(ka[MASK_ROW:MAX_ROW + 1].bitcast(F32), -1.0).then_inc(rows_set, 1)
        pool.memset(qa[MASK_ROW:MAX_ROW + 1, :, :, :].bitcast(F32), 1.0).then_inc(rows_set, 1)
        with pool.Fori(0, B) as b:
            for g in range(G):
                for kt in range(1, ADD_KT):
                    step = g * KT + kt
                    if kt == 1 and g >= 1:
                        pool.wait_ge(summed, b * G + g)
                    if kt >= 2:
                        pool.wait_ge(added, (b * G + g) * N_ADD + kt - 1)
                    pool.wait_ge(exp_done, b * N_EXP + 2 * step + 2)
                    before = pt[:, (step - 1) % NPT, :, :] if kt == 1 else acc[:]
                    pool.tensor_tensor(acc[:], before, pt[:, step % NPT, :, :], ALU.add).then_inc(added, 1)

    @block.scalar
    def _(act):
        act.wait_ge(vec_loaded, 16)
        act.activation(tg[:], vec[:, V_GATE:V_GATE + 1], ACT.Tanh).then_inc(gate_ready, 1)

        def squares(b, h):
            if h == 1:
                act.wait_ge(var_filled, b * HALF + 1)
            for t in range(ET):
                act.wait_ge(centred, b * HALF * ET + h * ET + t + 1)
                act.activation(sq[:, t, :], tile_half(c, t, h), ACT.Square).then_inc(squared, 1)

        def deviations(b):
            for h in range(HALF):
                act.wait_ge(var_filled, b * HALF + h + 1)
                act.activation(rstd[:, h, :], bank[:, h, :], ACT.Sqrt, bias=vec[:, V_EPS:V_EPS + 1]).then_inc(sd_ready, 1)

        def affine(b):
            for h in range(HALF):
                for t in range(ET):
                    act.wait_ge(scaled, b * HALF * ET + h * ET + t + 1)
                    act.activation(tile_half(c, t, h), tile_half(c, t, h), ACT.Identity, scale=v("ln_gamma", t),
                                   bias=v("ln_beta", t)).then_inc(normed, 1)

        def high_part(b, g, i, first=False):
            n = (b * G + g) * 3
            if i == 0 and not first:
                act.wait_ge(placed, (b * G + g) * N_PLACED)
            act.wait_ge(kq_filled, n + i + 1)
            to = part[:, 0:2, S2:S2 + L] if i == 2 else part[:, 0:3:2, i * L:(i + 1) * L]
            act.activation(to, bank[:, KQ, :].unsqueeze(1).to_broadcast([P, 2, L]), ACT.Copy).then_inc(kq_high, 1)

        def values(b, i):
            act.wait_ge(values_filled, b * KT + i + 1)
            act.activation(vals[:, i, :], bank[:, EXP + i % 4, :], ACT.Copy).then_inc(values_read, 1)

        def prepare_first(b, first=False):
            for i, fills in enumerate(FIRST_FILLS):
                for n in fills:
                    high_part(b, 0, n, first)
                if i < KT // 2:
                    values(b, i)
            for i in range(KT // 2):
                values(b, KT // 2 + i)
                if i < 3:
                    high_part(b, 1, i)

        def exponentials(b, step):
            for u in range(2):
                n = 2 * step + u
                act.wait_ge(scored, b * N_EXP + n + 1)
                if u == 0 and step >= NPT:
                    act.wait_ge(pv_done, b * N_STEP + step - NPT + 1)
                    g, kt = (step - NPT) // KT, (step - NPT) % KT
                    if kt < ADD_KT:
                        act.wait_ge(added, (b * G + g) * N_ADD + max(kt, 1))
                e = EXP + 2 * (n % 2)
                act.activation(pt[:, step % NPT, 2 * u:2 * u + 2, :], bank[:, e:e + 2, :], ACT.Exp,
                               scale=SCALE).then_inc(exp_done, 1)

        def group_out(b, g):
            act.wait_ge(pv_done, b * N_STEP + g * KT + KT)
            act.activation(o[:, g, :], bank[:, OUT, :], ACT.Copy).then_inc(o_read, 1)

        def batch(b, prepare):
            for g in range(G):
                for kt in range(KT):
                    exponentials(b, g * KT + kt)
                    if kt == 0 and g >= 1:
                        group_out(b, g - 1)
                    for i in fill_slots(g, kt):
                        high_part(b, g + 2, i)
                    if g == G - 2 and kt == MEAN_KT + 2 and prepare:
                        squares(b + 1, 0)
                    if g == G - 1 and kt == 1 and prepare:
                        squares(b + 1, 1)
                    if g == G - 1 and kt == 3 and prepare:
                        deviations(b + 1)
            group_out(b, G - 1)
            if prepare:
                affine(b + 1)
                prepare_first(b + 1)

        squares(0, 0)
        squares(0, 1)
        deviations(0)
        affine(0)
        prepare_first(0, True)
        with act.Fori(0, B - 1) as b:
            batch(b, True)
        batch(B - 1, False)

    @block.vector
    def _(dve):
        def centre(b, h):
            dve.wait_ge(mean_filled, b * HALF + h + 1)
            for t in range(ET):
                dve.tensor_tensor(tile_half(c, t, h), tile_half(c, t, h), bank[:, KQ, :],
                                  ALU.subtract).then_inc(centred, 1)

        def scale(b):
            for h in range(HALF):
                dve.wait_ge(sd_ready, b * HALF + h + 1)
                dve.reciprocal(rstd[:, h, :], rstd[:, h, :]).then_inc(inverted, 1)
                dve.wait_ge(inverted, b * HALF + h + 1)
                for t in range(ET):
                    dve.tensor_tensor(tile_half(c, t, h), tile_half(c, t, h), rstd[:, h, :],
                                      ALU.mult).then_inc(scaled, 1)
            dve.wait_ge(mask_loaded, b * 16 + 16)
            dve.tensor_scalar(maskf, mask8[:].rearrange("o (h l) -> o h l", l=L), 1.0, -MASKED, ALU.subtract,
                              ALU.mult).then_inc(mask_made, 1)

        def low_part(b, g, i):
            dve.wait_ge(kq_high, (b * G + g) * 3 + i + 1)
            s = slice(i * L, (i + 1) * L)
            dve.tensor_tensor(part[:, 2 if i == 2 else 1, s], bank[:, KQ, :], part[:, 0, s].bitcast(F32),
                              ALU.subtract).then_inc(kq_low, 1)

        def maximum(b, g, i):
            dve.wait_ge(scores_filled, (b * G + g) * NS + i + 1)
            n = i // HALF
            dve.reduce_max(mx[:, i % HALF, n:n + 1], bank[:, (i + 1) % 2, :], AX.X).then_inc(scores_read, 1)

        def maxima(b, g):
            gi = b * G + g
            dve.wait_ge(scores_read, gi * NS + NS)
            dve.tensor_tensor(mxx[:], mx[:, 0, :], mx[:, 1, :], ALU.max).then_inc(max_ready, 1)
            dve.wait_ge(max_turned, gi + 1)
            if g + 1 < G:
                dve.wait_ge(kq_low, gi * 3 + 6)
            dve.tensor_copy(mt[:], bank[0:GH * ET, 1, 0:P]).then_inc(max_taken, 1)

        def keep_sum(b, g):
            dve.wait_ge(summed, b * G + g + 1)
            if g == 0:
                dve.tensor_copy(ssum[:], bank[:, KQ, :]).then_inc(sum_kept, 1)
            else:
                dve.wait_ge(sum_kept, b * G + g)
                dve.tensor_tensor(ssum[:], ssum[:], bank[:, KQ, :], ALU.add).then_inc(sum_kept, 1)

        def first_maxima(b):
            for n, slots in enumerate(FIRST_SCORES):
                for i in slots:
                    maximum(b, 0, i)
                low_part(b, 1, n)
            maxima(b, 0)

        def batch(b, prepare):
            for g in range(G):
                if g >= 1:
                    keep_sum(b, g - 1)
                for kt in range(KT):
                    if g + 1 < G:
                        for i in score_slots(kt):
                            maximum(b, g + 1, i)
                    for i in fill_slots(g, kt):
                        low_part(b, g + 2, i)
                    if g == G - 2 and prepare and kt in (MEAN_KT, MEAN_KT + 1):
                        if kt == MEAN_KT:
                            dve.wait_ge(mask_placed, b * 2 * N_MASK + 2 * N_MASK)
                        centre(b + 1, kt - MEAN_KT)
                    if kt == TURN_KT and g + 1 < G:
                        maxima(b, g + 1)
            if prepare:
                scale(b + 1)
            keep_sum(b, G - 1)
            if prepare:
                low_part(b + 1, 0, 0)
            dve.wait_ge(sum_kept, b * G + G)
            dve.reciprocal(ssum[:], ssum[:]).then_inc(sum_inverted, 1)
            if prepare:
                low_part(b + 1, 0, 1)
                low_part(b + 1, 0, 2)
            for g in range(G):
                dve.wait_ge(sum_spread, b * G + g + 1)
                dve.wait_ge(o_read, b * G + g + 1)
                dve.tensor_tensor(o[:, g, :], o[:, g, :], bank[:, EXP + g, :], ALU.mult).then_inc(o_normed, 1)
            dve.wait_ge(xr_loaded, b * 16 + 16)
            for m in range(ET):
                dve.wait_ge(out_filled, b * ET + m + 1)
                dve.scalar_tensor_tensor(out=xr[:, m, :], in0=bank[:, EXP + m, :], scalar=tg[:, 0:1],
                                         in1=xr[:, m, :], op0=ALU.mult, op1=ALU.add).then_inc(out_done, 1)
            if prepare:
                first_maxima(b + 1)

        centre(0, 0)
        centre(0, 1)
        scale(0)
        for i in range(3):
            low_part(0, 0, i)
        dve.wait_ge(gate_ready, 1)
        first_maxima(0)
        with dve.Fori(0, B - 1) as b:
            batch(b, True)
        batch(B - 1, False)

    @block.tensor
    def _(pe):
        def rows(to, pairs):
            for n, (lhsT, rhs) in enumerate(pairs):
                ins = pe.matmul(to, lhsT, rhs, start=(n == 0), stop=(n == len(pairs) - 1))
            return ins

        def mean(b, h):
            if h == 0:
                pe.wait_ge(c_loaded, b * 16 + 16)
            else:
                pe.wait_ge(centred, b * HALF * ET + ET)
            rows(bank[:, KQ, :], [(mean_w[:], tile_half(c, t, h)) for t in range(ET)]).then_inc(mean_filled, 1)

        def variance(b, h):
            for t in range(ET):
                pe.wait_ge(squared, b * HALF * ET + h * ET + t + 1)
                ins = pe.matmul(bank[:, h, :], mean_w[:], sq[:, t, :], start=(t == 0), stop=(t == ET - 1))
            ins.then_inc(var_filled, 1)

        def fill(b, g, i, t):
            if t == 0 and (i >= 1 or g == 1):
                pe.wait_ge(kq_low, (b * G + g) * 3 + i)
            weight, src = (W["Wq2"], xq) if i == 2 else (W["Wk2"], c)
            s = slice(0, L) if i == 2 else slice(i * L, (i + 1) * L)
            ins = pe.matmul(bank[:, KQ, :], weight[:, t, g * P:(g + 1) * P], src[:, t, s], start=(t == 0),
                            stop=(t == ET - 1))
            if t == ET - 1:
                ins.then_inc(kq_filled, 1)

        def scores(b, g, i):
            gi = b * G + g
            if i == 0:
                pe.wait_ge(placed, gi * N_PLACED + N_PLACED)
                if g < 2:
                    pe.wait_ge(mask_placed, b * 2 * N_MASK + (g + 1) * N_MASK)
                if g >= 1:
                    pe.wait_ge(max_taken, gi)
            if i >= 2:
                pe.wait_ge(scores_read, gi * NS + i - 1)
            n, h = i // HALF, i % HALF
            j, qt = n // ET, n % ET
            pe.matmul(bank[:, (i + 1) % 2, :], qa[0:MASK_ROW + 1, g % 2, j, qt * P:(qt + 1) * P],
                      ka[0:MASK_ROW + 1, g % 2, h, j, :], start=True, stop=True).then_inc(scores_filled, 1)

        def turn_maxima(b, g):
            pe.wait_ge(max_ready, b * G + g + 1)
            pe.transpose(bank[0:GH * ET, 1, 0:P], mxx[:], ident[:]).then_inc(max_turned, 1)

        def value_rows(b, i, t):
            if t == 0 and i >= 4:
                pe.wait_ge(values_read, b * KT + i - 3)
            ins = pe.matmul(bank[:, EXP + i % 4, :], c[:, t, i * P:(i + 1) * P], W["Wv2"][:, t, :], start=(t == 0),
                            stop=(t == ET - 1))
            if t == ET - 1:
                ins.then_inc(values_filled, 1)

        def first_half(b, before=None):
            for i, fills in enumerate(FIRST_FILLS):
                for n in fills:
                    if n < HALF:
                        pe.wait_ge(normed, (b * HALF + n + 1) * ET)
                    else:
                        pe.wait_ge(xq_loaded, b * 16 + 16)
                    if n == 0 and before is not None:
                        pe.wait_ge(sum_kept, before * G + G)
                    for t in range(ET):
                        fill(b, 0, n, t)
                if i < KT // 2:
                    for t in range(ET):
                        value_rows(b, i, t)

        def second_half(b):
            for n, slots in enumerate(FIRST_SCORES):
                for t in range(ET):
                    value_rows(b, KT // 2 + n, t)
                    for i in slots[len(slots) * 2 * t // 8:len(slots) * (2 * t + 1) // 8]:
                        scores(b, 0, i)
                    fill(b, 1, n, t)
                    for i in slots[len(slots) * (2 * t + 1) // 8:len(slots) * (2 * t + 2) // 8]:
                        scores(b, 0, i)
            for t in range(ET):
                value_rows(b, KT - 1, t)
                if t == 1:
                    turn_maxima(b, 0)

        def scores_again(b, g, kt):
            for u in range(2):
                n = 2 * (g * KT + kt) + u
                if n >= 2:
                    pe.wait_ge(exp_done, b * N_EXP + n - 1)
                for j in (2 * u, 2 * u + 1):
                    ins = pe.matmul(bank[:, EXP + 2 * (n % 2) + j % 2, :], ka[:, g % 2, kt * P // L, j, kt * P % L:kt * P % L + P],
                                    qa[:, g % 2, j, :], start=True, stop=True)
                ins.then_inc(scored, 1)

        def attend(b, step):
            g, kt = step // KT, step % KT
            pe.wait_ge(exp_done, b * N_EXP + 2 * step + 2)
            if kt == 0 and g >= 1:
                pe.wait_ge(o_read, b * G + g)
            for j in range(GH):
                ins = pe.matmul(bank[D1 * j:D1 * (j + 1), OUT, :], vals[:, kt, g * P + D1 * j:g * P + D1 * (j + 1)],
                                pt[:, step % NPT, j, :], start=(kt == 0), stop=(kt == KT - 1))
            if kt == ADD_KT:
                if g + 2 < G:
                    pe.wait_ge(kq_low, (b * G + g + 2) * 3 + 3)
                else:
                    pe.wait_ge(sum_kept, b * G + g)
            if kt >= ADD_KT:
                ins = sum_rows(g, pt[:, step % NPT, :, :], kt == ADD_KT, False)
            ins.then_inc(pv_done, 1)

        def sum_rows(g, probs, start, stop):
            for j in range(GH):
                ins = pe.matmul(bank[D1 * j:D1 * (j + 1), KQ, :], one[:, g * D1:(g + 1) * D1], probs[:, j, :],
                                start=start, stop=stop)
            return ins

        def sum_group(b, g):
            pe.wait_ge(added, (b * G + g) * N_ADD + N_ADD)
            sum_rows(g, acc[:], False, True).then_inc(summed, 1)

        def batch(b, prepare):
            pe.wait_ge(values_read, b * KT + KT)
            for g in range(G):
                pe.wait_ge(max_placed, (b * G + g) * 16 + 16)
                for kt in range(KT):
                    scores_again(b, g, kt)
                    slots = score_slots(kt) if g + 1 < G else []
                    for i in fill_slots(g, kt):
                        if i == 0 and g == 0:
                            pe.wait_ge(kq_low, b * G * 3 + 6)
                        elif i == 0:
                            pe.wait_ge(sum_kept, b * G + g)
                        for t in range(ET):
                            for n in slots[len(slots) * t // ET:len(slots) * (t + 1) // ET]:
                                scores(b, g + 1, n)
                            fill(b, g + 2, i, t)
                    done = len(slots) if fill_slots(g, kt) else 2
                    if not fill_slots(g, kt):
                        for n in slots[:2]:
                            scores(b, g + 1, n)
                    if kt == TURN_KT and g + 1 < G:
                        turn_maxima(b, g + 1)
                    if kt == ADD_KT + 1 and g == G - 2 and prepare:
                        pe.wait_ge(centred, (b + 1) * HALF * ET + HALF * ET)
                    if g * KT + kt >= 1:
                        attend(b, g * KT + kt - 1)
                    for i in slots[done:]:
                        scores(b, g + 1, i)
                    if kt == 0 and g >= 1:
                        sum_group(b, g - 1)
                    if g == G - 2 and prepare and kt in (MEAN_KT, MEAN_KT + 1):
                        if kt == MEAN_KT:
                            pe.wait_ge(sum_kept, b * G + g)
                        mean(b + 1, kt - MEAN_KT)
                    if g == G - 1 and prepare and kt in (0, 2):
                        if kt == 0:
                            pe.wait_ge(max_taken, b * G + G)
                        variance(b + 1, kt // 2)
            attend(b, N_STEP - 1)
            sum_group(b, G - 1)
            if prepare:
                first_half(b + 1, b)
            pe.wait_ge(sum_inverted, b + 1)
            for g in range(G):
                if prepare:
                    pe.wait_ge(values_read, (b + 1) * KT + g + 1)
                rows(bank[:, EXP + g, :], [(spread_w[:, g * P:(g + 1) * P], ssum[:])]).then_inc(sum_spread, 1)
            pe.wait_ge(o_normed, b * G + G)
            for m in range(ET):
                rows(bank[:, EXP + m, :], [(W["Wo2"][:, t, m * P:(m + 1) * P], o[:, t, :])
                                           for t in range(ET)]).then_inc(out_filled, 1)
            pe.wait_ge(out_done, b * ET + ET)
            if prepare:
                second_half(b + 1)

        pe.wait_ge(mean_loaded, 16)
        mean(0, 0)
        mean(0, 1)
        variance(0, 0)
        variance(0, 1)
        pe.wait_ge(consts_loaded, N_CONST)
        first_half(0)
        second_half(0)
        with pe.Fori(0, B - 1) as b:
            batch(b, True)
        batch(B - 1, False)


def build(nc, a, out_dram):
    x2_dram = nc.dram_tensor("x2_dram", [B, P, ET, L], F32, kind="Internal").ap()
    with ExitStack() as both:
        shared = both.enter_context(nc.sbuf_tensor("shared", [P, ET * S2], F32))
        c_loaded = both.enter_context(nc.semaphore("c_loaded"))
        with ExitStack() as ctx:
            time_mix(nc, ctx, a, x2_dram, shared, c_loaded)
        with ExitStack() as ctx:
            cross_attention(nc, ctx, a, x2_dram, out_dram, shared, c_loaded)


def kernel(**inputs):
    import concourse.bacc as bacc
    from concourse.bass_utils import run_bass_kernel_spmd

    i = {k: np.asarray(v) for k, v in inputs.items()}
    t0, t1 = "L0_xattn_", "L1_xattn_"
    x, c = i["x"], i["ctx_2048"]

    def tiled(z):
        return z.reshape(z.shape[0], z.shape[1], ET, P).transpose(0, 3, 2, 1)

    w_v, w_g, w_o = i[t0 + "Wv"].T[:, VALUE_ORDER], i[t0 + "Wg"].T[:, VALUE_ORDER], i[t0 + "Wo"].T[VALUE_ORDER]
    rows = [i[t0 + n] for n in ("ln1_w", "ln1_b", "ln2_w", "ln2_b", "maa_x")]
    rows += list(i[t0 + "maa_stack"])
    rows += [i[t0 + "time_decay"], i[t0 + "faaaa"].reshape(E)]
    rows += [i[t0 + "gn_w"][VALUE_ORDER], i[t0 + "gn_b"][VALUE_ORDER]]
    rows += [i[t0 + n] for n in ("ffn_maa_k", "ffn_maa_r")]
    rows += [i[t1 + "ln_gamma"], i[t1 + "ln_beta"]]
    vecs = np.stack(rows).reshape(len(rows), ET, P).transpose(2, 0, 1).reshape(P, len(rows) * ET)
    vecs = np.concatenate([vecs, np.full((P, 1), EPS, np.float32), np.broadcast_to(i[t1 + "gate"], (P, 1))], 1)
    arrays = {
        "xT": tiled(x), "ctxT": tiled(c), "prev": tiled(c[:, 0:2]),
        "s0": c[:, 2:2 + D0].reshape(B, ET, P, D0).transpose(0, 2, 1, 3),
        "mask": i["mask_BxS2_bf1"].view(np.uint8), "vecs": vecs, "consts": shape_constants(),
        "maa_w1": i[t0 + "maa_w1"], "maa_w2": i[t0 + "maa_w2"].reshape(5 * MIX, E),
        "decay_w1": i[t0 + "decay_w1"], "decay_w2": i[t0 + "decay_w2"],
        "Wr": i[t0 + "Wr"].T, "Wk": i[t0 + "Wk"].T, "Wg": w_g, "Wv": w_v, "Wo": w_o,
        "fWk": i[t0 + "ffn_Wk"].T, "fWr": i[t0 + "ffn_Wr"].T, "fWv": i[t0 + "ffn_Wv"].T,
        "Wq2": i[t1 + "Wq"].T, "Wk2": i[t1 + "Wk"].T, "Wv2": i[t1 + "Wv"].T, "Wo2": i[t1 + "Wo"].T,
    }
    arrays = {f"in_{k}": np.ascontiguousarray(z) for k, z in arrays.items()}
    nc = bacc.Bacc("TRN2", target_bir_lowering=False, num_devices=1)
    a = {k[3:]: nc.dram_tensor(k, z.shape, mybir.dt.from_np(z.dtype), kind="ExternalInput").ap()
         for k, z in arrays.items()}
    out = nc.dram_tensor("out", (B, P, ET, L), F32, kind="ExternalOutput").ap()
    build(nc, a, out)
    got = run_bass_kernel_spmd(nc, [arrays], core_ids=[0]).results[0]["out"]
    return np.ascontiguousarray(got.transpose(0, 3, 2, 1)).reshape(B, L, E)
```
